# Optimizing a Trainium2 kernel written in Bass

```python
import numpy as np
import jax
import jax.numpy as jnp

def _softmax(x, axis=-1):
    return jax.nn.softmax(x, axis=axis)

def _gelu(x):
    return jax.nn.gelu(x, approximate=True)

def _silu(x):
    return jax.nn.silu(x)

def _sigmoid(x):
    return jax.nn.sigmoid(x)

def _layernorm(x, axis=-1, eps=1e-05):
    m = jnp.mean(x, axis=axis, keepdims=True)
    v = jnp.var(x, axis=axis, keepdims=True)
    return (x - m) / jnp.sqrt(v + eps)

def _scatter_add(tgt, idx, src, axis=0):
    return tgt.at[idx].add(src)

def _segment_sum(src, seg, n):
    return jax.ops.segment_sum(src, seg, n)
kernel_name = 'mk_pixart_resid_d4_seqx_r8_5deb8b'

def setup_inputs(seed: int=0):
    np.random.seed(seed)
    _w = jnp.asarray

    def _rec_inputs():
        import jax
        import jax.numpy as jnp
        _rk = jax.random.key(seed)
        x = -0.0002928 + 1 * jax.random.normal(jax.random.fold_in(_rk, 1), (4, 512, 128), jnp.float32)
        _lenS = 512 - jax.random.randint(jax.random.fold_in(_rk, 7), (4,), 0, max(1, 512 // 4) + 1, jnp.int32)
        _lenS2 = 77 - jax.random.randint(jax.random.fold_in(_rk, 8), (4,), 0, max(1, 77 // 4) + 1, jnp.int32)
        _ctx_1024P = jax.random.normal(jax.random.fold_in(_rk, 11), (4, 16, 128), jnp.float32)
        _ctx_1024c = jax.random.dirichlet(jax.random.fold_in(_rk, 511), 0.3 * jnp.ones((16,), jnp.float32), (4, 77))
        _ctx_1024t = jnp.einsum('bsk,bkd->bsd', _ctx_1024c, _ctx_1024P)
        _ctx_1024t = _ctx_1024t * jax.lax.rsqrt(jnp.mean(jnp.square(_ctx_1024t)) + 1e-12) * 0.953939
        ctx_1024 = -1.39393e-06 + 0.999914 * (_ctx_1024t + 0.3 * jax.random.normal(jax.random.fold_in(_rk, 611), (4, 77, 128), jnp.float32))
        condB_tau = jax.random.uniform(jax.random.fold_in(_rk, 12), (4,), jnp.float32, 0.0, 1.23395)
        fside_BxS2_0 = -0.00205293 + 0.99739 * jax.random.normal(jax.random.fold_in(_rk, 13), (4, 77), jnp.float32)
        condB_pt = jax.random.uniform(jax.random.fold_in(_rk, 15), (4,), jnp.float32, 0.0, 226.919)
        return (x, ctx_1024, condB_tau, fside_BxS2_0, condB_pt, _lenS2)
    x, ctx_1024, condB_tau, fside_BxS2_0, condB_pt, _lenS2 = _rec_inputs()

    def _L0_xcond_setup():
        import jax, jax.numpy as jnp
        import numpy as np
        B, S, D, H = (2, 256, 128, 16)
        DK = D // H

        def _split_heads(x):
            b, s, _ = x.shape
            return x.reshape(b, s, H, DK).transpose(0, 2, 1, 3)
        key = jax.random.key(seed)
        ks = jax.random.split(key, 14)
        inp = {'query': jax.random.normal(ks[0], (B, S, D), jnp.float32), 'key': jax.random.normal(ks[1], (B, S, D), jnp.float32), 'value': jax.random.normal(ks[2], (B, S, D), jnp.float32), 'tau': jax.random.uniform(ks[3], (B, 1), jnp.float32, 0.5, 1.5), 'delta': jax.random.normal(ks[4], (B, S), jnp.float32)}
        sc = 1.0 / np.sqrt(D)
        for i, name in enumerate(['q', 'k', 'v', 'o']):
            inp[f'W{name}'] = jax.random.normal(ks[5 + 2 * i], (D, D), jnp.float32) * sc
            inp[f'b{name}'] = jax.random.normal(ks[6 + 2 * i], (D,), jnp.float32) * 0.01
        return inp
    _L0_xcond_all = _L0_xcond_setup()
    _L0_xcond_in = {k: v for k, v in _L0_xcond_all.items() if k in ('Wq', 'bq', 'Wk', 'bk', 'Wv', 'bv', 'Wo', 'bo')}
    del _L0_xcond_all

    def _L0_ffn_setup():
        import jax, jax.numpy as jnp
        import numpy as np
        E = 16
        K = 4
        B, S, H, I = (4, 128, 128, 256)
        key = jax.random.key(seed)
        k0, k1, k2, k3 = jax.random.split(key, 4)
        scale = 0.02
        return {'hidden_states': jax.random.normal(k0, (B, S, H), jnp.float32), 'router_w': jax.random.normal(k1, (H, E), jnp.float32) * scale, 'router_b': jnp.zeros((E,), jnp.float32), 'w1': jax.random.normal(k2, (E, H, I), jnp.float32) * scale, 'b1': jnp.zeros((E, I), jnp.float32), 'w2': jax.random.normal(k3, (E, I, H), jnp.float32) * scale, 'b2': jnp.zeros((E, H), jnp.float32)}
    _L0_ffn_all = _L0_ffn_setup()
    _L0_ffn_in = {k: v for k, v in _L0_ffn_all.items() if k in ('router_w', 'router_b', 'w1', 'b1', 'w2', 'b2')}
    del _L0_ffn_all

    def _L1_xcond_setup():
        import jax, jax.numpy as jnp
        import numpy as np
        D_MODEL = 128
        N_HEADS = 16
        key = jax.random.key(seed)
        ks = jax.random.split(key, 16)
        B, L, S, D = (4, 256, 256, D_MODEL)
        inp = {'q': jax.random.normal(ks[0], (B, L, D), jnp.float32), 'k': jax.random.normal(ks[1], (B, S, D), jnp.float32), 'v': jax.random.normal(ks[2], (B, S, D), jnp.float32), 'tau': jax.random.uniform(ks[3], (B, 1), jnp.float32, 0.5, 1.5), 'delta': jax.random.normal(ks[4], (B, S), jnp.float32)}
        s = 1.0 / np.sqrt(D)
        inp['Wq'] = jax.random.normal(ks[5], (D, D), jnp.float32) * s
        inp['bq'] = jnp.zeros((D,), jnp.float32)
        inp['Wk'] = jax.random.normal(ks[6], (D, D), jnp.float32) * s
        inp['bk'] = jnp.zeros((D,), jnp.float32)
        inp['Wv'] = jax.random.normal(ks[7], (D, D), jnp.float32) * s
        inp['bv'] = jnp.zeros((D,), jnp.float32)
        inp['Wo'] = jax.random.normal(ks[8], (D, D), jnp.float32) * s
        inp['bo'] = jnp.zeros((D,), jnp.float32)
        return inp
    _L1_xcond_all = _L1_xcond_setup()
    _L1_xcond_in = {k: v for k, v in _L1_xcond_all.items() if k in ('Wq', 'bq', 'Wk', 'bk', 'Wv', 'bv', 'Wo', 'bo')}
    del _L1_xcond_all

    def _L1_ffn_setup():
        import jax, jax.numpy as jnp
        import numpy as np
        B, S, D, H, E = (4, 256, 128, 256, 8)
        key = jax.random.key(seed)
        ks = jax.random.split(key, 8)
        scale = 0.02
        return {'x': jax.random.normal(ks[0], (B, S, D), dtype=jnp.float32), 'Wr': jax.random.normal(ks[1], (D, E), dtype=jnp.float32) * scale, 'br': jnp.zeros((E,), dtype=jnp.float32), 'W1': jax.random.normal(ks[2], (E, D, H), dtype=jnp.float32) * scale, 'b1': jnp.zeros((E, H), dtype=jnp.float32), 'W2': jax.random.normal(ks[3], (E, H, D), dtype=jnp.float32) * scale, 'b2': jnp.zeros((E, D), dtype=jnp.float32)}
    _L1_ffn_all = _L1_ffn_setup()
    _L1_ffn_in = {k: v for k, v in _L1_ffn_all.items() if k in ('Wr', 'br', 'W1', 'b1', 'W2', 'b2')}
    del _L1_ffn_all

    def _L2_xcond_setup():
        import jax, jax.numpy as jnp
        import numpy as np
        N, L, H, Q = (64, 258, 128, 32)
        WINDOW = 16.0
        DEV_POW = 128.0
        key = jax.random.key(seed)
        k1, k2, k3, k4, k5, k6 = jax.random.split(key, 6)
        encoder_outputs = jax.random.normal(k1, (N, L, H), dtype=jnp.float32)
        decoder_h_t = jax.random.normal(k2, (N, Q, H), dtype=jnp.float32)
        src_len = jax.random.randint(k3, (N,), 32, L + 1).astype(jnp.int32)
        p_t = jax.random.uniform(k4, (N,), dtype=jnp.float32) * (src_len.astype(jnp.float32) - 1.0)
        W_a = jax.random.normal(k5, (H, H), dtype=jnp.float32) * (1.0 / np.sqrt(H))
        W_c = jax.random.normal(k6, (H, 2 * H), dtype=jnp.float32) * (1.0 / np.sqrt(2 * H))
        return {'encoder_outputs': encoder_outputs, 'decoder_h_t': decoder_h_t, 'src_len': src_len, 'p_t': p_t, 'W_a': W_a, 'W_c': W_c}
    _L2_xcond_all = _L2_xcond_setup()
    _L2_xcond_in = {k: v for k, v in _L2_xcond_all.items() if k in ('W_a', 'W_c')}
    del _L2_xcond_all

    def _L2_ffn_setup():
        import jax, jax.numpy as jnp
        import numpy as np
        H = 16
        E = 8
        EPS = 1e-05

        def _layernorm(x, g, b):
            mu = jnp.mean(x, axis=-1, keepdims=True)
            var = jnp.mean(jnp.square(x - mu), axis=-1, keepdims=True)
            return (x - mu) * jax.lax.rsqrt(var + EPS) * g + b
        key = jax.random.key(seed)
        T, B, C = (128, 8, 128)
        ks = jax.random.split(key, 12)
        s = 0.02
        return {'x': jax.random.normal(ks[0], (T, B, C), jnp.float32), 'in_proj_w': jax.random.normal(ks[1], (3 * C, C), jnp.float32) * s, 'in_proj_b': jnp.zeros((3 * C,), jnp.float32), 'out_w': jax.random.normal(ks[2], (C, C), jnp.float32) * s, 'out_b': jnp.zeros((C,), jnp.float32), 'ln1_g': jnp.ones((C,), jnp.float32), 'ln1_b': jnp.zeros((C,), jnp.float32), 'router_w': jax.random.normal(ks[3], (E, C), jnp.float32) * s, 'router_b': jnp.zeros((E,), jnp.float32), 'w1': jax.random.normal(ks[4], (E, C, C), jnp.float32) * s, 'b1': jnp.zeros((E, C), jnp.float32), 'w2': jax.random.normal(ks[5], (E, C, C), jnp.float32) * s, 'b2': jnp.zeros((E, C), jnp.float32), 'ln2_g': jnp.ones((C,), jnp.float32), 'ln2_b': jnp.zeros((C,), jnp.float32)}
    _L2_ffn_all = _L2_ffn_setup()
    _L2_ffn_in = {k: v for k, v in _L2_ffn_all.items() if k in ('in_proj_w', 'in_proj_b', 'out_w', 'out_b', 'ln1_g', 'ln1_b', 'router_w', 'router_b', 'w1', 'b1', 'w2', 'b2', 'ln2_g', 'ln2_b')}
    del _L2_ffn_all

    def _L3_xcond_setup():
        import jax, jax.numpy as jnp
        import numpy as np
        B, S, D, H = (2, 256, 128, 16)
        DK = D // H

        def _split_heads(x):
            b, s, _ = x.shape
            return x.reshape(b, s, H, DK).transpose(0, 2, 1, 3)
        key = jax.random.key(seed)
        ks = jax.random.split(key, 14)
        inp = {'query': jax.random.normal(ks[0], (B, S, D), jnp.float32), 'key': jax.random.normal(ks[1], (B, S, D), jnp.float32), 'value': jax.random.normal(ks[2], (B, S, D), jnp.float32), 'tau': jax.random.uniform(ks[3], (B, 1), jnp.float32, 0.5, 1.5), 'delta': jax.random.normal(ks[4], (B, S), jnp.float32)}
        sc = 1.0 / np.sqrt(D)
        for i, name in enumerate(['q', 'k', 'v', 'o']):
            inp[f'W{name}'] = jax.random.normal(ks[5 + 2 * i], (D, D), jnp.float32) * sc
            inp[f'b{name}'] = jax.random.normal(ks[6 + 2 * i], (D,), jnp.float32) * 0.01
        return inp
    _L3_xcond_all = _L3_xcond_setup()
    _L3_xcond_in = {k: v for k, v in _L3_xcond_all.items() if k in ('Wq', 'bq', 'Wk', 'bk', 'Wv', 'bv', 'Wo', 'bo')}
    del _L3_xcond_all

    def _L3_ffn_setup():
        import jax, jax.numpy as jnp
        import numpy as np
        DIM = 128
        INTER = 64
        E = 16
        TOPK = 4
        N_GROUPS = 4
        TOPK_GROUPS = 2
        ROUTE_SCALE = 1.0
        INIT_STD = 0.02
        B, S = (2, 128)
        key = jax.random.key(seed)
        ks = jax.random.split(key, 8)
        return {'x': jax.random.normal(ks[0], (B, S, DIM), jnp.float32), 'gate_w': jax.random.normal(ks[1], (E, DIM), jnp.float32) * INIT_STD, 'gate_bias': jnp.zeros((E,), jnp.float32), 'w1': jax.random.normal(ks[2], (E, INTER, DIM), jnp.float32) * INIT_STD, 'w2': jax.random.normal(ks[3], (E, DIM, INTER), jnp.float32) * INIT_STD, 'w3': jax.random.normal(ks[4], (E, INTER, DIM), jnp.float32) * INIT_STD, 'ws1': jax.random.normal(ks[5], (INTER, DIM), jnp.float32) * INIT_STD, 'ws2': jax.random.normal(ks[6], (DIM, INTER), jnp.float32) * INIT_STD, 'ws3': jax.random.normal(ks[7], (INTER, DIM), jnp.float32) * INIT_STD}
    _L3_ffn_all = _L3_ffn_setup()
    _L3_ffn_in = {k: v for k, v in _L3_ffn_all.items() if k in ('gate_w', 'gate_bias', 'w1', 'w2', 'w3', 'ws1', 'ws2', 'ws3')}
    del _L3_ffn_all
    return {'x': x, 'ctx_1024': ctx_1024, 'condB_tau': condB_tau, 'fside_BxS2_0': fside_BxS2_0, 'condB_pt': condB_pt, '_lenS2': _lenS2, 'L0_xcond_Wq': _L0_xcond_in['Wq'], 'L0_xcond_bq': _L0_xcond_in['bq'], 'L0_xcond_Wk': _L0_xcond_in['Wk'], 'L0_xcond_bk': _L0_xcond_in['bk'], 'L0_xcond_Wv': _L0_xcond_in['Wv'], 'L0_xcond_bv': _L0_xcond_in['bv'], 'L0_xcond_Wo': _L0_xcond_in['Wo'], 'L0_xcond_bo': _L0_xcond_in['bo'], 'L0_ffn_router_w': _L0_ffn_in['router_w'], 'L0_ffn_router_b': _L0_ffn_in['router_b'], 'L0_ffn_w1': _L0_ffn_in['w1'], 'L0_ffn_b1': _L0_ffn_in['b1'], 'L0_ffn_w2': _L0_ffn_in['w2'], 'L0_ffn_b2': _L0_ffn_in['b2'], 'L1_xcond_Wq': _L1_xcond_in['Wq'], 'L1_xcond_bq': _L1_xcond_in['bq'], 'L1_xcond_Wk': _L1_xcond_in['Wk'], 'L1_xcond_bk': _L1_xcond_in['bk'], 'L1_xcond_Wv': _L1_xcond_in['Wv'], 'L1_xcond_bv': _L1_xcond_in['bv'], 'L1_xcond_Wo': _L1_xcond_in['Wo'], 'L1_xcond_bo': _L1_xcond_in['bo'], 'L1_ffn_Wr': _L1_ffn_in['Wr'], 'L1_ffn_br': _L1_ffn_in['br'], 'L1_ffn_W1': _L1_ffn_in['W1'], 'L1_ffn_b1': _L1_ffn_in['b1'], 'L1_ffn_W2': _L1_ffn_in['W2'], 'L1_ffn_b2': _L1_ffn_in['b2'], 'L2_xcond_W_a': _L2_xcond_in['W_a'], 'L2_xcond_W_c': _L2_xcond_in['W_c'], 'L2_ffn_in_proj_w': _L2_ffn_in['in_proj_w'], 'L2_ffn_in_proj_b': _L2_ffn_in['in_proj_b'], 'L2_ffn_out_w': _L2_ffn_in['out_w'], 'L2_ffn_out_b': _L2_ffn_in['out_b'], 'L2_ffn_ln1_g': _L2_ffn_in['ln1_g'], 'L2_ffn_ln1_b': _L2_ffn_in['ln1_b'], 'L2_ffn_router_w': _L2_ffn_in['router_w'], 'L2_ffn_router_b': _L2_ffn_in['router_b'], 'L2_ffn_w1': _L2_ffn_in['w1'], 'L2_ffn_b1': _L2_ffn_in['b1'], 'L2_ffn_w2': _L2_ffn_in['w2'], 'L2_ffn_b2': _L2_ffn_in['b2'], 'L2_ffn_ln2_g': _L2_ffn_in['ln2_g'], 'L2_ffn_ln2_b': _L2_ffn_in['ln2_b'], 'L3_xcond_Wq': _L3_xcond_in['Wq'], 'L3_xcond_bq': _L3_xcond_in['bq'], 'L3_xcond_Wk': _L3_xcond_in['Wk'], 'L3_xcond_bk': _L3_xcond_in['bk'], 'L3_xcond_Wv': _L3_xcond_in['Wv'], 'L3_xcond_bv': _L3_xcond_in['bv'], 'L3_xcond_Wo': _L3_xcond_in['Wo'], 'L3_xcond_bo': _L3_xcond_in['bo'], 'L3_ffn_gate_w': _L3_ffn_in['gate_w'], 'L3_ffn_gate_bias': _L3_ffn_in['gate_bias'], 'L3_ffn_w1': _L3_ffn_in['w1'], 'L3_ffn_w2': _L3_ffn_in['w2'], 'L3_ffn_w3': _L3_ffn_in['w3'], 'L3_ffn_ws1': _L3_ffn_in['ws1'], 'L3_ffn_ws2': _L3_ffn_in['ws2'], 'L3_ffn_ws3': _L3_ffn_in['ws3']}

def reference(x, ctx_1024, condB_tau, fside_BxS2_0, condB_pt, _lenS2, L0_xcond_Wq, L0_xcond_bq, L0_xcond_Wk, L0_xcond_bk, L0_xcond_Wv, L0_xcond_bv, L0_xcond_Wo, L0_xcond_bo, L0_ffn_router_w, L0_ffn_router_b, L0_ffn_w1, L0_ffn_b1, L0_ffn_w2, L0_ffn_b2, L1_xcond_Wq, L1_xcond_bq, L1_xcond_Wk, L1_xcond_bk, L1_xcond_Wv, L1_xcond_bv, L1_xcond_Wo, L1_xcond_bo, L1_ffn_Wr, L1_ffn_br, L1_ffn_W1, L1_ffn_b1, L1_ffn_W2, L1_ffn_b2, L2_xcond_W_a, L2_xcond_W_c, L2_ffn_in_proj_w, L2_ffn_in_proj_b, L2_ffn_out_w, L2_ffn_out_b, L2_ffn_ln1_g, L2_ffn_ln1_b, L2_ffn_router_w, L2_ffn_router_b, L2_ffn_w1, L2_ffn_b1, L2_ffn_w2, L2_ffn_b2, L2_ffn_ln2_g, L2_ffn_ln2_b, L3_xcond_Wq, L3_xcond_bq, L3_xcond_Wk, L3_xcond_bk, L3_xcond_Wv, L3_xcond_bv, L3_xcond_Wo, L3_xcond_bo, L3_ffn_gate_w, L3_ffn_gate_bias, L3_ffn_w1, L3_ffn_w2, L3_ffn_w3, L3_ffn_ws1, L3_ffn_ws2, L3_ffn_ws3):
    import jax
    import jax.numpy as jnp

    def _L0_xcond_ref(query, key, value, tau, delta, Wq, bq, Wk, bk, Wv, bv, Wo, bo):
        import jax, jax.numpy as jnp
        import numpy as np
        B, S, D, H = (2, 256, 128, 16)
        DK = D // H

        def _split_heads(x):
            b, s, _ = x.shape
            return x.reshape(b, s, H, DK).transpose(0, 2, 1, 3)
        q = _split_heads(query @ Wq.T + bq)
        k = _split_heads(key @ Wk.T + bk)
        v = _split_heads(value @ Wv.T + bv)
        scores = jnp.einsum('bhqd,bhkd->bhqk', q, k)
        scores = scores * tau[:, :, None, None] + delta[:, None, None, :]
        scores = scores / jnp.sqrt(jnp.asarray(DK, scores.dtype))
        p_attn = jax.nn.softmax(scores, axis=-1)
        x = jnp.einsum('bhqk,bhkd->bhqd', p_attn, v)
        x = x.transpose(0, 2, 1, 3).reshape(query.shape[0], -1, H * DK)
        return x @ Wo.T + bo

    def _L0_ffn_ref(hidden_states, router_w, router_b, w1, b1, w2, b2):
        import jax, jax.numpy as jnp
        import numpy as np
        E = 16
        K = 4
        B, S, H, I = (4, 128, 128, 256)
        b, s, h = hidden_states.shape
        logits = hidden_states @ router_w + router_b
        probs = jax.nn.softmax(logits, axis=-1)
        topw, topi = jax.lax.top_k(probs, K)
        topw = topw / jnp.sum(topw, axis=-1, keepdims=True)
        combine = jnp.sum(jax.nn.one_hot(topi, E, dtype=hidden_states.dtype) * topw[..., None], axis=2)
        x = hidden_states.reshape(b * s, h)
        c = combine.reshape(b * s, E)

        def body(acc, expert):
            w1e, b1e, w2e, b2e, ce = expert
            hmid = jax.nn.gelu(x @ w1e + b1e, approximate=False)
            return (acc + (hmid @ w2e + b2e) * ce[:, None], None)
        out, _ = jax.lax.scan(body, jnp.zeros_like(x), (w1, b1, w2, b2, c.T))
        return out.reshape(b, s, h)

    def _L1_xcond_ref(q, k, v, tau, delta, Wq, bq, Wk, bk, Wv, bv, Wo, bo):
        import jax, jax.numpy as jnp
        import numpy as np
        D_MODEL = 128
        N_HEADS = 16
        B, L, D = q.shape
        S = k.shape[1]
        H = N_HEADS
        E = D // H
        qh = (q @ Wq.T + bq).reshape(B, L, H, E)
        kh = (k @ Wk.T + bk).reshape(B, S, H, E)
        vh = (v @ Wv.T + bv).reshape(B, S, H, E)
        scale = 1.0 / np.sqrt(E).astype(np.float32)
        scores = jnp.einsum('blhe,bshe->bhls', qh, kh)
        scores = scores * tau[:, None, None, :] + delta[:, None, None, :]
        a = jax.nn.softmax(scale * scores, axis=-1)
        out = jnp.einsum('bhls,bshd->blhd', a, vh).reshape(B, L, D)
        return out @ Wo.T + bo

    def _L1_ffn_ref(x, Wr, br, W1, b1, W2, b2):
        import jax, jax.numpy as jnp
        import numpy as np
        B, S, D, H, E = (4, 256, 128, 256, 8)
        d = x.shape[-1]
        tokens = x.reshape(-1, d)
        logits = tokens @ Wr + br
        probs = jax.nn.softmax(logits, axis=-1)
        expert = jnp.argmax(probs, axis=-1)
        max_prob = jnp.take_along_axis(probs, expert[:, None], axis=-1)
        h = jax.nn.relu(jnp.einsum('td,edh->teh', tokens, W1) + b1[None])
        y = jnp.einsum('teh,ehd->ted', h, W2) + b2[None]
        out = jnp.take_along_axis(y, expert[:, None, None], axis=1)[:, 0, :]
        return (out * max_prob).reshape(x.shape)

    def _L2_xcond_ref(encoder_outputs, decoder_h_t, src_len, p_t, W_a, W_c):
        import jax, jax.numpy as jnp
        import numpy as np
        N, L, H, Q = (64, 258, 128, 32)
        WINDOW = 16.0
        DEV_POW = 128.0
        n, l, h = encoder_outputs.shape
        idx = jnp.arange(l, dtype=jnp.float32)
        src_end = src_len.astype(jnp.float32)
        attn_start = jnp.maximum(p_t - WINDOW, 0.0)
        attn_end = jnp.minimum(p_t + WINDOW, src_end)
        mask = (idx[None, :] < attn_start[:, None]) | (idx[None, :] > attn_end[:, None])
        score = jnp.einsum('nqh,hk,nlk->nql', decoder_h_t, W_a, encoder_outputs)
        score = jnp.where(mask[:, None, :], -1000000000.0, score)
        align = jax.nn.softmax(score, axis=2)
        gauss = jnp.exp(-(idx[None, :] - p_t[:, None]) ** 2 / DEV_POW)
        align = align * gauss[:, None, :]
        context = jnp.einsum('nql,nlh->nqh', align, encoder_outputs)
        cat = jnp.concatenate([context, decoder_h_t], axis=2)
        return jnp.tanh(cat @ W_c.T)

    def _L2_ffn_ref(x, in_proj_w, in_proj_b, out_w, out_b, ln1_g, ln1_b, router_w, router_b, w1, b1, w2, b2, ln2_g, ln2_b):
        import jax, jax.numpy as jnp
        import numpy as np
        H = 16
        E = 8
        EPS = 1e-05

        def _layernorm(x, g, b):
            mu = jnp.mean(x, axis=-1, keepdims=True)
            var = jnp.mean(jnp.square(x - mu), axis=-1, keepdims=True)
            return (x - mu) * jax.lax.rsqrt(var + EPS) * g + b
        T, B, C = x.shape
        D = C // H
        qkv = x @ in_proj_w.T + in_proj_b
        q, k, v = jnp.split(qkv, 3, axis=-1)
        q = q.reshape(T, B, H, D)
        k = k.reshape(T, B, H, D)
        v = v.reshape(T, B, H, D)
        scale = 1.0 / np.sqrt(D).astype(np.float32)
        scores = jnp.einsum('tbhd,sbhd->bhts', q, k) * scale
        attn = jax.nn.softmax(scores, axis=-1)
        ctx = jnp.einsum('bhts,sbhd->tbhd', attn, v).reshape(T, B, C)
        attn_out = ctx @ out_w.T + out_b
        h = _layernorm(x + attn_out, ln1_g, ln1_b)
        flat = h.reshape(-1, C)
        logits = flat @ router_w.T + router_b
        probs = jax.nn.softmax(logits, axis=-1)
        _, top_i = jax.lax.top_k(probs, 2)
        assign = jnp.max(top_i, axis=-1)
        out = jnp.zeros_like(flat)
        for e in range(E):
            he = jax.nn.gelu(flat @ w1[e].T + b1[e], approximate=False)
            oe = he @ w2[e].T + b2[e]
            out = jnp.where((assign == e)[:, None], oe, out)
        moe_out = out.reshape(T, B, C)
        return _layernorm(h + moe_out, ln2_g, ln2_b)

    def _L3_xcond_ref(query, key, value, tau, delta, Wq, bq, Wk, bk, Wv, bv, Wo, bo):
        import jax, jax.numpy as jnp
        import numpy as np
        B, S, D, H = (2, 256, 128, 16)
        DK = D // H

        def _split_heads(x):
            b, s, _ = x.shape
            return x.reshape(b, s, H, DK).transpose(0, 2, 1, 3)
        q = _split_heads(query @ Wq.T + bq)
        k = _split_heads(key @ Wk.T + bk)
        v = _split_heads(value @ Wv.T + bv)
        scores = jnp.einsum('bhqd,bhkd->bhqk', q, k)
        scores = scores * tau[:, :, None, None] + delta[:, None, None, :]
        scores = scores / jnp.sqrt(jnp.asarray(DK, scores.dtype))
        p_attn = jax.nn.softmax(scores, axis=-1)
        x = jnp.einsum('bhqk,bhkd->bhqd', p_attn, v)
        x = x.transpose(0, 2, 1, 3).reshape(query.shape[0], -1, H * DK)
        return x @ Wo.T + bo

    def _L3_ffn_ref(x, gate_w, gate_bias, w1, w2, w3, ws1, ws2, ws3):
        import jax, jax.numpy as jnp
        import numpy as np
        DIM = 128
        INTER = 64
        E = 16
        TOPK = 4
        N_GROUPS = 4
        TOPK_GROUPS = 2
        ROUTE_SCALE = 1.0
        INIT_STD = 0.02
        B, S = (2, 128)
        Bx, Sx, D = x.shape
        T = Bx * Sx
        xf = x.reshape(T, D)
        scores = jax.nn.sigmoid(xf @ gate_w.T)
        original_scores = scores
        s = scores + gate_bias
        sg = s.reshape(T, N_GROUPS, E // N_GROUPS)
        group_scores = sg.max(axis=-1)
        _, gidx = jax.lax.top_k(group_scores, TOPK_GROUPS)
        keep = jnp.zeros((T, N_GROUPS), bool).at[jnp.arange(T)[:, None], gidx].set(True)
        s_masked = jnp.where(keep[:, :, None], sg, -jnp.inf).reshape(T, E)
        _, idx = jax.lax.top_k(s_masked, TOPK)
        weights = jnp.take_along_axis(original_scores, idx, axis=1) * ROUTE_SCALE
        comb = jnp.zeros((T, E), x.dtype).at[jnp.arange(T)[:, None], idx].add(weights)
        h1 = jnp.einsum('td,eid->tei', xf, w1)
        h3 = jnp.einsum('td,eid->tei', xf, w3)
        h = jax.nn.silu(h1) * h3
        y = jnp.einsum('tei,edi,te->td', h, w2, comb)
        z = jax.nn.silu(xf @ ws1.T) * (xf @ ws3.T) @ ws2.T
        return (y + z).reshape(Bx, Sx, D)
    x = x + _L0_xcond_ref(_layernorm(x, axis=-1), ctx_1024, ctx_1024, condB_tau[:, None], fside_BxS2_0, L0_xcond_Wq, L0_xcond_bq, L0_xcond_Wk, L0_xcond_bk, L0_xcond_Wv, L0_xcond_bv, L0_xcond_Wo, L0_xcond_bo)
    x = x + _L0_ffn_ref(_layernorm(x, axis=-1), L0_ffn_router_w, L0_ffn_router_b, L0_ffn_w1, L0_ffn_b1, L0_ffn_w2, L0_ffn_b2)
    x = x + _L1_xcond_ref(_layernorm(x, axis=-1), ctx_1024, ctx_1024, condB_tau[:, None], fside_BxS2_0, L1_xcond_Wq, L1_xcond_bq, L1_xcond_Wk, L1_xcond_bk, L1_xcond_Wv, L1_xcond_bv, L1_xcond_Wo, L1_xcond_bo)
    x = x + _L1_ffn_ref(_layernorm(x, axis=-1), L1_ffn_Wr, L1_ffn_br, L1_ffn_W1, L1_ffn_b1, L1_ffn_W2, L1_ffn_b2)
    x = x + _L2_xcond_ref(ctx_1024, _layernorm(x, axis=-1), _lenS2, condB_pt, L2_xcond_W_a, L2_xcond_W_c)
    x = x + _L2_ffn_ref(_layernorm(x, axis=-1), L2_ffn_in_proj_w, L2_ffn_in_proj_b, L2_ffn_out_w, L2_ffn_out_b, L2_ffn_ln1_g, L2_ffn_ln1_b, L2_ffn_router_w, L2_ffn_router_b, L2_ffn_w1, L2_ffn_b1, L2_ffn_w2, L2_ffn_b2, L2_ffn_ln2_g, L2_ffn_ln2_b)
    x = x + _L3_xcond_ref(_layernorm(x, axis=-1), ctx_1024, ctx_1024, condB_tau[:, None], fside_BxS2_0, L3_xcond_Wq, L3_xcond_bq, L3_xcond_Wk, L3_xcond_bk, L3_xcond_Wv, L3_xcond_bv, L3_xcond_Wo, L3_xcond_bo)
    x = x + _L3_ffn_ref(_layernorm(x, axis=-1), L3_ffn_gate_w, L3_ffn_gate_bias, L3_ffn_w1, L3_ffn_w2, L3_ffn_w3, L3_ffn_ws1, L3_ffn_ws2, L3_ffn_ws3)
    return x

_drawn_inputs = setup_inputs


def setup_inputs(seed=0):
    import zlib

    import numpy as np

    out = dict(_drawn_inputs(seed))
    spreads = {'L0_ffn_router_b': (0.0, 0.311),
     'L0_ffn_b1': (0.0, 0.8),
     'L0_ffn_b2': (0.0, 0.1),
     'L1_xcond_bq': (0.0, 0.683),
     'L1_xcond_bk': (0.0, 2.0),
     'L1_xcond_bv': (0.0, 0.1),
     'L1_xcond_bo': (0.0, 0.1),
     'L1_ffn_br': (0.0, 0.797),
     'L1_ffn_b1': (0.0, 0.8),
     'L1_ffn_b2': (0.0, 0.553),
     'L2_ffn_in_proj_b': (0.0, 0.755),
     'L2_ffn_out_b': (0.0, 0.1),
     'L2_ffn_ln1_g': (1.0, 0.2),
     'L2_ffn_ln1_b': (0.0, 0.1),
     'L2_ffn_router_b': (0.0, 0.31),
     'L2_ffn_b1': (0.0, 0.8),
     'L2_ffn_b2': (0.0, 0.1),
     'L2_ffn_ln2_g': (1.0, 0.2),
     'L2_ffn_ln2_b': (0.0, 0.1),
     'L3_ffn_gate_bias': (0.0, 0.8)}
    factors = {'condB_pt': 8.0,
     'L0_xcond_bq': 8.0,
     'L0_xcond_bk': 64.0,
     'L0_xcond_bv': 5.139,
     'L0_xcond_bo': 6.435,
     'L0_ffn_w1': 3.815,
     'L0_ffn_w2': 3.392,
     'L1_ffn_Wr': 3.941,
     'L1_ffn_W1': 8.0,
     'L1_ffn_W2': 7.131,
     'L2_ffn_in_proj_w': 4.393,
     'L2_ffn_out_w': 3.733,
     'L2_ffn_w1': 5.265,
     'L2_ffn_w2': 4.864,
     'L3_xcond_bq': 24.236,
     'L3_xcond_bk': 64.0,
     'L3_xcond_bv': 8.0,
     'L3_xcond_bo': 8.0,
     'L3_ffn_gate_w': 8.0,
     'L3_ffn_w1': 8.0,
     'L3_ffn_w2': 8.0,
     'L3_ffn_w3': 8.0,
     'L3_ffn_ws1': 8.0,
     'L3_ffn_ws2': 8.0,
     'L3_ffn_ws3': 8.0}
    for name, (base, spread) in spreads.items():
        noise = np.random.default_rng([zlib.crc32(name.encode()), seed]).standard_normal(out[name].shape)
        drawn = base * np.exp(spread * noise) if base else spread * noise
        out[name] = jnp.asarray(drawn.astype(out[name].dtype))
    for name, factor in factors.items():
        out[name] = (out[name] * factor).astype(out[name].dtype)
    return out
```

```python
from contextlib import ExitStack

import numpy as np

import concourse.bass as bass
from concourse import mybir
from concourse.alu_op_type import AluOpType as ALU

F32 = mybir.dt.float32
BF16 = mybir.dt.bfloat16
U32 = mybir.dt.uint32
I32 = mybir.dt.int32
ACT = mybir.ActivationFunctionType
AX = mybir.AxisListType

P = 128
NB = 4
SQ = 512
TPB = SQ // P
NT = NB * TPB
SK = 77
CK = NB * SK
NH = 16
DK = P // NH
NG = 4
HPG = NH // NG
PAIRS = NH // 2
EPS = 1e-5
ATT_SCALE = float(np.float32(1.0) / np.sqrt(np.float32(DK)))
BIG = 1e30
WINDOW, DEV_POW, MASKED = 16.0, 128.0, 1e9

ATTN, MOE, LOCAL, MHA, GLU = "attn", "moe", "local", "mha", "glu"
LAYERS = [ATTN, MOE, ATTN, MOE, LOCAL, MHA, ATTN, GLU]
NL = len(LAYERS)
ATTN_NO = {0: 0, 2: 1, 6: 2}
EXPERTS = {1: 16, 3: 8, 5: 8, 7: 16}
HIDDEN_CHUNKS = {1: 2, 3: 2, 5: 1}
GLU_PAIRS = 9

ROWS = {}
ROWS_N = 0
for _name, _n in (("bv0", 128), ("bv1", 128), ("bv2", 128), ("bo0", 128), ("bo1", 128), ("bo2", 128),
                  ("rb1", 16), ("rb3", 8), ("rb5", 8), ("rb7", 16), ("in_b", 384), ("out_b", 128),
                  ("ln1_g", 128), ("ln1_b", 128), ("ln2_g", 128), ("ln2_b", 128), ("tau", 4), ("pt", 4)):
    ROWS[_name] = (ROWS_N, ROWS_N + _n)
    ROWS_N += _n

CONSTS = {}
CONSTS_N = 0
for _name, _n in (("ident", 128), ("head_mask", HPG), ("low_rows", 1), ("high_rows", 1), ("pick_head", NH),
                  ("iota16", 16), ("iota77", SK), ("iota_col", 1)):
    CONSTS[_name] = (CONSTS_N, CONSTS_N + _n)
    CONSTS_N += _n

COLS = {}
COLS_N = 0
for _name, _n in (("bq0", 1), ("bq1", 1), ("bq2", 1), ("bk0", 1), ("bk1", 1), ("bk2", 1),
                  ("b1_1", 32), ("b1_3", 16), ("b1_5", 8)):
    COLS[_name] = (COLS_N, COLS_N + _n)
    COLS_N += _n

WIDE = ("wide0", "wide1")
SMALL = ("small0", "small1")
ACC = ("acc0", "acc1")
BANK = {"wide0": 0, "wide1": 2, "small0": 4, "small1": 5, "acc0": 6, "acc1": 7}


def num_row(h):
    return 32 * (h % 4) + 8 * ((h // 4) % 2) + 16 * (h // 8)


class Slots:

    def __init__(self, made, read):
        self.made, self.read = made, read
        self.uses = dict.fromkeys(BANK, 0)
        self.turn = {}
        self.where = {}

    def take(self, job, kind):
        turn = self.turn.get(kind, 0)
        self.turn[kind] = turn + 1
        slot = kind[turn % len(kind)]
        self.uses[slot] += 1
        self.where[job] = (slot, self.uses[slot])
        return slot

    def before(self, job):
        slot, n = self.where[job]
        return (self.read[slot], n - 1) if n > 1 else None

    def is_made(self, job):
        slot, n = self.where[job]
        return self.made[slot], n

    def is_read(self, job):
        slot, n = self.where[job]
        return self.read[slot], n

    def bank(self, job):
        return BANK[self.where[job][0]]


def build(nc, A, out):
    with ExitStack() as ctx:
        def sb(name, shape, dt=F32):
            return ctx.enter_context(nc.sbuf_tensor("s_" + name, shape, dt))

        def sem(name):
            return ctx.enter_context(nc.semaphore(name))

        PS = ctx.enter_context(nc.psum_tensor("psum_all", [P, 8, 512], F32))

        X = sb("x_resid", [P, NT, P])
        XN = sb("x_normed", [P, NT, P])
        XT = sb("x_turned", [P, NB, SQ])
        consts = sb("consts", [P, CONSTS_N])
        rows = sb("rows", [P, ROWS_N])
        cols = sb("cols", [P, COLS_N])
        ctxT = sb("ctxT", [P, CK])
        ctxN = sb("ctxN", [SK, NB, P])
        wattn = sb("wattn", [P, 3, 4, P])
        arena = sb("arena", [P, 8192])
        w1 = {1: arena[:, 0:4096].rearrange("p (e h) -> p e h", e=16)}
        w2 = {1: arena[:, 4096:8192].rearrange("p (e c d) -> p e c d", e=16, c=2)}
        w1[3] = sb("w1_3", [P, 8, 256])
        w2[3] = sb("w2_3", [P, 8, 2, P])
        w1[5] = sb("w1_5", [P, 8, P])
        w2[5] = sb("w2_5", [P, 8, 1, P])
        w1[7], w3_7, w2[7] = (arena[:, 1152 * j:1152 * j + 1152].rearrange("p (e c) -> p e c", e=GLU_PAIRS)
                              for j in range(3))
        b2 = {1: sb("b2_1", [16, P]), 3: sb("b2_3", [8, P]), 5: sb("b2_5", [8, P])}
        router = sb("router", [P, 16 + 8 + 8 + 16])
        rw = {1: router[:, 0:16], 3: router[:, 16:24], 5: router[:, 24:32], 7: router[:, 32:48]}
        wloc = sb("wloc", [P, 3, P])
        win5 = sb("win5", [P, 4 * P])
        QKV = arena[:, 0:6144].rearrange("p (t s c) -> p t s c", t=NB, s=TPB)
        PROD = arena[:, 6144:8192]
        H5 = sb("h5", [P, NT, P])
        PV5 = w1[3][:, :, :].rearrange("p e c -> p (e c)")
        LCTX = w2[3][:, :, :, :].rearrange("p e c d -> p (e c d)").rearrange("p (t j d) -> p t j d", t=NB, j=TPB)

        stats = sb("stats", [P, TPB, 6])
        mv = sb("mv", [P, 2, TPB, 2])
        vare = sb("vare", [P, 2, TPB])
        rstd = sb("rstd", [P, 2, TPB])
        mhalf = sb("minus_half", [P, TPB])

        KS1 = sb("ks1", [P, NH, CK], BF16)
        KS2 = sb("ks2", [P, NH, CK], BF16)
        att = sb("att", [P, 6, SQ])
        spare = att[:, :, :].rearrange("p a b -> p (a b)")
        kf, kr = spare[:, 0:CK], spare[:, CK:2 * CK]
        kparts = spare[:, 2 * CK:2 * CK + 3 * CK // 2].bitcast(BF16).rearrange("p (j s) -> p j s", j=3)
        KB = spare[:, 1078:1078 + 3 * HPG * CK // 2].bitcast(BF16).rearrange("p (j h s) -> p j h s", j=3, h=HPG)
        keep = spare[:, 0:CK].rearrange("p (b s) -> p b s", b=NB)
        negm = spare[:, CK:2 * CK].rearrange("p (b s) -> p b s", b=NB)
        Eloc = spare[:, 2 * CK:3 * CK]
        Gc = spare[0:SK, 3 * CK:3 * CK + NB * P].rearrange("p (b d) -> p b d", b=NB)
        m5 = spare[:, 1536:2560].rearrange("p (a b c) -> p a b c", a=2, b=2)
        V2 = sb("v2", [SK, NB, NH, 32])
        tscale = sb("tscale", [P, NB])
        qf = sb("qf", [P, SQ])
        qr = sb("qr", [P, SQ])
        qparts = sb("qparts", [P, 2, 3, SQ], BF16)
        T1 = sb("t1", [P, 2, NG, SQ], BF16)
        T2 = sb("t2", [P, 2, NG, SQ], BF16)
        nmx = sb("nmx", [P, 2, TPB, NH])
        nmxh = sb("nmxh", [P, TPB, NH], BF16)
        nmx2 = sb("nmx2", [P, 2, TPB, 2 * NH])
        ES = 3
        HS = 3
        hT = sb("hT", [P, HS, 2, SQ])
        Eexp = hT[0:SK, :, :, :]
        gl = hT
        drow = hT[0:1, 0, :, :].rearrange("p a b -> p (a b)")[:, 0:3 * CK].rearrange("p (j s) -> p j s", j=3)
        dparts = hT[0:1, 1, 0, 0:3 * CK // 2].bitcast(BF16).rearrange("p (j s) -> p j s", j=3)
        LPT = T1[:, :, :, :].rearrange("p a b c -> p (a b c)").bitcast(F32).rearrange("p (b c) -> p b c", b=NB)
        LS = (T2[:, :, :, :].rearrange("p a b c -> p (a b c)").bitcast(F32)[:, 0:NB * TPB * SK]
              .rearrange("p (b i s) -> p b i s", b=NB, i=TPB))
        C = sb("combine", [P, NT, 16])
        cT = sb("cT", [64, 2, SQ])
        cT7 = cT[:, 0, :].bitcast(BF16).rearrange("p (a b) -> p a b", a=2)
        lg = sb("lg", [P, TPB, 16])
        v8 = sb("v8", [P, TPB, 8])
        i8 = sb("i8", [P, TPB, 8], U32)
        if8 = sb("if8", [P, TPB, 8])
        oh = sb("oh", [P, TPB, 4, 16])
        r16 = sb("r16", [P, 4, TPB, 16])
        g8 = sb("g8", [P, TPB, 8])
        r1 = sb("r1", [P, 4, TPB])
        lrow = sb("lrow", [P, 6, NB])
        leni = sb("leni", [P, NB], I32)
        gau = sb("gau", [SK, 3, NB])
        c7h = sb("c7h", [P, 2, TPB, 16], BF16)
        c7 = sb("c7", [P, 2, TPB, 64])
        pick7 = sb("pick7", [64, GLU_PAIRS * P], BF16)

        ident = consts[:, 0:128]

        def const(name, n=P):
            a, b = CONSTS[name]
            return consts[0:n, a:b]

        def row(name, n=P):
            a, b = ROWS[name]
            return rows[0:n, a:b]

        def col(name, j=0):
            a = COLS[name][0] + j
            return cols[:, a:a + 1]

        slots = Slots({s: sem(f"made_{s}") for s in BANK}, {s: sem(f"read_{s}") for s in BANK})
        s_x = [sem(f"x_loaded{b}") for b in range(NB)]
        s_c = sem("consts_loaded")
        s_w = {k: sem(f"weights_loaded_{k}") for k in ("a", "m1", "m3", "m5", "m7", "loc")}
        s_out = sem("out_written")
        s_stat = sem("mean_var_ready")
        s_vare = sem("var_eps_ready")
        s_rstd = sem("rstd_ready")
        s_xn = sem("normed_ready")
        s_bo = sem("bo_added")
        s_pool0 = sem("pool_consts_ready")
        s_ones = sem("dve_consts_ready")
        s_delta = sem("delta_parts_ready")
        s_drow = sem("delta_rows_placed")
        s_kb = sem("k_blocks_ready")
        s_ks = [sem(f"k_placed{a}") for a in range(3)]
        s_v2 = sem("v2_ready")
        s_q3 = sem("q_parts_ready")
        s_t1 = [sem(f"t1_placed{u}") for u in range(12)]
        s_t2 = [sem(f"t2_placed{u}") for u in range(12)]
        s_nmx = sem("max_ready")
        s_D = sem("den_ready")
        s_R = sem("rden_ready")
        s_prod = sem("att_out_ready")
        s_lr = sem("logits_ready")
        s_le = sem("logit_exps_ready")
        s_cw = sem("combine_ready")
        s_sil = sem("silu_ready")
        s_glu = sem("glu_hidden_ready")
        s_lg = sem("gauss_arg_ready")
        s_ge = sem("gauss_ready")
        s_gc = sem("gauss_context_ready")
        s_ls = sem("local_scores_ready")
        s_lx = sem("local_exps_ready")
        s_lp = sem("local_probs_ready")
        s_p5 = sem("qk_products_ready")
        s_s5 = sem("mha_shifted_ready")
        s_e5 = sem("mha_exps_ready")
        s_c5 = sem("mha_ctx_ready")
        s_h5 = sem("h_ready")
        s_pin = sem("qkv_ready")
        s_actc = sem("act_chain")
        s_dve = [sem(f"dve_chain{i}") for i in range(NL + 1)]
        s_pv = sem("values_summed")
        s_yglu = sem("glu_summed")

        units = [(L, b) for L in range(NL) for b in range(NB)]
        attn_units = [(L, b) for L, b in units if LAYERS[L] == ATTN]
        n_attn = {u: i for i, u in enumerate(attn_units)}
        moe_units = [(L, b) for L, b in units if LAYERS[L] in (MOE, MHA, GLU)]
        n_moe = {u: i for i, u in enumerate(moe_units)}
        exp_units = [u for u in moe_units if LAYERS[u[0]] == MOE]
        n_exp = {u: i for i, u in enumerate(exp_units)}
        def steps_of(L):
            return PAIRS if LAYERS[L] == ATTN else GLU_PAIRS if LAYERS[L] == GLU else EXPERTS[L]

        def following(u):
            L, b = u
            if b < NB - 1:
                return (L, b + 1)
            return (L + 1, 0) if L + 1 < NL and LAYERS[L + 1] not in (LOCAL, MHA) else None

        def place(n_pieces, steps):
            if n_pieces == 7:
                at = [0, 1, 3, 4, 5, 6, 7]
            else:
                at = [0, 3, 5]
            return [x * steps // 8 for x in at[:n_pieces]]

        norms = [("in", 0, 0)]
        for L, b in units:
            if LAYERS[L] == LOCAL:
                if b == 0:
                    norms += [("in", L, c) for c in range(NB)]
                continue
            if LAYERS[L] == MHA and b == 0:
                norms += [("in", L, c) for c in range(NB)] + [("ln1", L, c) for c in range(NB)]
            nxt = following((L, b))
            if nxt and LAYERS[nxt[0]] != MHA:
                norms.append(("in", *nxt))
            if LAYERS[L] == MHA:
                norms.append(("ln2", L, b))
        n_in = {x[1:]: i + 1 for i, x in enumerate(x for x in norms if x[0] == "in")}

        def values_summed(eng, n):
            u, p = divmod(n, PAIRS)
            half = PAIRS // 2
            if p % half == half - 1:
                eng.wait_ge(*slots.is_made(("PV", *attn_units[u], p // half)))
            else:
                eng.wait_ge(s_pv, (PAIRS - 2) * u + p - p // half + 1)

        def glu_summed(eng, n):
            b, p = divmod(n, GLU_PAIRS)
            if p < GLU_PAIRS - 1:
                eng.wait_ge(s_yglu, (GLU_PAIRS - 1) * b + p + 1)
            else:
                eng.wait_ge(*slots.is_made(("Y", 7, b)))

        block = ctx.enter_context(nc.Block())

        @block.tensor
        def _(pe):
            def start(job, kind):
                slots.take(job, kind)
                w = slots.before(job)
                if w:
                    pe.wait_ge(*w)
                return slots.bank(job)

            def finish(job, ins):
                ins.then_inc(slots.is_made(job)[0], 1)

            def have(job):
                pe.wait_ge(*slots.is_read(job))

            def turn(job, src, ready, value):
                pe.wait_ge(ready, value)
                k = start(job, SMALL)
                for i in range(TPB):
                    mm = pe.transpose(PS[:, k, 128 * i:128 * i + 128], src[:, i, :], ident)
                finish(job, mm)

            def front(L, b):
                turn(("T", L, b), XN[:, TPB * b:TPB * b + TPB, :], s_xn, n_in[L, b])

            def k_prep(a):
                pe.wait_ge(s_w["a"], 16 * 2)
                pe.wait_ge(s_c, 16 * 8)
                k = start(("K", a), SMALL)
                finish(("K", a), pe.matmul(PS[:, k, 0:CK], wattn[:, a, 1, :], ctxT[:, :], start=True, stop=True))
                k = start(("V", a), SMALL)
                for b in range(NB):
                    mm = pe.matmul(PS[0:SK, k, 128 * b:128 * b + 128], ctxT[:, SK * b:SK * b + SK],
                                   wattn[:, a, 2, :], start=True, stop=True)
                finish(("V", a), mm)

            def project_q(L, b):
                have(("T", L, b))
                k = start(("Q", L, b), SMALL)
                finish(("Q", L, b), pe.matmul(PS[:, k, :], wattn[:, ATTN_NO[L], 0, :], XT[:, b, :],
                                              start=True, stop=True))

            def max_scores(L, b, i):
                u = n_attn[L, b]
                if i == 0:
                    pe.wait_ge(s_t1[u], 16 * 12)
                    pe.wait_ge(s_ks[ATTN_NO[L]], 16 * 24)
                    pe.wait_ge(s_drow, 16 * 3)
                    pe.wait_ge(s_ones, 2)
                    pe.wait_ge(s_pool0, 4)
                for g in range(NG):
                    k = start(("M", L, b, i, g), SMALL)
                    o = PS[:, k, 0:HPG * SK].rearrange("p (h s) -> p h s", h=HPG)
                    finish(("M", L, b, i, g),
                           pe.matmul(o, T1[:, u % 2, g, 128 * i:128 * i + 128],
                                     KS1[:, HPG * g:HPG * g + HPG, SK * b:SK * b + SK], start=True, stop=True))

            def turn_max(L, b):
                u = n_attn[L, b]
                pe.wait_ge(s_nmx, u + 1)
                k = start(("MT", L, b), SMALL)
                for i in range(TPB):
                    mm = pe.transpose(PS[0:2 * NH, k, 128 * i:128 * i + 128], nmx2[:, u % 2, i, :], ident)
                finish(("MT", L, b), mm)

            def attn_unit(L, b, hook):
                u = n_attn[L, b]

                def scores(p):
                    k = start(("S", L, b, p), WIDE)
                    for y in range(2):
                        h = 2 * p + y
                        keys = slice(SK * b, SK * b + SK)
                        pe.matmul(PS[0:SK, k + y, :], KS1[:, h, keys], T1[:, u % 2, h // HPG, :],
                                  start=True, stop=False)
                        mm = pe.matmul(PS[0:SK, k + y, :], KS2[:, h, keys], T2[:, u % 2, h // HPG, :],
                                       start=False, stop=True)
                    finish(("S", L, b, p), mm)

                have(("MT", L, b))
                pe.wait_ge(s_t2[u], 16 * 12)
                pe.wait_ge(s_v2, ATTN_NO[L] + 1)
                scores(0)
                scores(1)
                for p in range(PAIRS):
                    if p % (PAIRS // 2) == 0:
                        k = start(("PV", L, b, p // (PAIRS // 2)), ACC)
                    have(("S", L, b, p))
                    for y in range(2):
                        h = 2 * p + y
                        j, sub = h % 4, (h // 4) % 2
                        mm = pe.matmul(PS[32 * j:32 * j + 32, k, :], V2[:, b, h, :],
                                       Eexp[:, (PAIRS * u + p) % ES, y, :], start=(sub == 0), stop=(sub == 1))
                    if p % (PAIRS // 2) == PAIRS // 2 - 1:
                        finish(("PV", L, b, p // (PAIRS // 2)), mm)
                    else:
                        mm.then_inc(s_pv, 1)
                    if p + 2 < PAIRS:
                        scores(p + 2)
                    hook(p)

            def attn_out(L, b):
                pe.wait_ge(s_prod, n_attn[L, b] + 1)
                k = start(("O", L, b), SMALL)
                for i in range(TPB):
                    mm = pe.matmul(PS[:, k, 128 * i:128 * i + 128], att[:, 5, 128 * i:128 * i + 128],
                                   wattn[:, ATTN_NO[L], 3, :], start=True, stop=True)
                finish(("O", L, b), mm)

            def route(L, b):
                have(("T2" if LAYERS[L] == MHA else "T", L, b))
                k = start(("R", L, b), SMALL)
                for i in range(TPB):
                    mm = pe.matmul(PS[:, k, 16 * i:16 * i + EXPERTS[L]], XT[:, b, 128 * i:128 * i + 128], rw[L],
                                   start=True, stop=True)
                finish(("R", L, b), mm)

            def turn_combine(L, b):
                n = n_moe[L, b]
                pe.wait_ge(s_cw, n + 1)
                k = start(("CT", L, b), SMALL)
                for i in range(TPB):
                    if LAYERS[L] == GLU:
                        mm = pe.transpose(PS[0:64, k, 128 * i:128 * i + 128], c7[:, b % 2, i, :], ident)
                    else:
                        mm = pe.transpose(PS[0:EXPERTS[L], k, 128 * i:128 * i + 128],
                                          C[:, TPB * b + i, 0:EXPERTS[L]], ident)
                finish(("CT", L, b), mm)

            def moe_unit(L, b, hook):
                E, NC = EXPERTS[L], HIDDEN_CHUNKS[L]
                pe.wait_ge(s_w[f"m{L}"], 16 * 3)

                def hidden(e):
                    k = start(("H", L, b, e), WIDE)
                    for c in range(NC):
                        mm = pe.matmul(PS[:, k + c, :], w1[L][:, e, 128 * c:128 * c + 128], XT[:, b, :],
                                       start=True, stop=True)
                    finish(("H", L, b, e), mm)

                hidden(0)
                have(("CT", L, b))
                k = start(("B2", L, b), ACC)
                for i in range(TPB):
                    mm = pe.matmul(PS[:, k, 128 * i:128 * i + 128], cT[0:E, b % 2, 128 * i:128 * i + 128],
                                   b2[L][:, :], start=True, stop=True)
                finish(("B2", L, b), mm)
                for e in range(E):
                    if e + 1 < E:
                        hidden(e + 1)
                    k = start(("Y", L, b, e), ACC)
                    have(("H", L, b, e))
                    hs = (E * b + e) % HS
                    for i in range(TPB):
                        for c in range(NC):
                            mm = pe.matmul(PS[:, k, 128 * i:128 * i + 128],
                                           hT[:, hs, c, 128 * i:128 * i + 128],
                                           w2[L][:, e, c, :], start=(c == 0), stop=(c == NC - 1))
                    finish(("Y", L, b, e), mm)
                    hook(e)

            def glu_unit(L, b, hook):
                pe.wait_ge(s_w["m7"], 16 * 3)
                pe.wait_ge(s_ones, 3)

                def hidden(p):
                    k = start(("H", L, b, p), WIDE)
                    pe.matmul(PS[:, k, :], w1[7][:, p, :], XT[:, b, :], start=True, stop=True)
                    finish(("H", L, b, p),
                           pe.matmul(PS[:, k + 1, :], w3_7[:, p, :], XT[:, b, :], start=True, stop=True))
                    k = start(("CB", L, b, p), SMALL)
                    finish(("CB", L, b, p), pe.matmul(PS[:, k, :], pick7[:, 128 * p:128 * p + 128],
                                                      cT7[:, b % 2, :], start=True, stop=True))

                have(("CT", L, b))
                hidden(0)
                for p in range(GLU_PAIRS):
                    if p + 1 < GLU_PAIRS:
                        hidden(p + 1)
                    if p == 0:
                        k = start(("Y", L, b), ACC)
                    have(("CB", L, b, p))
                    for i in range(TPB):
                        mm = pe.matmul(PS[:, k, 128 * i:128 * i + 128], gl[:, (GLU_PAIRS * b + p) % 3, 1, 128 * i:128 * i + 128],
                                       w2[7][:, p, :], start=(p == 0 and i == 0), stop=(p == GLU_PAIRS - 1),
                                       skip_group_check=True)
                    if p == GLU_PAIRS - 1:
                        finish(("Y", L, b), mm)
                    else:
                        mm.then_inc(s_yglu, 1)
                    hook(p)

            def local_layer(L):
                for b in range(NB):
                    front(L, b)
                pe.wait_ge(s_w["loc"], 16)
                k = start(("E4",), SMALL)
                finish(("E4",), pe.matmul(PS[:, k, 0:CK], wloc[:, 0, :], ctxT[:, :], start=True, stop=True))
                for b in range(NB):
                    have(("T", L, b))
                    have(("E4",))
                    k = start(("LS", b), SMALL)
                    for i in range(TPB):
                        mm = pe.matmul(PS[:, k, SK * i:SK * i + SK], XT[:, b, 128 * i:128 * i + 128],
                                       Eloc[:, SK * b:SK * b + SK], start=True, stop=True)
                    finish(("LS", b), mm)
                for b in range(NB):
                    pe.wait_ge(s_lp, b + 1)
                    k = start(("LT", b), SMALL)
                    for i in range(TPB):
                        mm = pe.transpose(PS[0:SK, k, 128 * i:128 * i + 128], LS[:, b, i, :], ident)
                    finish(("LT", b), mm)
                pe.wait_ge(s_gc, 1)
                for b in range(NB):
                    have(("LT", b))
                    k = start(("LC", b), SMALL)
                    finish(("LC", b), pe.matmul(PS[:, k, :], Gc[:, b, :], LPT[0:SK, b, :],
                                                start=True, stop=True))
                for b in range(NB):
                    have(("LC", b))
                    k = start(("LO", b), SMALL)
                    for i in range(TPB):
                        o = PS[:, k, 128 * i:128 * i + 128]
                        pe.matmul(o, hT[:, b % HS, b // HS, 128 * i:128 * i + 128], wloc[:, 1, :],
                                  start=True, stop=False)
                        mm = pe.matmul(o, XT[:, b, 128 * i:128 * i + 128], wloc[:, 2, :], start=False, stop=True)
                    finish(("LO", b), mm)

            def mha_layer(L):
                for b in range(NB):
                    front(L, b)
                pe.wait_ge(s_w["m5"], 16 * 3)
                for b in range(NB):
                    have(("T", L, b))
                    for i in range(TPB):
                        k = start(("QKV", b, i), SMALL)
                        finish(("QKV", b, i), pe.matmul(PS[:, k, 0:3 * P], XT[:, b, 128 * i:128 * i + 128],
                                                        win5[:, 0:3 * P], start=True, stop=True))
                pe.wait_ge(s_c5, TPB)
                for b in range(NB):
                    k = start(("AT", b), SMALL)
                    for i in range(TPB):
                        mm = pe.transpose(PS[:, k, 128 * i:128 * i + 128], LCTX[:, b, i, :], ident)
                    finish(("AT", b), mm)
                    have(("AT", b))
                    k = start(("AO", b), SMALL)
                    for i in range(TPB):
                        mm = pe.matmul(PS[:, k, 128 * i:128 * i + 128],
                                       hT[:, b % HS, b // HS, 128 * i:128 * i + 128],
                                       win5[:, 3 * P:4 * P], start=True, stop=True)
                    finish(("AO", b), mm)
                mha_front(L, 0)
                route(L, 0)
                turn_combine(L, 0)

            def mha_front(L, b):
                turn(("T2", L, b), H5[:, TPB * b:TPB * b + TPB, :], s_h5, b + 1)

            def pieces(u):
                if u is None:
                    return []
                L, b = u
                if LAYERS[L] == ATTN:
                    return ([lambda: front(L, b), lambda: project_q(L, b)]
                            + [lambda i=i: max_scores(L, b, i) for i in range(TPB)] + [lambda: turn_max(L, b)])
                first = (lambda: mha_front(L, b)) if LAYERS[L] == MHA else (lambda: front(L, b))
                return [first, lambda: route(L, b), lambda: turn_combine(L, b)]

            k_prep(0)
            for f in pieces((0, 0)):
                f()
            for n, (L, b) in enumerate(units):
                if LAYERS[L] == LOCAL:
                    if b == 0:
                        attn_done = None
                        local_layer(L)
                    continue
                if LAYERS[L] == MHA and b == 0:
                    mha_layer(L)
                todo = pieces(following((L, b)))
                at = place(len(todo), steps_of(L))
                prev = units[n - 1] if n and LAYERS[units[n - 1][0]] == ATTN else None

                def hook(step):
                    for f, x in zip(todo, at):
                        if x == step:
                            f()
                    if step == 2 and prev:
                        attn_out(*prev)
                    if step == 3 and (L, b) == (1, 2):
                        k_prep(1)
                    if step == 3 and (L, b) == (3, 1):
                        k_prep(2)

                {ATTN: attn_unit, MOE: moe_unit, MHA: moe_unit, GLU: glu_unit}[LAYERS[L]](L, b, hook)

        @block.vector
        def _(dve):
            count = [0] * (NL + 1)
            stage = [0]

            def link(ins):
                j = stage[0]
                count[j] += 1
                ins.then_inc(s_dve[j], 1)
                dve.wait_ge(s_dve[j], count[j])

            def made(job):
                dve.wait_ge(*slots.is_made(job))
                return slots.bank(job)

            def read(job, ins):
                ins.then_inc(slots.is_read(job)[0], 1)

            def settled(job):
                dve.wait_ge(*slots.is_read(job))

            def norm(which, L, b, src, dst, post=None):
                n = norms.index((which, L, b))
                if n >= 1:
                    dve.wait_ge(s_stat, n)
                for i in range(TPB):
                    ins = dve.bn_stats(stats[:, i, :], src[:, i, :])
                link(ins)
                for i in range(TPB):
                    ins = dve.bn_aggr(mv[:, n % 2, i, :], stats[:, i, :])
                ins.then_inc(s_stat, 1)
                dve.wait_ge(s_stat, n + 1)
                dve.wait_ge(s_rstd, n + 1)
                for i in range(TPB):
                    ins = dve.tensor_scalar(dst[:, i, :], src[:, i, :], mv[:, n % 2, i, 0:1], rstd[:, n % 2, i:i + 1],
                                            ALU.subtract, ALU.mult)
                if which == "in":
                    ins.then_inc(s_xn, 1)
                else:
                    link(ins)

            def tiles(t, b):
                return t[:, TPB * b:TPB * b + TPB, :]

            def front(L, b):
                if L == 0:
                    dve.wait_ge(s_x[b], 16)
                norm("in", L, b, tiles(X, b), tiles(XN, b))

            def delta_parts():
                link(dve.tensor_scalar(drow[:, 1, :], drow[:, 0, :], ATT_SCALE, None, ALU.mult))
                link(dve.tensor_copy(dparts[:, 0, :], drow[:, 1, :]))
                link(dve.tensor_tensor(drow[:, 2, :], drow[:, 1, :], dparts[:, 0, :], ALU.subtract))
                link(dve.tensor_copy(dparts[:, 1, :], drow[:, 2, :]))
                dve.tensor_tensor(dparts[:, 2, :], drow[:, 2, :], dparts[:, 1, :], ALU.subtract).then_inc(s_delta, 1)

            def k_prep(a):
                k = made(("K", a))
                read(("K", a), dve.tensor_scalar(kf[:, :], PS[:, k, 0:CK], col(f"bk{a}"), None, ALU.add))
                settled(("K", a))
                link(dve.tensor_copy(kparts[:, 0, :], kf[:, :]))
                link(dve.tensor_tensor(kr[:, :], kf[:, :], kparts[:, 0, :], ALU.subtract))
                link(dve.tensor_copy(kparts[:, 1, :], kr[:, :]))
                link(dve.tensor_tensor(kparts[:, 2, :], kr[:, :], kparts[:, 1, :], ALU.subtract))
                if a:
                    dve.wait_ge(s_ks[a - 1], 16 * 24)
                mask = const("head_mask")
                for j in range(3):
                    for h in range(HPG):
                        ins = dve.tensor_scalar(KB[:, j, h, :], kparts[:, j, :], mask[:, h:h + 1], None, ALU.mult)
                ins.then_inc(s_kb, 1)
                k = made(("V", a))
                dve.wait_ge(s_pool0, 3)
                v = PS[0:SK, k, :].rearrange("s (b h d) -> s b h d", b=NB, h=NH)
                bias = row(f"bv{a}", SK).rearrange("s (h d) -> s h d", h=NH)
                for half in range(2):
                    for sub in range(2):
                        hs = slice(8 * half + 4 * sub, 8 * half + 4 * sub + 4)
                        c0 = 16 * half + 8 * sub
                        for b in range(NB):
                            ins = dve.tensor_tensor(V2[:, b, hs, c0:c0 + DK], v[:, b, hs, :], bias[:, hs, :], ALU.add)
                read(("V", a), ins)
                settled(("V", a))
                dve.engine_nop().then_inc(s_v2, 1)

            def split_q(L, b):
                u = n_attn[L, b]
                k = made(("Q", L, b))
                if u:
                    dve.wait_ge(s_q3, u)
                read(("Q", L, b), dve.tensor_scalar(qf[:, :], PS[:, k, :], col(f"bq{ATTN_NO[L]}"), tscale[:, b:b + 1],
                                                    ALU.add, ALU.mult))
                settled(("Q", L, b))
                if u >= 2:
                    dve.wait_ge(s_t1[u - 2], 16 * 12)
                    dve.wait_ge(s_t2[u - 2], 16 * 12)
                q = qparts[:, u % 2, :, :]
                link(dve.tensor_copy(q[:, 0, :], qf[:, :]))
                link(dve.tensor_tensor(qr[:, :], qf[:, :], q[:, 0, :], ALU.subtract))
                link(dve.tensor_copy(q[:, 1, :], qr[:, :]))
                dve.tensor_tensor(q[:, 2, :], qr[:, :], q[:, 1, :], ALU.subtract).then_inc(s_q3, 1)

            def max_scores(L, b, i):
                u = n_attn[L, b]
                if u >= 1 and i == 0:
                    dve.wait_ge(s_nmx, u)
                for g in range(NG):
                    job = ("M", L, b, i, g)
                    k = made(job)
                    read(job, dve.tensor_reduce(nmx[:, u % 2, i, HPG * g:HPG * g + HPG],
                                                PS[:, k, 0:HPG * SK].rearrange("p (h s) -> p h s", h=HPG),
                                                AX.X, ALU.max, negate=True))

            def max_parts(L, b):
                u = n_attn[L, b]
                settled(("M", L, b, TPB - 1, NG - 2))
                settled(("M", L, b, TPB - 1, NG - 1))
                m = nmx[:, u % 2, :, :]
                link(dve.tensor_copy(nmxh[:, :, :], m))
                dve.tensor_copy(nmx2[:, u % 2, :, 0:NH], nmxh[:, :, :])
                dve.tensor_tensor(nmx2[:, u % 2, :, NH:2 * NH], m, nmxh[:, :, :], ALU.subtract).then_inc(s_nmx, 1)

            def join_heads(L, b):
                u = n_attn[L, b]
                low, high = const("low_rows"), const("high_rows")
                ja, jb = ("PV", L, b, 0), ("PV", L, b, 1)
                k = made(ja)
                dve.tensor_scalar(att[:, 0, :], PS[:, k, :], high, None, ALU.mult)
                read(ja, dve.tensor_scalar(att[:, 1, :], PS[:, k, :], low, None, ALU.mult))
                settled(ja)
                k = made(jb)
                dve.scalar_tensor_tensor(att[:, 2, :], PS[:, k, :], low, att[:, 0, :], ALU.mult, ALU.add).then_inc(s_D, 1)
                read(jb, dve.scalar_tensor_tensor(att[:, 3, :], PS[:, k, :], high, att[:, 1, :], ALU.mult, ALU.add))

            def divide_heads(L, b):
                u = n_attn[L, b]
                settled(("PV", L, b, 1))
                dve.wait_ge(s_R, u + 1)
                link(dve.stream_shuffle(att[:, 0, :], att[:, 4, :], [(i + 16) % 32 for i in range(32)]))
                dve.tensor_tensor(att[:, 5, :], att[:, 3, :], att[:, 0, :], ALU.mult).then_inc(s_prod, 1)

            def add_out(L, b):
                k = made(("O", L, b))
                dve.wait_ge(s_bo, n_attn[L, b] + 1)
                x = tiles(X, b)
                read(("O", L, b), dve.tensor_tensor(x, PS[:, k, :].rearrange("p (i d) -> p i d", i=TPB), x, ALU.add))
                settled(("O", L, b))

            def spread(ap, n):
                return ap.unsqueeze(len(ap.shape)).to_broadcast(list(ap.shape) + [n])

            def over(ap, n):
                return ap.unsqueeze(1).to_broadcast([ap.shape[0], n] + list(ap.shape[1:]))

            def top(values, n=16):
                for i in range(TPB):
                    ins = dve.max(v8[:, i, :], values[:, i, 0:n])
                link(ins)
                for i in range(TPB):
                    ins = dve.max_index(i8[:, i, :], v8[:, i, :], values[:, i, 0:n])
                link(ins)
                link(dve.tensor_copy(if8[:, :, :], i8[:, :, :]))

            def chosen(dst, K, n):
                io = const("iota16")[:, 0:n]
                for i in range(TPB):
                    ins = dve.tensor_tensor(oh[:, i, 0:K, 0:n], over(io, K), spread(if8[:, i, 0:K], n), ALU.is_equal)
                link(ins)
                for i in range(TPB):
                    ins = dve.tensor_reduce(dst[:, i, :], oh[:, i, 0:K, 0:n].rearrange("p k e -> p e k"), AX.X, ALU.add)
                link(ins)

            def logits_of(L, b):
                k = made(("R", L, b))
                E = EXPERTS[L]
                z = PS[:, k, 0:16 * TPB].rearrange("p (i e) -> p i e", i=TPB)[:, :, 0:E]
                read(("R", L, b), dve.tensor_tensor(lg[:, :, 0:E], z, over(row(f"rb{L}"), TPB), ALU.add))
                settled(("R", L, b))
                return lg[:, :, 0:E]

            def route_moe(L, b):
                E = EXPERTS[L]
                n = n_moe[L, b]
                if n:
                    dve.wait_ge(s_cw, n)
                z = logits_of(L, b)
                top(z, E)
                w = r16[:, 0, :, 0:E]
                x = n_exp[L, b]
                dve.tensor_tensor(w, z, spread(v8[:, :, 0], E), ALU.subtract).then_inc(s_lr, 1)
                mask = r16[:, 1, :, 0:E]
                chosen(mask, 4 if L == 1 else 1, E)
                dve.wait_ge(s_le, x + 1)
                ex = r16[:, 2, :, 0:E]
                em = r16[:, 3, :, 0:E]
                link(dve.tensor_tensor(em, ex, mask, ALU.mult))
                link(dve.tensor_reduce(r1[:, 0, :], em if L == 1 else ex, AX.X, ALU.add))
                link(dve.reciprocal(r1[:, 1, :], r1[:, 0, :]))
                dve.tensor_tensor(tiles(C, b)[:, :, 0:E], em, spread(r1[:, 1, :], E), ALU.mult).then_inc(s_cw, 1)
                dve.wait_ge(s_cw, n + 1)

            def route_mha(L, b):
                E = EXPERTS[L]
                n = n_moe[L, b]
                z = logits_of(L, b)
                top(z, E)
                link(dve.tensor_tensor(r1[:, 2, :], if8[:, :, 0], if8[:, :, 1], ALU.max))
                dve.tensor_tensor(tiles(C, b)[:, :, 0:E], over(const("iota16")[:, 0:E], TPB), spread(r1[:, 2, :], E),
                                  ALU.is_equal).then_inc(s_cw, 1)
                dve.wait_ge(s_cw, n + 1)

            def route_glu(L, b):
                n = n_moe[L, b]
                dve.wait_ge(s_cw, n)
                dve.wait_ge(*slots.is_read(("R", L, b)))
                sig, s = r16[:, 0, :, :], r16[:, 1, :, :]
                link(dve.tensor_tensor(s, sig, over(row("rb7"), TPB), ALU.add))
                link(dve.tensor_reduce(g8[:, :, 0:4], s.rearrange("p i (g e) -> p i g e", g=4), AX.X, ALU.max))
                top(g8, 8)
                kg = r16[:, 2, :, 0:4]
                chosen(kg, 2, 4)
                kb = r16[:, 2, :, 4:8]
                link(dve.tensor_scalar(kb, kg, BIG, BIG, ALU.mult, ALU.subtract))
                sm = r16[:, 3, :, :]
                for i in range(TPB):
                    ins = dve.tensor_tensor(sm[:, i, :].rearrange("p (g e) -> p g e", g=4),
                                            s[:, i, :].rearrange("p (g e) -> p g e", g=4), spread(kg[:, i, :], 4), ALU.mult)
                link(ins)
                for i in range(TPB):
                    v = sm[:, i, :].rearrange("p (g e) -> p g e", g=4)
                    ins = dve.tensor_tensor(v, v, spread(kb[:, i, :], 4), ALU.add)
                link(ins)
                top(sm)
                mask = r16[:, 2, :, :]
                chosen(mask, 4, 16)
                c = tiles(C, b)
                link(dve.tensor_tensor(c, sig, mask, ALU.mult))
                d = c7[:, b % 2, :, :]
                link(dve.tensor_copy(c7h[:, 0, :, :], c))
                dve.tensor_copy(d[:, :, 0:16], c7h[:, 0, :, :])
                link(dve.tensor_tensor(lg[:, :, :], c, c7h[:, 0, :, :], ALU.subtract))
                link(dve.tensor_copy(c7h[:, 1, :, :], lg[:, :, :]))
                dve.tensor_copy(d[:, :, 16:32], c7h[:, 1, :, :])
                dve.tensor_tensor(d[:, :, 32:48], lg[:, :, :], c7h[:, 1, :, :], ALU.subtract).then_inc(s_cw, 1)
                dve.wait_ge(s_cw, n + 1)

            def moe_unit(L, b, hook):
                dst = H5 if L == 5 else X
                E = EXPERTS[L]
                k = made(("B2", L, b))
                d = tiles(dst, b)
                read(("B2", L, b), dve.tensor_tensor(d, PS[:, k, :].rearrange("p (i d) -> p i d", i=TPB), d, ALU.add))
                last = ("B2", L, b)
                for e in range(E):
                    k = made(("Y", L, b, e))
                    settled(last)
                    for i in range(TPB):
                        t = TPB * b + i
                        ins = dve.scalar_tensor_tensor(dst[:, t, :], PS[:, k, 128 * i:128 * i + 128],
                                                       C[:, t, e:e + 1], dst[:, t, :], ALU.mult, ALU.add)
                    last = ("Y", L, b, e)
                    read(last, ins)
                    hook(e)
                settled(last)
                if L == 5:
                    y = tiles(XN, b)
                    norm("ln2", L, b, d, y)
                    g, s = over(row("ln2_g"), TPB), over(row("ln2_b"), TPB)
                    link(dve.tensor_tensor(y, y, g, ALU.mult))
                    link(dve.tensor_tensor(y, y, s, ALU.add))
                    link(dve.tensor_tensor(tiles(X, b), tiles(X, b), y, ALU.add))

            def glu_unit(L, b, hook):
                for p in range(GLU_PAIRS):
                    x = (GLU_PAIRS * b + p) % 3
                    n = GLU_PAIRS * b + p
                    dve.wait_ge(s_sil, n + 1)
                    k = made(("H", L, b, p))
                    read(("H", L, b, p), dve.tensor_tensor(gl[:, x, 0, :], PS[:, k + 1, :], gl[:, x, 0, :], ALU.mult))
                    settled(("H", L, b, p))
                    k = made(("CB", L, b, p))
                    if n >= 3:
                        glu_summed(dve, n - 3)
                    read(("CB", L, b, p), dve.tensor_tensor(gl[:, x, 1, :], PS[:, k, :], gl[:, x, 0, :], ALU.mult))
                    hook(p)
                k = made(("Y", L, b))
                x = tiles(X, b)
                read(("Y", L, b), dve.tensor_tensor(x, PS[:, k, :].rearrange("p (i d) -> p i d", i=TPB), x, ALU.add))

            def window_prep():
                pt = row("pt")
                st, en, lf = lrow[:, 0, :], lrow[:, 1, :], lrow[:, 2, :]
                dve.wait_ge(s_ks[2], 16 * 24)
                link(dve.tensor_copy(lf, leni[:, :]))
                link(dve.tensor_scalar(st, pt, WINDOW, 0.0, ALU.subtract, ALU.max))
                link(dve.tensor_scalar(lrow[:, 3, :], pt, WINDOW, None, ALU.add))
                link(dve.tensor_tensor(en, lrow[:, 3, :], lf, ALU.min))
                io = const("iota77")
                for b in range(NB):
                    ins = dve.tensor_scalar(negm[:, b, :], io, st[:, b:b + 1], None, ALU.is_ge)
                link(ins)
                for b in range(NB):
                    ins = dve.scalar_tensor_tensor(keep[:, b, :], io, en[:, b:b + 1], negm[:, b, :], ALU.is_le, ALU.mult)
                link(ins)
                link(dve.tensor_scalar(negm[:, :, :], keep[:, :, :], MASKED, MASKED, ALU.mult, ALU.subtract))
                link(dve.tensor_scalar(gau[:, 0, :], row("pt", SK), const("iota_col", SK), None, ALU.subtract))
                dve.tensor_tensor(gau[:, 1, :], gau[:, 0, :], gau[:, 0, :], ALU.mult).then_inc(s_lg, 1)

            def local_layer(L):
                dve.wait_ge(s_ge, 1)
                for b in range(NB):
                    ins = dve.tensor_scalar(Gc[:, b, :], ctxN[:, b, :], gau[:, 2, b:b + 1], None, ALU.mult)
                ins.then_inc(s_gc, 1)
                for b in range(NB):
                    front(L, b)
                for b in range(NB):
                    k = made(("LS", b))
                    s = LS[:, b, :, :]
                    read(("LS", b), dve.tensor_tensor(s, PS[:, k, 0:TPB * SK].rearrange("p (i s) -> p i s", i=TPB),
                                                      over(keep[:, b, :], TPB), ALU.mult))
                    settled(("LS", b))
                    link(dve.tensor_tensor(s, s, over(negm[:, b, :], TPB), ALU.add))
                    link(dve.tensor_reduce(r1[:, 0, :], s, AX.X, ALU.max))
                    dve.tensor_tensor(s, s, spread(r1[:, 0, :], SK), ALU.subtract).then_inc(s_ls, 1)
                for b in range(NB):
                    s = LS[:, b, :, :]
                    dve.wait_ge(s_lx, b + 1)
                    link(dve.tensor_reduce(r1[:, 1, :], s, AX.X, ALU.add))
                    link(dve.reciprocal(r1[:, 2, :], r1[:, 1, :]))
                    dve.tensor_tensor(s, s, spread(r1[:, 2, :], SK), ALU.mult).then_inc(s_lp, 1)
                for b in range(NB):
                    dve.wait_ge(*slots.is_read(("LO", b)))
                    x = tiles(X, b)
                    link(dve.tensor_tensor(x, tiles(XN, b), x, ALU.add))

            def mha_layer(L):
                for b in range(NB):
                    front(L, b)
                for b in range(NB):
                    for i in range(TPB):
                        k = made(("QKV", b, i))
                        read(("QKV", b, i), dve.tensor_tensor(QKV[:, b, i, :], PS[:, k, 0:3 * P], row("in_b"), ALU.add))
                settled(("QKV", NB - 1, TPB - 1))
                settled(("QKV", NB - 1, TPB - 2))
                dve.engine_nop().then_inc(s_pin, 1)
                for j in range(TPB):
                    dve.wait_ge(s_p5, j + 1)
                    sc = m5[:, j % 2, 0, :]
                    link(dve.tensor_reduce(sc, PROD.rearrange("p (x d) -> p x d", d=DK), AX.X, ALU.add))
                    sc4 = sc.rearrange("p (t s h) -> p t s h", t=NB, s=NB)
                    mx = m5[:, j % 2, 1, 0:NB * NH].rearrange("p (t h) -> p t h", t=NB)
                    link(dve.tensor_reduce(mx, sc4.rearrange("p t s h -> p t h s"), AX.X, ALU.max))
                    for t in range(NB):
                        ins = dve.tensor_tensor(sc4[:, t, :, :], sc4[:, t, :, :], over(mx[:, t, :], NB), ALU.subtract)
                    ins.then_inc(s_s5, 1)
                    dve.wait_ge(s_e5, j + 1)
                    sm = m5[:, j % 2, 1, 64:128].rearrange("p (t h) -> p t h", t=NB)
                    rs = m5[:, j % 2, 1, 128:192].rearrange("p (t h) -> p t h", t=NB)
                    link(dve.tensor_reduce(sm, sc4.rearrange("p t s h -> p t h s"), AX.X, ALU.add))
                    link(dve.reciprocal(rs, sm))
                    for t in range(NB):
                        ins = dve.tensor_tensor(sc4[:, t, :, :], sc4[:, t, :, :], over(rs[:, t, :], NB), ALU.mult)
                    link(ins)
                    pv = PV5.rearrange("p (t s c) -> p t s c", t=NB, s=NB)
                    for t in range(NB):
                        for s in range(NB):
                            ins = dve.tensor_tensor(pv[:, t, s, :].rearrange("p (h d) -> p h d", h=NH),
                                                    spread(sc4[:, t, s, :], DK),
                                                    QKV[:, s, j, 2 * P:3 * P].rearrange("p (h d) -> p h d", h=NH), ALU.mult)
                    link(ins)
                    for t in range(NB):
                        ins = dve.tensor_reduce(LCTX[:, t, j, :], pv[:, t, :, :].rearrange("p s c -> p c s"), AX.X, ALU.add)
                    ins.then_inc(s_c5, 1)
                    dve.wait_ge(s_c5, j + 1)
                for b in range(NB):
                    k = made(("AO", b))
                    h = tiles(H5, b)
                    read(("AO", b), dve.tensor_tensor(h, PS[:, k, :].rearrange("p (i d) -> p i d", i=TPB), tiles(XN, b), ALU.add))
                    settled(("AO", b))
                    link(dve.tensor_tensor(h, h, over(row("out_b"), TPB), ALU.add))
                    norm("ln1", L, b, h, h)
                    link(dve.tensor_tensor(h, h, over(row("ln1_g"), TPB), ALU.mult))
                    dve.tensor_tensor(h, h, over(row("ln1_b"), TPB), ALU.add).then_inc(s_h5, 1)
                    dve.wait_ge(s_h5, b + 1)
                route_mha(L, 0)

            def pieces(u):
                if u is None:
                    return []
                L, b = u
                if LAYERS[L] == ATTN:
                    return ([lambda: front(L, b), lambda: split_q(L, b)]
                            + [lambda i=i: max_scores(L, b, i) for i in range(TPB)] + [lambda: max_parts(L, b)])
                first = (lambda: None) if LAYERS[L] == MHA else (lambda: front(L, b))
                r = {MOE: route_moe, MHA: route_mha, GLU: route_glu}[LAYERS[L]]
                return [first, lambda: r(L, b), lambda: None]

            stage[0] = NL
            dve.wait_ge(s_c, 16 * 8)
            dve.memset(KS1[96:128, :, :], 0.0).then_inc(s_ones, 1)
            dve.tensor_copy(KS2[96:128, :, :], spread(const("pick_head")[96:128, :], CK)).then_inc(s_ones, 1)
            dve.tensor_copy(pick7[:, :], XN[0:64, 0:GLU_PAIRS, :].rearrange("p a b -> p (a b)")).then_inc(s_ones, 1)
            link(dve.tensor_scalar(tscale[:, :], row("tau"), ATT_SCALE, None, ALU.mult))
            delta_parts()
            link(dve.memset(g8[:, :, :], -3e38))
            k_prep(0)
            link(dve.memset(c7[:, :, :, 48:64], 0.0))
            link(dve.memset(c7[:, :, :, 48:49], 1.0))
            for f in pieces((0, 0)):
                f()
            for n, (L, b) in enumerate(units):
                stage[0] = L
                if LAYERS[L] == LOCAL:
                    if b == 0:
                        local_layer(L)
                    continue
                if LAYERS[L] == MHA and b == 0:
                    mha_layer(L)
                todo = pieces(following((L, b)))
                at = place(len(todo), steps_of(L))
                prev = units[n - 1] if n and LAYERS[units[n - 1][0]] == ATTN else None
                if prev:
                    join_heads(*prev)

                def hook(step):
                    for f, x in zip(todo, at):
                        if x == step:
                            f()
                    if step == 0 and prev:
                        divide_heads(*prev)
                    if step == 2 and prev:
                        add_out(*prev)
                    if step == 3 and (L, b) == (1, 2):
                        k_prep(1)
                    if step == 3 and (L, b) == (3, 1):
                        k_prep(2)
                    if step == 3 and (L, b) == (3, 2):
                        window_prep()

                if LAYERS[L] == ATTN:
                    for p in range(PAIRS):
                        hook(p)
                else:
                    {MOE: moe_unit, MHA: moe_unit, GLU: glu_unit}[LAYERS[L]](L, b, hook)


        @block.scalar
        def _(act):
            chain = [0]

            def made(job):
                act.wait_ge(*slots.is_made(job))
                return slots.bank(job)

            def read(job, ins):
                ins.then_inc(slots.is_read(job)[0], 1)

            def move(job, dst, src):
                k = made(job)
                read(job, nc.scalar.copy(dst, src(k)))

            def front(L, b):
                move(("T", L, b), XT[:, b, :], lambda k: PS[:, k, :])

            def place_max(L, b):
                u = n_attn[L, b]
                move(("MT", L, b), T2[96:128, u % 2, :, :],
                     lambda k: PS[0:2 * NH, k, :].unsqueeze(1).to_broadcast([2 * NH, NG, SQ]))

            def attn_unit(L, b, hook):
                u = n_attn[L, b]
                for p in range(PAIRS):
                    k = made(("S", L, b, p))
                    if PAIRS * u + p >= ES:
                        values_summed(act, PAIRS * u + p - ES)
                    read(("S", L, b, p), nc.scalar.activation(Eexp[:, (PAIRS * u + p) % ES, :, :], PS[0:SK, k:k + 2, :], ACT.Exp))
                    hook(p)

            def invert_sums(L, b):
                u = n_attn[L, b]
                act.wait_ge(s_D, u + 1)
                chain[0] += 1
                nc.scalar.activation(att[:, 4, :], att[:, 2, :], ACT.Ln).then_inc(s_actc, 1)
                act.wait_ge(s_actc, chain[0])
                nc.scalar.activation(att[:, 4, :], att[:, 4, :], ACT.Exp, scale=-1.0).then_inc(s_R, 1)

            def route(L, b):
                E = EXPERTS[L]
                if LAYERS[L] == GLU:
                    act.wait_ge(s_cw, n_moe[L, b])
                    k = made(("R", L, b))
                    read(("R", L, b), nc.scalar.activation(r16[:, 0, :, :], PS[:, k, 0:16 * TPB].rearrange("p (i e) -> p i e", i=TPB),
                                                           ACT.Sigmoid))
                elif LAYERS[L] == MOE:
                    act.wait_ge(s_lr, n_exp[L, b] + 1)
                    nc.scalar.activation(r16[:, 2, :, 0:E], r16[:, 0, :, 0:E], ACT.Exp).then_inc(s_le, 1)

            def turn_combine(L, b):
                if LAYERS[L] == GLU:
                    move(("CT", L, b), cT7[:, b % 2, :], lambda k: PS[0:64, k, :])
                else:
                    move(("CT", L, b), cT[0:EXPERTS[L], b % 2, :], lambda k: PS[0:EXPERTS[L], k, :])

            def moe_unit(L, b, hook):
                E, NC = EXPERTS[L], HIDDEN_CHUNKS[L]
                for e in range(E):
                    k = made(("H", L, b, e))
                    n = E * b + e
                    if n >= HS:
                        act.wait_ge(*slots.is_made(("Y", L, (n - HS) // E, (n - HS) % E)))
                    for c in range(NC):
                        ins = nc.scalar.activation(hT[:, n % HS, c, :], PS[:, k + c, :], ACT.Relu if L == 3 else ACT.Gelu,
                                                   bias=col(f"b1_{L}", NC * e + c))
                    read(("H", L, b, e), ins)
                    hook(e)

            def glu_unit(L, b, hook):
                for p in range(GLU_PAIRS):
                    n = GLU_PAIRS * b + p
                    k = made(("H", L, b, p))
                    if n >= 3:
                        m = n - 3
                        act.wait_ge(*slots.is_read(("CB", L, m // GLU_PAIRS, m % GLU_PAIRS)))
                    nc.scalar.activation(gl[:, n % 3, 0, :], PS[:, k, :], ACT.Silu).then_inc(s_sil, 1)
                    hook(p)

            def local_layer(L):
                act.wait_ge(s_lg, 1)
                nc.scalar.activation(gau[:, 2, :], gau[:, 1, :], ACT.Exp, scale=-1.0 / DEV_POW).then_inc(s_ge, 1)
                for b in range(NB):
                    front(L, b)
                move(("E4",), Eloc, lambda k: PS[:, k, 0:CK])
                for b in range(NB):
                    act.wait_ge(s_ls, b + 1)
                    nc.scalar.activation(LS[:, b, :, :], LS[:, b, :, :], ACT.Exp).then_inc(s_lx, 1)
                for b in range(NB):
                    move(("LT", b), LPT[0:SK, b, :], lambda k: PS[0:SK, k, :])
                for b in range(NB):
                    move(("LC", b), hT[:, b % HS, b // HS, :], lambda k: PS[:, k, :])
                for b in range(NB):
                    k = made(("LO", b))
                    read(("LO", b), nc.scalar.activation(XN[:, TPB * b:TPB * b + TPB, :],
                                                         PS[:, k, :].rearrange("p (i d) -> p i d", i=TPB), ACT.Tanh))

            def mha_layer(L):
                for b in range(NB):
                    front(L, b)
                for j in range(TPB):
                    act.wait_ge(s_s5, j + 1)
                    sc = m5[:, j % 2, 0, :]
                    nc.scalar.activation(sc, sc, ACT.Exp, scale=ATT_SCALE).then_inc(s_e5, 1)
                for b in range(NB):
                    move(("AT", b), hT[:, b % HS, b // HS, :], lambda k: PS[:, k, :])
                move(("T2", L, 0), XT[:, 0, :], lambda k: PS[:, k, :])
                turn_combine(L, 0)

            def pieces(u):
                if u is None:
                    return []
                L, b = u
                if LAYERS[L] == ATTN:
                    return [lambda: front(L, b)] + [lambda: None] * 5 + [lambda: place_max(L, b)]
                first = (lambda: move(("T2", L, b), XT[:, b, :], lambda k: PS[:, k, :])) if LAYERS[L] == MHA else (lambda: front(L, b))
                return [first, lambda: route(L, b), lambda: turn_combine(L, b)]

            for f in pieces((0, 0)):
                f()
            for n, (L, b) in enumerate(units):
                if b == 0 and L:
                    if LAYERS[L - 1] == ATTN:
                        values_summed(act, PAIRS * n_attn[L - 1, NB - 1] + PAIRS - 1)
                    elif LAYERS[L - 1] in (MOE, MHA):
                        act.wait_ge(*slots.is_made(("Y", L - 1, NB - 1, EXPERTS[L - 1] - 1)))
                if LAYERS[L] == LOCAL:
                    if b == 0:
                        local_layer(L)
                    continue
                if LAYERS[L] == MHA and b == 0:
                    mha_layer(L)
                todo = pieces(following((L, b)))
                at = place(len(todo), steps_of(L))
                prev = units[n - 1] if n and LAYERS[units[n - 1][0]] == ATTN else None

                def hook(step):
                    for f, x in zip(todo, at):
                        if x == step:
                            f()
                    if step == 0 and prev:
                        invert_sums(*prev)

                {ATTN: attn_unit, MOE: moe_unit, MHA: moe_unit, GLU: glu_unit}[LAYERS[L]](L, b, hook)

        @block.gpsimd
        def _(pool):
            pool.memset(mhalf[:, :], -0.5).then_inc(s_pool0, 1)
            pool.memset(V2[:, :, :, :], 0.0).then_inc(s_pool0, 1)
            pool.wait_ge(s_pool0, 2)
            for half in range(2):
                for sub in range(2):
                    h0, c0 = 8 * half + 4 * sub, 16 - 16 * half + 8 * sub
                    for b in range(NB):
                        ins = pool.memset(V2[:, b, h0:h0 + 4, c0:c0 + DK], 1.0)
            ins.then_inc(s_pool0, 1)
            pool.memset(T1[96:128, :, :, :], 1.0).then_inc(s_pool0, 1)
            pool.wait_ge(s_pool0, 4)
            pool.wait_ge(s_c, 16 * 8)
            for n, (which, L, b) in enumerate(norms):
                if (which, L, b) == ("ln1", 5, 0):
                    pool.wait_ge(s_pin, 1)
                    for j in range(TPB):
                        if j:
                            pool.wait_ge(s_s5, j)
                        prod = PROD.rearrange("p (t s c) -> p t s c", t=NB, s=NB)
                        for t in range(NB):
                            ins = pool.tensor_tensor(prod[:, t, :, :],
                                                     QKV[:, t, j, 0:P].unsqueeze(1).to_broadcast([P, NB, P]),
                                                     QKV[:, :, j, P:2 * P], ALU.mult)
                        ins.then_inc(s_p5, 1)
                pool.wait_ge(s_stat, n + 1)
                pool.tensor_scalar(vare[:, n % 2, :], mv[:, n % 2, :, 1], EPS, None, ALU.add).then_inc(s_vare, 1)
                pool.wait_ge(s_vare, n + 1)
                pool.tensor_tensor(rstd[:, n % 2, :], vare[:, n % 2, :], mhalf[:, :], ALU.pow).then_inc(s_rstd, 1)
                if which == "in" and LAYERS[L] == ATTN:
                    pool.wait_ge(s_xn, n_in[L, b])
                    x = X[:, TPB * b:TPB * b + TPB, :]
                    bo = row(f"bo{ATTN_NO[L]}").unsqueeze(1).to_broadcast([P, TPB, P])
                    pool.tensor_tensor(x, x, bo, ALU.add).then_inc(s_bo, 1)

        @block.sync
        def _(sp):
            xd = A["x"].rearrange("(t p) d -> p t d", p=P)
            sp.dma_start(consts[:, :], A["consts"]).then_inc(s_c, 16)
            sp.dma_start(ctxT[:, :], A["ctxT"]).then_inc(s_c, 16)
            sp.dma_start(wattn[:, 0, :, :], A["wattn"][:, 0]).then_inc(s_w["a"], 16)
            sp.dma_start(X[:, 0:TPB, :], xd[:, 0:TPB, :]).then_inc(s_x[0], 16)
            sp.dma_start(cols[:, :], A["cols"]).then_inc(s_c, 16)
            sp.dma_start(rows[:, :], A["rows"].partition_broadcast(P)).then_inc(s_c, 16)
            sp.dma_start(drow[:, 0, :], A["delta"]).then_inc(s_c, 16)
            sp.dma_start(ctxN[:, :, :], A["ctxN"]).then_inc(s_c, 16)
            sp.dma_start(leni[:, :], A["lens"].partition_broadcast(P)).then_inc(s_c, 16)
            sp.dma_start(XN[0:64, 0:GLU_PAIRS, :], A["pick_pair"]).then_inc(s_c, 16)
            for b in range(1, NB):
                sp.dma_start(X[:, TPB * b:TPB * b + TPB, :], xd[:, TPB * b:TPB * b + TPB, :]).then_inc(s_x[b], 16)
            sp.dma_start(router[:, :], A["router"]).then_inc(s_w["a"], 16)

            def place_k(a):
                sp.wait_ge(s_kb, a + 1)
                for q, (K, part) in enumerate(((KS1, 0), (KS1, 0), (KS1, 0), (KS2, 1), (KS2, 1), (KS2, 2))):
                    for g in range(NG):
                        sp.dma_start(K[32 * (q % 3):32 * (q % 3) + 32, HPG * g:HPG * g + HPG, :],
                                     KB[32 * g:32 * g + 32, part, :, :]).then_inc(s_ks[a], 16)

            def place_q(u):
                sp.wait_ge(s_q3, u + 1)
                for q, (T, part, done) in enumerate(((T1, 0, s_t1), (T1, 1, s_t1), (T1, 2, s_t1),
                                                     (T2, 0, s_t2), (T2, 1, s_t2), (T2, 0, s_t2))):
                    for g in range(NG):
                        sp.dma_start(T[32 * (q % 3):32 * (q % 3) + 32, u % 2, g, :],
                                     qparts[32 * g:32 * g + 32, u % 2, part, :]).then_inc(done[u], 16)

            sp.wait_ge(s_ones, 1)
            sp.wait_ge(s_delta, 1)
            for j in range(3):
                sp.dma_start(KS1[96 + j:97 + j, :, :], dparts[:, j, :].unsqueeze(1).to_broadcast([1, NH, CK])).then_inc(s_drow, 16)
            place_k(0)
            place_q(0)
            for a in (1, 2):
                sp.dma_start(wattn[:, a, :, :], A["wattn"][:, a]).then_inc(s_w["a"], 16)
            for L in (1, 3, 5):
                sp.dma_start(w1[L][:, :, :] if L > 1 else w1[L], A[f"w1_{L}"]).then_inc(s_w[f"m{L}"], 16)
                sp.dma_start(w2[L][:, :, :, :] if L > 1 else w2[L], A[f"w2_{L}"]).then_inc(s_w[f"m{L}"], 16)
                sp.dma_start(b2[L][:, :], A[f"b2_{L}"]).then_inc(s_w[f"m{L}"], 16)
            sp.dma_start(wloc[:, :, :], A["wloc"]).then_inc(s_w["loc"], 16)
            sp.dma_start(win5[:, :], A["win5"]).then_inc(s_w["loc"], 16)
            for u in range(1, 4):
                place_q(u)
            place_k(1)
            for u in range(4, 8):
                place_q(u)
            place_k(2)
            sp.wait_ge(s_c5, TPB)
            sp.dma_start(w1[7], A["w1_7"]).then_inc(s_w["m7"], 16)
            sp.dma_start(w3_7, A["w3_7"]).then_inc(s_w["m7"], 16)
            sp.dma_start(w2[7], A["w2_7"]).then_inc(s_w["m7"], 16)
            for u in range(8, 12):
                place_q(u)
            od = out.rearrange("(t p) d -> p t d", p=P)
            for b in range(NB):
                sp.wait_ge(*slots.is_read(("Y", 7, b)))
                sp.dma_start(od[:, TPB * b:TPB * b + TPB, :], X[:, TPB * b:TPB * b + TPB, :]).then_inc(s_out, 16)
            sp.wait_ge(s_out, 16 * NB)


def constants():
    r = np.arange(P)
    c = np.zeros((P, CONSTS_N), np.float32)

    def put(name, v):
        a, b = CONSTS[name]
        c[:, a:b] = v

    put("ident", np.eye(P))
    put("head_mask", (r[:, None] % 32) // DK == np.arange(HPG)[None])
    put("low_rows", (r % 32 < 16)[:, None])
    put("high_rows", (r % 32 >= 16)[:, None])
    put("pick_head", r[:, None] % NH == np.arange(NH)[None])
    put("iota16", np.arange(16)[None])
    put("iota77", np.arange(SK)[None])
    put("iota_col", r[:, None])
    pick = np.zeros((64, GLU_PAIRS, P), np.float32)
    for p in range(GLU_PAIRS - 1):
        for half in range(2):
            for part in range(3):
                pick[16 * part + 2 * p + half, p, 64 * half:64 * half + 64] = 1
    pick[48, GLU_PAIRS - 1, :] = 1
    return c, pick


def lay_out(i):
    f = {k: np.asarray(v) for k, v in i.items()}
    A = {}
    A["consts"], A["pick_pair"] = constants()
    A["x"] = f["x"].reshape(NB * SQ, P)
    A["ctxT"] = f["ctx_1024"].reshape(CK, P).T
    A["ctxN"] = f["ctx_1024"].transpose(1, 0, 2)
    A["delta"] = f["fside_BxS2_0"].reshape(1, CK)
    A["lens"] = f["_lenS2"]
    order = np.zeros(P, np.int64)
    for h in range(NH):
        order[num_row(h):num_row(h) + DK] = DK * h + np.arange(DK)
    sets = []
    for L in (0, 1, 3):
        w = [f[f"L{L}_xcond_W{n}"].T for n in "qkvo"]
        w[3] = w[3][order]
        sets.append(np.stack(w, 1))
    A["wattn"] = np.stack(sets, 1)
    A["router"] = np.concatenate([f["L0_ffn_router_w"], f["L1_ffn_Wr"], f["L2_ffn_router_w"].T, f["L3_ffn_gate_w"].T], 1)
    for L, n, k1, k2, kb in ((1, 0, "w1", "w2", "b2"), (3, 1, "W1", "W2", "b2")):
        A[f"w1_{L}"] = f[f"L{n}_ffn_{k1}"].transpose(1, 0, 2)
        w = f[f"L{n}_ffn_{k2}"]
        A[f"w2_{L}"] = w.reshape(w.shape[0], 2, P, P).transpose(2, 0, 1, 3)
        A[f"b2_{L}"] = f[f"L{n}_ffn_{kb}"]
    A["w1_5"] = f["L2_ffn_w1"].transpose(2, 0, 1)
    A["w2_5"] = f["L2_ffn_w2"].transpose(2, 0, 1)[:, :, None]
    A["b2_5"] = f["L2_ffn_b2"]
    A["wloc"] = np.stack([f["L2_xcond_W_a"].T, f["L2_xcond_W_c"][:, :P].T, f["L2_xcond_W_c"][:, P:].T], 1)
    A["win5"] = np.concatenate([f["L2_ffn_in_proj_w"].T, f["L2_ffn_out_w"].T], 1)
    pad = np.zeros((P, 64), np.float32)
    for n in (1, 3):
        w = np.concatenate([f[f"L3_ffn_w{n}"].reshape(16 * 64, P).T, f[f"L3_ffn_ws{n}"].T, pad], 1)
        A[f"w{n}_7"] = w.reshape(P, GLU_PAIRS, P)
    w = np.concatenate([f["L3_ffn_w2"].transpose(0, 2, 1).reshape(16 * 64, P), f["L3_ffn_ws2"].T, pad.T], 0)
    A["w2_7"] = w.reshape(GLU_PAIRS, P, P).transpose(1, 0, 2)
    cols = [f[f"L{L}_xcond_b{n}"][:, None] for n in "qk" for L in (0, 1, 3)]
    cols += [f["L0_ffn_b1"].reshape(32, P).T, f["L1_ffn_b1"].reshape(16, P).T, f["L2_ffn_b1"].T]
    A["cols"] = np.concatenate(cols, 1)
    A["rows"] = np.concatenate([f[f"L{L}_xcond_b{n}"] for n in "vo" for L in (0, 1, 3)] + [
        f["L0_ffn_router_b"], f["L1_ffn_br"], f["L2_ffn_router_b"], f["L3_ffn_gate_bias"], f["L2_ffn_in_proj_b"],
        f["L2_ffn_out_b"], f["L2_ffn_ln1_g"], f["L2_ffn_ln1_b"], f["L2_ffn_ln2_g"], f["L2_ffn_ln2_b"],
        f["condB_tau"], f["condB_pt"]])
    return {k: np.ascontiguousarray(v) for k, v in A.items()}


def kernel(**inputs):
    import numpy as _np
    import concourse.bacc as _bacc
    from concourse import mybir as _mybir
    from concourse.bass_utils import run_bass_kernel_spmd as _run

    nc = _bacc.Bacc("TRN2", target_bir_lowering=False, num_devices=1)
    arrays = {f"in_{k}": v for k, v in lay_out(inputs).items()}
    args = {k[3:]: nc.dram_tensor(k, v.shape, _mybir.dt.from_np(v.dtype), kind="ExternalInput").ap()
            for k, v in arrays.items()}
    out = nc.dram_tensor("out_0", (NB * SQ, P), F32, kind="ExternalOutput").ap()
    build(nc, args, out)
    r = _run(nc, [arrays], core_ids=[0])
    return _np.asarray(r.results[0]["out_0"]).reshape(NB, SQ, P)
```

```python
from contextlib import ExitStack

import numpy as np

import concourse.bass as bass
from concourse import mybir
from concourse.alu_op_type import AluOpType as ALU

F32 = mybir.dt.float32
BF16 = mybir.dt.bfloat16
U32 = mybir.dt.uint32
I32 = mybir.dt.int32
ACT = mybir.ActivationFunctionType
AX = mybir.AxisListType

P = 128
NB = 4
SQ = 512
TPB = SQ // P
NT = NB * TPB
SK = 77
CK = NB * SK
NH = 16
DK = P // NH
NG = 4
HPG = NH // NG
PAIRS = NH // 2
EPS = 1e-5
ATT_SCALE = float(np.float32(1.0) / np.sqrt(np.float32(DK)))
BIG = 1e30
WINDOW, DEV_POW, MASKED = 16.0, 128.0, 1e9

ATTN, MOE, LOCAL, MHA, GLU = "attn", "moe", "local", "mha", "glu"
LAYERS = [ATTN, MOE, ATTN, MOE, LOCAL, MHA, ATTN, GLU]
NL = len(LAYERS)
ATTN_NO = {0: 0, 2: 1, 6: 2}
EXPERTS = {1: 16, 3: 8, 5: 8, 7: 16}
HIDDEN_CHUNKS = {1: 2, 3: 2, 5: 1}
GLU_PAIRS = 9

ROWS = {}
ROWS_N = 0
for _name, _n in (("bv0", 128), ("bv1", 128), ("bv2", 128), ("bo0", 128), ("bo1", 128), ("bo2", 128),
                  ("rb1", 16), ("rb3", 8), ("rb5", 8), ("rb7", 16), ("in_b", 384), ("out_b", 128),
                  ("ln1_g", 128), ("ln1_b", 128), ("ln2_g", 128), ("ln2_b", 128), ("tau", 4), ("pt", 4)):
    ROWS[_name] = (ROWS_N, ROWS_N + _n)
    ROWS_N += _n

CONSTS = {}
CONSTS_N = 0
for _name, _n in (("ident", 128), ("head_mask", HPG), ("low_rows", 1), ("high_rows", 1), ("pick_head", NH),
                  ("iota16", 16), ("iota77", SK), ("iota_col", 1)):
    CONSTS[_name] = (CONSTS_N, CONSTS_N + _n)
    CONSTS_N += _n

COLS = {}
COLS_N = 0
for _name, _n in (("bq0", 1), ("bq1", 1), ("bq2", 1), ("bk0", 1), ("bk1", 1), ("bk2", 1),
                  ("b1_1", 32), ("b1_3", 16), ("b1_5", 8)):
    COLS[_name] = (COLS_N, COLS_N + _n)
    COLS_N += _n

WIDE = ("wide0", "wide1")
SMALL = ("small0", "small1")
ACC = ("acc0", "acc1")
BANK = {"wide0": 0, "wide1": 2, "small0": 4, "small1": 5, "acc0": 6, "acc1": 7}


def num_row(h):
    return 32 * (h % 4) + 8 * ((h // 4) % 2) + 16 * (h // 8)


class Slots:

    def __init__(self, made, read):
        self.made, self.read = made, read
        self.uses = dict.fromkeys(BANK, 0)
        self.turn = {}
        self.where = {}

    def take(self, job, kind):
        turn = self.turn.get(kind, 0)
        self.turn[kind] = turn + 1
        slot = kind[turn % len(kind)]
        self.uses[slot] += 1
        self.where[job] = (slot, self.uses[slot])
        return slot

    def before(self, job):
        slot, n = self.where[job]
        return (self.read[slot], n - 1) if n > 1 else None

    def is_made(self, job):
        slot, n = self.where[job]
        return self.made[slot], n

    def is_read(self, job):
        slot, n = self.where[job]
        return self.read[slot], n

    def bank(self, job):
        return BANK[self.where[job][0]]


def build(nc, A, out):
    with ExitStack() as ctx:
        def sb(name, shape, dt=F32):
            return ctx.enter_context(nc.sbuf_tensor("s_" + name, shape, dt))

        def sem(name):
            return ctx.enter_context(nc.semaphore(name))

        PS = ctx.enter_context(nc.psum_tensor("psum_all", [P, 8, 512], F32))

        X = sb("x_resid", [P, NT, P])
        XN = sb("x_normed", [P, NT, P])
        XT = sb("x_turned", [P, NB, SQ])
        consts = sb("consts", [P, CONSTS_N])
        rows = sb("rows", [P, ROWS_N])
        cols = sb("cols", [P, COLS_N])
        ctxT = sb("ctxT", [P, CK])
        ctxN = sb("ctxN", [SK, NB, P])
        wattn = sb("wattn", [P, 3, 4, P])
        arena = sb("arena", [P, 8192])
        w1 = {1: arena[:, 0:4096].rearrange("p (e h) -> p e h", e=16)}
        w2 = {1: arena[:, 4096:8192].rearrange("p (e c d) -> p e c d", e=16, c=2)}
        w1[3] = sb("w1_3", [P, 8, 256])
        w2[3] = sb("w2_3", [P, 8, 2, P])
        w1[5] = sb("w1_5", [P, 8, P])
        w2[5] = sb("w2_5", [P, 8, 1, P])
        w1[7], w3_7, w2[7] = (arena[:, 1152 * j:1152 * j + 1152].rearrange("p (e c) -> p e c", e=GLU_PAIRS)
                              for j in range(3))
        b2 = {1: sb("b2_1", [16, P]), 3: sb("b2_3", [8, P]), 5: sb("b2_5", [8, P])}
        router = sb("router", [P, 16 + 8 + 8 + 16])
        rw = {1: router[:, 0:16], 3: router[:, 16:24], 5: router[:, 24:32], 7: router[:, 32:48]}
        wloc = sb("wloc", [P, 3, P])
        win5 = sb("win5", [P, 4 * P])
        QKV = arena[:, 0:6144].rearrange("p (t s c) -> p t s c", t=NB, s=TPB)
        H5 = sb("h5", [P, NT, P])
        PV5 = w1[3][:, :, :].rearrange("p e c -> p (e c)")
        LCTX = w2[3][:, :, :, :].rearrange("p e c d -> p (e c d)").rearrange("p (t j d) -> p t j d", t=NB, j=TPB)

        stats = sb("stats", [P, TPB, 6])
        mv = sb("mv", [P, 2, TPB, 2])
        vare = sb("vare", [P, 2, TPB])
        rstd = sb("rstd", [P, 2, TPB])
        mhalf = sb("minus_half", [P, TPB])

        KS1 = sb("ks1", [P, NH, CK], BF16)
        KS2 = sb("ks2", [P, NH, CK], BF16)
        att = sb("att", [P, 6, SQ])
        spare = att[:, :, :].rearrange("p a b -> p (a b)")
        kf, kr = spare[:, 0:CK], spare[:, CK:2 * CK]
        kparts = spare[:, 2 * CK:2 * CK + 3 * CK // 2].bitcast(BF16).rearrange("p (j s) -> p j s", j=3)
        KB = spare[:, 1078:1078 + 3 * HPG * CK // 2].bitcast(BF16).rearrange("p (j h s) -> p j h s", j=3, h=HPG)
        keep = spare[:, 0:CK].rearrange("p (b s) -> p b s", b=NB)
        negm = spare[:, CK:2 * CK].rearrange("p (b s) -> p b s", b=NB)
        Eloc = spare[:, 2 * CK:3 * CK]
        Gc = spare[0:SK, 3 * CK:3 * CK + NB * P].rearrange("p (b d) -> p b d", b=NB)
        m5 = spare[:, 1536:2560].rearrange("p (a b c) -> p a b c", a=2, b=2)
        V2 = sb("v2", [SK, NB, NH, 32])
        tscale = sb("tscale", [P, NB])
        QS = 3
        qf = sb("qf", [P, SQ])
        qr = sb("qr", [P, SQ])
        qparts = sb("qparts", [P, 3, SQ], BF16)
        T1 = sb("t1", [P, QS, NG, SQ], BF16)
        T2 = sb("t2", [P, QS, NG, SQ], BF16)
        nmx = sb("nmx", [P, 2, TPB, NH])
        nmxh = sb("nmxh", [P, TPB, NH], BF16)
        nmx2 = sb("nmx2", [P, 2, TPB, 2 * NH])
        ES = 3
        HS = 3
        hT = sb("hT", [P, HS, 2, SQ])
        Eexp = hT[0:SK, :, :, :]
        gl = hT
        PROD = (arena[:, 6144:8192], hT[:, 0:2, :, :].rearrange("p a b c -> p (a b c)"))
        drow = hT[0:1, 0, :, :].rearrange("p a b -> p (a b)")[:, 0:3 * CK].rearrange("p (j s) -> p j s", j=3)
        dparts = hT[0:1, 1, 0, 0:3 * CK // 2].bitcast(BF16).rearrange("p (j s) -> p j s", j=3)
        LPT = T1[:, 0:2, :, :].rearrange("p a b c -> p (a b c)").bitcast(F32).rearrange("p (b c) -> p b c", b=NB)
        LS = (T2[:, 0:2, :, :].rearrange("p a b c -> p (a b c)").bitcast(F32)[:, 0:NB * TPB * SK]
              .rearrange("p (b i s) -> p b i s", b=NB, i=TPB))
        C = sb("combine", [P, NT, 16])
        cT = sb("cT", [64, 2, SQ])
        cT7 = cT[:, 0, :].bitcast(BF16).rearrange("p (a b) -> p a b", a=2)
        lg = sb("lg", [P, TPB, 16])
        v8 = sb("v8", [P, TPB, 8])
        i8 = sb("i8", [P, TPB, 8], U32)
        if8 = sb("if8", [P, TPB, 8])
        oh = sb("oh", [P, TPB, 4, 16])
        r16 = sb("r16", [P, 4, TPB, 16])
        g8 = sb("g8", [P, TPB, 8])
        r1 = sb("r1", [P, 4, TPB])
        lrow = sb("lrow", [P, 6, NB])
        leni = sb("leni", [P, NB], I32)
        gau = sb("gau", [SK, 3, NB])
        c7h = sb("c7h", [P, 2, TPB, 16], BF16)
        c7 = sb("c7", [P, 2, TPB, 64])
        pick7 = sb("pick7", [64, GLU_PAIRS * P], BF16)

        ident = consts[:, 0:128]

        def const(name, n=P):
            a, b = CONSTS[name]
            return consts[0:n, a:b]

        def row(name, n=P):
            a, b = ROWS[name]
            return rows[0:n, a:b]

        def col(name, j=0):
            a = COLS[name][0] + j
            return cols[:, a:a + 1]

        slots = Slots({s: sem(f"made_{s}") for s in BANK}, {s: sem(f"read_{s}") for s in BANK})
        s_x = [sem(f"x_loaded{b}") for b in range(NB)]
        s_dl = sem("delta_loaded")
        s_kw = sem("context_and_key_weights_loaded")
        s_c = sem("consts_loaded")
        s_rows = sem("rows_loaded")
        s_pick = sem("picks_ready")
        s_ob = sem("out_bias_added")
        s_w = {k: sem(f"weights_loaded_{k}") for k in ("a", "m1", "m3", "m5", "m7", "loc")}
        s_out = sem("out_written")
        s_stat = sem("mean_var_ready")
        s_vare = sem("var_eps_ready")
        s_rstd = sem("rstd_ready")
        s_xn = sem("normed_ready")
        s_bo = sem("bo_added")
        s_pool0 = sem("pool_consts_ready")
        s_ones = sem("dve_consts_ready")
        s_delta = sem("delta_parts_ready")
        s_drow = sem("delta_rows_placed")
        s_kb = sem("k_blocks_ready")
        s_ks1 = [sem(f"ks1_placed{a}") for a in range(3)]
        s_ks = [sem(f"ks2_placed{a}") for a in range(3)]
        s_v2 = sem("v2_ready")
        s_q3 = sem("q_parts_ready")
        s_t1 = [sem(f"t1_placed{u}") for u in range(12)]
        s_t2 = [sem(f"t2_placed{u}") for u in range(12)]
        s_nmx = sem("max_ready")
        s_prod = sem("att_out_ready")
        s_lr = sem("logits_ready")
        s_le = sem("logit_exps_ready")
        s_cw = sem("combine_ready")
        s_sil = sem("silu_ready")
        s_glu = sem("glu_hidden_ready")
        s_lg = sem("gauss_arg_ready")
        s_ge = sem("gauss_ready")
        s_gc = sem("gauss_context_ready")
        s_ls = sem("local_scores_ready")
        s_lx = sem("local_exps_ready")
        s_lp = sem("local_probs_ready")
        s_p5 = sem("qk_products_ready")
        s_s5 = sem("mha_shifted_ready")
        s_e5 = sem("mha_exps_ready")
        s_c5 = sem("mha_ctx_ready")
        s_h5 = sem("h_ready")
        s_pin = sem("qkv_ready")
        s_actc = sem("act_chain")
        s_dve = [sem(f"dve_chain{i}") for i in range(NL + 1)]
        s_pv = sem("values_summed")
        s_yglu = sem("glu_summed")

        units = [(L, b) for L in range(NL) for b in range(NB)]
        attn_units = [(L, b) for L, b in units if LAYERS[L] == ATTN]
        n_attn = {u: i for i, u in enumerate(attn_units)}
        moe_units = [(L, b) for L, b in units if LAYERS[L] in (MOE, MHA, GLU)]
        n_moe = {u: i for i, u in enumerate(moe_units)}
        exp_units = [u for u in moe_units if LAYERS[u[0]] == MOE]
        n_exp = {u: i for i, u in enumerate(exp_units)}
        def steps_of(L):
            return PAIRS if LAYERS[L] == ATTN else GLU_PAIRS if LAYERS[L] == GLU else EXPERTS[L]

        def following(u):
            L, b = u
            if b < NB - 1:
                return (L, b + 1)
            return (L + 1, 0) if L + 1 < NL and LAYERS[L + 1] not in (LOCAL, MHA) else None

        def ahead(u, n):
            L, b = u
            v = (L, b + n) if b + n < NB else (L + 1, b + n - NB)
            return v if v[0] < NL and LAYERS[v[0]] == ATTN else None

        PLACES = {
            "pe": {"stats": 0, "norm": 0, "front": 1, "turn": 0, "Q": 2, "M0": 0, "M1": 1, "M2": 2, "M3": 3, "MT": 5, "R": 3, "CT": 6},
            "dve": {"stats": 6, "norm": 7, "front": 0, "turn": 0, "Q": 2, "M0": 0, "M1": 1, "M2": 2, "M3": 3, "MT": 3, "R": 3, "CT": 6},
            "act": {"stats": 0, "norm": 0, "front": 2, "turn": 1, "Q": 3, "M0": 0, "M1": 0, "M2": 0, "M3": 0, "MT": 6, "R": 3, "CT": 7},
        }

        DIVIDE_AT, OUT_AT, ADD_AT = 3, 6, 7

        def plan(u, engine):
            L, b = u
            todo = []
            v = following(u)
            if v:
                todo += [(stage, *v) for stage in (("M0", "M1", "M2", "M3", "MT") if LAYERS[v[0]] == ATTN
                                                   else ("front", "R", "CT"))]
            v = ahead(u, 2)
            if v:
                todo += [(stage, *v) for stage in ("front", "Q")]
            v = ahead(u, 3)
            if v:
                todo += [("stats", *v), ("norm", *v)]
            if L + 1 < NL and LAYERS[L + 1] == LOCAL and b:
                todo += [("front", L + 1, b - 1)]
            todo = [(PLACES[engine]["turn" if x[0] == "front" and LAYERS[x[1]] == ATTN else x[0]], *x) for x in todo]
            todo.sort(key=lambda x: x[0])
            return [(x[0] * steps_of(u[0]) // 8, *x[1:]) for x in todo]

        BEFORE = ([(stage, 0, 0) for stage in ("keys", "stats", "norm", "front", "Q", "values")]
                  + [(stage, 0, 1) for stage in ("stats", "norm", "front")]
                  + [(stage, 0, 0) for stage in ("M0", "M1", "M2", "M3", "MT")]
                  + [("Q", 0, 1), ("stats", 0, 2), ("norm", 0, 2)])

        norms = [("in", L, b) for stage, L, b in BEFORE if stage == "stats"]
        for L, b in units:
            if LAYERS[L] == LOCAL:
                if b == 0:
                    norms += [("in", L, NB - 1)]
                continue
            if LAYERS[L] == MHA and b == 0:
                norms += [("in", L, c) for c in range(NB)] + [("ln1", L, c) for c in range(NB)]
            norms += [("in", *v) for _, stage, *v in plan((L, b), "dve")
                      if stage == "stats" or stage == "front" and LAYERS[v[0]] != MHA and LAYERS[v[0]] != ATTN]
            if LAYERS[L] == MHA:
                norms.append(("ln2", L, b))
        n_in = {x[1:]: i + 1 for i, x in enumerate(x for x in norms if x[0] == "in")}

        def values_summed(eng, n):
            u, p = divmod(n, PAIRS)
            g = p // 2
            if g % 2:
                eng.wait_ge(*slots.is_made(("PV", *attn_units[u], g // 2)))
            else:
                eng.wait_ge(s_pv, 2 * u + g // 2 + 1)

        def glu_summed(eng, n):
            b, p = divmod(n, GLU_PAIRS)
            if p < GLU_PAIRS - 1:
                eng.wait_ge(s_yglu, (GLU_PAIRS - 1) * b + p + 1)
            else:
                eng.wait_ge(*slots.is_made(("Y", 7, b)))

        block = ctx.enter_context(nc.Block())

        @block.tensor
        def _(pe):
            def start(job, kind):
                slots.take(job, kind)
                w = slots.before(job)
                if w:
                    pe.wait_ge(*w)
                return slots.bank(job)

            def finish(job, ins):
                ins.then_inc(slots.is_made(job)[0], 1)

            def have(job):
                pe.wait_ge(*slots.is_read(job))

            def turn(job, src, ready, value):
                pe.wait_ge(ready, value)
                k = start(job, SMALL)
                for i in range(TPB):
                    mm = pe.transpose(PS[:, k, 128 * i:128 * i + 128], src[:, i, :], ident)
                finish(job, mm)

            def front(L, b):
                turn(("T", L, b), XN[:, TPB * b:TPB * b + TPB, :], s_xn, n_in[L, b])

            def keys(a):
                if a:
                    pe.wait_ge(s_w["a"], 16 * 3)
                else:
                    pe.wait_ge(s_kw, 16 * 2)
                k = start(("K", a), SMALL)
                finish(("K", a), pe.matmul(PS[:, k, 0:CK], wattn[:, a, 1, :], ctxT[:, :], start=True, stop=True))

            def values(a):
                k = start(("V", a), SMALL)
                for b in range(NB):
                    mm = pe.matmul(PS[0:SK, k, 128 * b:128 * b + 128], ctxT[:, SK * b:SK * b + SK],
                                   wattn[:, a, 2, :], start=True, stop=True)
                finish(("V", a), mm)

            def k_prep(a):
                keys(a)
                values(a)

            def project_q(L, b):
                have(("T", L, b))
                k = start(("Q", L, b), SMALL)
                finish(("Q", L, b), pe.matmul(PS[:, k, :], wattn[:, ATTN_NO[L], 0, :], XT[:, b, :],
                                              start=True, stop=True))

            def max_scores(L, b, i):
                u = n_attn[L, b]
                if i == 0:
                    pe.wait_ge(s_t1[u], 16 * 12)
                    pe.wait_ge(s_ks1[ATTN_NO[L]], 16 * 12)
                    pe.wait_ge(s_drow, 16 * 3)
                    pe.wait_ge(s_pool0, 4)
                for g in range(NG):
                    k = start(("M", L, b, i, g), SMALL)
                    o = PS[:, k, 0:HPG * SK].rearrange("p (h s) -> p h s", h=HPG)
                    finish(("M", L, b, i, g),
                           pe.matmul(o, T1[:, u % QS, g, 128 * i:128 * i + 128],
                                     KS1[:, HPG * g:HPG * g + HPG, SK * b:SK * b + SK], start=True, stop=True))

            def turn_max(L, b):
                u = n_attn[L, b]
                pe.wait_ge(s_nmx, u + 1)
                k = start(("MT", L, b), SMALL)
                for i in range(TPB):
                    mm = pe.transpose(PS[0:2 * NH, k, 128 * i:128 * i + 128], nmx2[:, u % 2, i, :], ident)
                finish(("MT", L, b), mm)

            def attn_unit(L, b, hook):
                u = n_attn[L, b]

                def scores(p):
                    k = start(("S", L, b, p), WIDE)
                    for y in range(2):
                        h = 2 * p + y
                        keys = slice(SK * b, SK * b + SK)
                        pe.matmul(PS[0:SK, k + y, :], KS1[:, h, keys], T1[:, u % QS, h // HPG, :],
                                  start=True, stop=False)
                        mm = pe.matmul(PS[0:SK, k + y, :], KS2[:, h, keys], T2[:, u % QS, h // HPG, :],
                                       start=False, stop=True)
                    finish(("S", L, b, p), mm)

                have(("MT", L, b))
                pe.wait_ge(s_t2[u], 16 * 12)
                pe.wait_ge(s_ks[ATTN_NO[L]], 16 * 12)
                pe.wait_ge(s_pick, 1)
                pe.wait_ge(s_v2, ATTN_NO[L] + 1)
                scores(0)
                scores(1)
                for p in range(PAIRS):
                    if p % 2:
                        g = p // 2
                        if g % 2 == 0:
                            k = start(("PV", L, b, g // 2), ACC)
                        have(("S", L, b, p - 1))
                        have(("S", L, b, p))
                        for j in range(HPG):
                            mm = pe.matmul(PS[32 * j:32 * j + 32, k, :], V2[:, b, HPG * g + j, :],
                                           Eexp[:, (PAIRS * u + p - 1 + j // 2) % ES, j % 2, :],
                                           start=(g % 2 == 0), stop=(g % 2 == 1))
                        if g % 2:
                            finish(("PV", L, b, g // 2), mm)
                        else:
                            mm.then_inc(s_pv, 1)
                    if p + 2 < PAIRS:
                        scores(p + 2)
                    hook(p)

            def attn_out(L, b):
                pe.wait_ge(s_prod, n_attn[L, b] + 1)
                k = start(("O", L, b), SMALL)
                for i in range(TPB):
                    mm = pe.matmul(PS[:, k, 128 * i:128 * i + 128], att[:, 5, 128 * i:128 * i + 128],
                                   wattn[:, ATTN_NO[L], 3, :], start=True, stop=True)
                finish(("O", L, b), mm)

            def route(L, b):
                have(("T2" if LAYERS[L] == MHA else "T", L, b))
                if (L, b) == (1, 0):
                    pe.wait_ge(s_w["a"], 16 * 3)
                k = start(("R", L, b), SMALL)
                for i in range(TPB):
                    mm = pe.matmul(PS[:, k, 16 * i:16 * i + EXPERTS[L]], XT[:, b, 128 * i:128 * i + 128], rw[L],
                                   start=True, stop=True)
                finish(("R", L, b), mm)

            def turn_combine(L, b):
                n = n_moe[L, b]
                pe.wait_ge(s_cw, n + 1)
                k = start(("CT", L, b), SMALL)
                for i in range(TPB):
                    if LAYERS[L] == GLU:
                        mm = pe.transpose(PS[0:64, k, 128 * i:128 * i + 128], c7[:, b % 2, i, :], ident)
                    else:
                        mm = pe.transpose(PS[0:EXPERTS[L], k, 128 * i:128 * i + 128],
                                          C[:, TPB * b + i, 0:EXPERTS[L]], ident)
                finish(("CT", L, b), mm)

            def moe_unit(L, b, hook):
                E, NC = EXPERTS[L], HIDDEN_CHUNKS[L]
                pe.wait_ge(s_w[f"m{L}"], 16 * 3)

                def hidden(e):
                    k = start(("H", L, b, e), WIDE)
                    for c in range(NC):
                        mm = pe.matmul(PS[:, k + c, :], w1[L][:, e, 128 * c:128 * c + 128], XT[:, b, :],
                                       start=True, stop=True)
                    finish(("H", L, b, e), mm)

                hidden(0)
                have(("CT", L, b))
                k = start(("B2", L, b), ACC)
                for i in range(TPB):
                    mm = pe.matmul(PS[:, k, 128 * i:128 * i + 128], cT[0:E, b % 2, 128 * i:128 * i + 128],
                                   b2[L][:, :], start=True, stop=True)
                finish(("B2", L, b), mm)
                for e in range(E):
                    if e + 1 < E:
                        hidden(e + 1)
                    k = start(("Y", L, b, e), ACC)
                    have(("H", L, b, e))
                    hs = (E * b + e) % HS
                    for i in range(TPB):
                        for c in range(NC):
                            mm = pe.matmul(PS[:, k, 128 * i:128 * i + 128],
                                           hT[:, hs, c, 128 * i:128 * i + 128],
                                           w2[L][:, e, c, :], start=(c == 0), stop=(c == NC - 1))
                    finish(("Y", L, b, e), mm)
                    hook(e)

            def glu_unit(L, b, hook):
                pe.wait_ge(s_w["m7"], 16 * 3)
                pe.wait_ge(s_pick, 2)

                def hidden(p):
                    k = start(("H", L, b, p), WIDE)
                    pe.matmul(PS[:, k, :], w1[7][:, p, :], XT[:, b, :], start=True, stop=True)
                    finish(("H", L, b, p),
                           pe.matmul(PS[:, k + 1, :], w3_7[:, p, :], XT[:, b, :], start=True, stop=True))
                    k = start(("CB", L, b, p), SMALL)
                    finish(("CB", L, b, p), pe.matmul(PS[:, k, :], pick7[:, 128 * p:128 * p + 128],
                                                      cT7[:, b % 2, :], start=True, stop=True))

                have(("CT", L, b))
                hidden(0)
                for p in range(GLU_PAIRS):
                    if p + 1 < GLU_PAIRS:
                        hidden(p + 1)
                    if p == 0:
                        k = start(("Y", L, b), ACC)
                    have(("CB", L, b, p))
                    for i in range(TPB):
                        mm = pe.matmul(PS[:, k, 128 * i:128 * i + 128], gl[:, (GLU_PAIRS * b + p) % 3, 1, 128 * i:128 * i + 128],
                                       w2[7][:, p, :], start=(p == 0 and i == 0), stop=(p == GLU_PAIRS - 1),
                                       skip_group_check=True)
                    if p == GLU_PAIRS - 1:
                        finish(("Y", L, b), mm)
                    else:
                        mm.then_inc(s_yglu, 1)
                    hook(p)

            def local_layer(L):
                pe.wait_ge(s_w["loc"], 16)
                k = start(("E4",), SMALL)
                finish(("E4",), pe.matmul(PS[:, k, 0:CK], wloc[:, 0, :], ctxT[:, :], start=True, stop=True))
                for b in range(NB):
                    if b == NB - 1:
                        front(L, b)
                    have(("T", L, b))
                    have(("E4",))
                    k = start(("LS", b), SMALL)
                    for i in range(TPB):
                        mm = pe.matmul(PS[:, k, SK * i:SK * i + SK], XT[:, b, 128 * i:128 * i + 128],
                                       Eloc[:, SK * b:SK * b + SK], start=True, stop=True)
                    finish(("LS", b), mm)
                for b in range(NB):
                    pe.wait_ge(s_lp, b + 1)
                    k = start(("LT", b), SMALL)
                    for i in range(TPB):
                        mm = pe.transpose(PS[0:SK, k, 128 * i:128 * i + 128], LS[:, b, i, :], ident)
                    finish(("LT", b), mm)
                pe.wait_ge(s_gc, 1)
                for b in range(NB):
                    have(("LT", b))
                    k = start(("LC", b), SMALL)
                    finish(("LC", b), pe.matmul(PS[:, k, :], Gc[:, b, :], LPT[0:SK, b, :],
                                                start=True, stop=True))
                for b in range(NB):
                    have(("LC", b))
                    k = start(("LO", b), SMALL)
                    for i in range(TPB):
                        o = PS[:, k, 128 * i:128 * i + 128]
                        pe.matmul(o, hT[:, b % HS, b // HS, 128 * i:128 * i + 128], wloc[:, 1, :],
                                  start=True, stop=False)
                        mm = pe.matmul(o, XT[:, b, 128 * i:128 * i + 128], wloc[:, 2, :], start=False, stop=True)
                    finish(("LO", b), mm)

            def mha_layer(L):
                for b in range(NB):
                    front(L, b)
                pe.wait_ge(s_w["m5"], 16 * 3)
                for b in range(NB):
                    have(("T", L, b))
                for i in range(TPB):
                    for b in range(NB):
                        k = start(("QKV", b, i), SMALL)
                        finish(("QKV", b, i), pe.matmul(PS[:, k, 0:3 * P], XT[:, b, 128 * i:128 * i + 128],
                                                        win5[:, 0:3 * P], start=True, stop=True))
                pe.wait_ge(s_c5, TPB)
                for b in range(NB):
                    k = start(("AT", b), SMALL)
                    for i in range(TPB):
                        mm = pe.transpose(PS[:, k, 128 * i:128 * i + 128], LCTX[:, b, i, :], ident)
                    finish(("AT", b), mm)
                    have(("AT", b))
                    k = start(("AO", b), SMALL)
                    for i in range(TPB):
                        mm = pe.matmul(PS[:, k, 128 * i:128 * i + 128],
                                       hT[:, b % HS, b // HS, 128 * i:128 * i + 128],
                                       win5[:, 3 * P:4 * P], start=True, stop=True)
                    finish(("AO", b), mm)
                    if b == NB - 2:
                        mha_front(L, 0)
                route(L, 0)
                turn_combine(L, 0)

            def mha_front(L, b):
                turn(("T2", L, b), H5[:, TPB * b:TPB * b + TPB, :], s_h5, b + 1)

            def stage_of(stage, L, b):
                if stage in ("stats", "norm"):
                    pass
                elif stage == "keys":
                    pe.wait_ge(s_c, 16 * 2)
                    keys(0)
                elif stage == "values":
                    values(0)
                elif stage == "front":
                    (mha_front if LAYERS[L] == MHA else front)(L, b)
                elif stage == "Q":
                    project_q(L, b)
                elif stage == "MT":
                    turn_max(L, b)
                elif stage == "R":
                    route(L, b)
                elif stage == "CT":
                    turn_combine(L, b)
                else:
                    max_scores(L, b, int(stage[1]))

            for x in BEFORE:
                stage_of(*x)
            for n, (L, b) in enumerate(units):
                if LAYERS[L] == LOCAL:
                    if b == 0:
                        local_layer(L)
                    continue
                if LAYERS[L] == MHA and b == 0:
                    mha_layer(L)
                todo = plan((L, b), "pe")
                prev = units[n - 1] if n and LAYERS[units[n - 1][0]] == ATTN else None

                def hook(step):
                    for at, *x in todo:
                        if at == step:
                            stage_of(*x)
                    if step == OUT_AT and prev:
                        attn_out(*prev)
                    if step == 3 and (L, b) == (1, 2):
                        k_prep(1)
                    if step == 3 and (L, b) == (3, 1):
                        k_prep(2)

                {ATTN: attn_unit, MOE: moe_unit, MHA: moe_unit, GLU: glu_unit}[LAYERS[L]](L, b, hook)

        @block.vector
        def _(dve):
            count = [0] * (NL + 1)
            stage = [0]

            def link(ins):
                j = stage[0]
                count[j] += 1
                ins.then_inc(s_dve[j], 1)
                dve.wait_ge(s_dve[j], count[j])

            def made(job):
                dve.wait_ge(*slots.is_made(job))
                return slots.bank(job)

            def read(job, ins):
                ins.then_inc(slots.is_read(job)[0], 1)

            def settled(job):
                dve.wait_ge(*slots.is_read(job))

            def norm_stats(which, L, b, src):
                n = norms.index((which, L, b))
                if n >= 1:
                    dve.wait_ge(s_stat, n)
                for i in range(TPB):
                    ins = dve.bn_stats(stats[:, i, :], src[:, i, :])
                link(ins)
                for i in range(TPB):
                    ins = dve.bn_aggr(mv[:, n % 2, i, :], stats[:, i, :])
                ins.then_inc(s_stat, 1)

            def norm_apply(which, L, b, src, dst):
                n = norms.index((which, L, b))
                dve.wait_ge(s_stat, n + 1)
                dve.wait_ge(s_rstd, n + 1)
                for i in range(TPB):
                    ins = dve.tensor_scalar(dst[:, i, :], src[:, i, :], mv[:, n % 2, i, 0:1], rstd[:, n % 2, i:i + 1],
                                            ALU.subtract, ALU.mult)
                if which == "in":
                    ins.then_inc(s_xn, 1)
                else:
                    link(ins)

            def tiles(t, b):
                return t[:, TPB * b:TPB * b + TPB, :]

            def front_stats(L, b):
                if L == 0:
                    dve.wait_ge(s_x[b], 16)
                norm_stats("in", L, b, tiles(X, b))

            def front_apply(L, b):
                norm_apply("in", L, b, tiles(X, b), tiles(XN, b))

            def front(L, b):
                front_stats(L, b)
                front_apply(L, b)

            def delta_parts():
                link(dve.tensor_scalar(drow[:, 1, :], drow[:, 0, :], ATT_SCALE, None, ALU.mult))
                link(dve.tensor_copy(dparts[:, 0, :], drow[:, 1, :]))
                link(dve.tensor_tensor(drow[:, 2, :], drow[:, 1, :], dparts[:, 0, :], ALU.subtract))
                link(dve.tensor_copy(dparts[:, 1, :], drow[:, 2, :]))
                dve.tensor_tensor(dparts[:, 2, :], drow[:, 2, :], dparts[:, 1, :], ALU.subtract).then_inc(s_delta, 1)

            def keys(a):
                k = made(("K", a))
                read(("K", a), dve.tensor_scalar(kf[:, :], PS[:, k, 0:CK], col(f"bk{a}"), None, ALU.add))
                settled(("K", a))
                link(dve.tensor_copy(kparts[:, 0, :], kf[:, :]))
                link(dve.tensor_tensor(kr[:, :], kf[:, :], kparts[:, 0, :], ALU.subtract))
                link(dve.tensor_copy(kparts[:, 1, :], kr[:, :]))
                link(dve.tensor_tensor(kparts[:, 2, :], kr[:, :], kparts[:, 1, :], ALU.subtract))
                if a:
                    dve.wait_ge(s_ks1[a - 1], 16 * 12)
                    dve.wait_ge(s_ks[a - 1], 16 * 12)
                mask = const("head_mask")
                for j in range(3):
                    for h in range(HPG):
                        ins = dve.tensor_scalar(KB[:, j, h, :], kparts[:, j, :], mask[:, h:h + 1], None, ALU.mult)
                ins.then_inc(s_kb, 1)

            def values(a):
                k = made(("V", a))
                dve.wait_ge(s_pool0, 3)
                v = PS[0:SK, k, :].rearrange("s (b h d) -> s b h d", b=NB, h=NH)
                bias = row(f"bv{a}", SK).rearrange("s (h d) -> s h d", h=NH)
                for half in range(2):
                    for sub in range(2):
                        hs = slice(8 * half + 4 * sub, 8 * half + 4 * sub + 4)
                        c0 = 16 * half + 8 * sub
                        for b in range(NB):
                            ins = dve.tensor_tensor(V2[:, b, hs, c0:c0 + DK], v[:, b, hs, :], bias[:, hs, :], ALU.add)
                read(("V", a), ins)
                settled(("V", a))
                dve.engine_nop().then_inc(s_v2, 1)

            def k_prep(a):
                keys(a)
                values(a)

            def split_q(L, b):
                u = n_attn[L, b]
                k = made(("Q", L, b))
                if u:
                    dve.wait_ge(s_q3, u)
                else:
                    dve.wait_ge(s_rows, 16 * 4)
                    link(dve.tensor_scalar(tscale[:, :], row("tau"), ATT_SCALE, None, ALU.mult))
                read(("Q", L, b), dve.tensor_scalar(qf[:, :], PS[:, k, :], col(f"bq{ATTN_NO[L]}"), tscale[:, b:b + 1],
                                                    ALU.add, ALU.mult))
                settled(("Q", L, b))
                if u:
                    dve.wait_ge(s_t1[u - 1], 16 * 12)
                    dve.wait_ge(s_t2[u - 1], 16 * 12)
                q = qparts
                link(dve.tensor_copy(q[:, 0, :], qf[:, :]))
                link(dve.tensor_tensor(qr[:, :], qf[:, :], q[:, 0, :], ALU.subtract))
                link(dve.tensor_copy(q[:, 1, :], qr[:, :]))
                dve.tensor_tensor(q[:, 2, :], qr[:, :], q[:, 1, :], ALU.subtract).then_inc(s_q3, 1)

            def max_scores(L, b, i):
                u = n_attn[L, b]
                if u >= 1 and i == 0:
                    dve.wait_ge(s_nmx, u)
                for g in range(NG):
                    job = ("M", L, b, i, g)
                    k = made(job)
                    read(job, dve.tensor_reduce(nmx[:, u % 2, i, HPG * g:HPG * g + HPG],
                                                PS[:, k, 0:HPG * SK].rearrange("p (h s) -> p h s", h=HPG),
                                                AX.X, ALU.max, negate=True))

            def max_parts(L, b):
                u = n_attn[L, b]
                settled(("M", L, b, TPB - 1, NG - 2))
                settled(("M", L, b, TPB - 1, NG - 1))
                m = nmx[:, u % 2, :, :]
                link(dve.tensor_copy(nmxh[:, :, :], m))
                dve.tensor_copy(nmx2[:, u % 2, :, 0:NH], nmxh[:, :, :])
                dve.tensor_tensor(nmx2[:, u % 2, :, NH:2 * NH], m, nmxh[:, :, :], ALU.subtract).then_inc(s_nmx, 1)

            def join_heads(L, b):
                u = n_attn[L, b]
                low, high = const("low_rows"), const("high_rows")
                jb = ("PV", L, b, 1)
                settled(("PV", L, b, 0))
                k = made(jb)
                dve.scalar_tensor_tensor(att[:, 2, :], PS[:, k, :], low, att[:, 0, :], ALU.mult, ALU.add)
                read(jb, dve.scalar_tensor_tensor(att[:, 3, :], PS[:, k, :], high, att[:, 1, :], ALU.mult, ALU.add))

            def divide_heads(L, b):
                u = n_attn[L, b]
                settled(("PV", L, b, 1))
                link(dve.reciprocal(att[:, 4, :], att[:, 2, :]))
                link(dve.stream_shuffle(att[:, 2, :], att[:, 4, :], [(i + 16) % 32 for i in range(32)]))
                dve.tensor_tensor(att[:, 5, :], att[:, 3, :], att[:, 2, :], ALU.mult).then_inc(s_prod, 1)

            def add_out(L, b):
                k = made(("O", L, b))
                dve.wait_ge(s_bo, n_attn[L, b] + 1)
                x = tiles(X, b)
                read(("O", L, b), dve.tensor_tensor(x, PS[:, k, :].rearrange("p (i d) -> p i d", i=TPB), x, ALU.add))
                settled(("O", L, b))

            def spread(ap, n):
                return ap.unsqueeze(len(ap.shape)).to_broadcast(list(ap.shape) + [n])

            def over(ap, n):
                return ap.unsqueeze(1).to_broadcast([ap.shape[0], n] + list(ap.shape[1:]))

            def top(values, n=16):
                for i in range(TPB):
                    ins = dve.max(v8[:, i, :], values[:, i, 0:n])
                link(ins)
                for i in range(TPB):
                    ins = dve.max_index(i8[:, i, :], v8[:, i, :], values[:, i, 0:n])
                link(ins)
                link(dve.tensor_copy(if8[:, :, :], i8[:, :, :]))

            def chosen(dst, K, n):
                io = const("iota16")[:, 0:n]
                for i in range(TPB):
                    ins = dve.tensor_tensor(oh[:, i, 0:K, 0:n], over(io, K), spread(if8[:, i, 0:K], n), ALU.is_equal)
                link(ins)
                for i in range(TPB):
                    ins = dve.tensor_reduce(dst[:, i, :], oh[:, i, 0:K, 0:n].rearrange("p k e -> p e k"), AX.X, ALU.add)
                link(ins)

            def logits_of(L, b):
                k = made(("R", L, b))
                E = EXPERTS[L]
                z = PS[:, k, 0:16 * TPB].rearrange("p (i e) -> p i e", i=TPB)[:, :, 0:E]
                read(("R", L, b), dve.tensor_tensor(lg[:, :, 0:E], z, over(row(f"rb{L}"), TPB), ALU.add))
                settled(("R", L, b))
                return lg[:, :, 0:E]

            def route_moe(L, b):
                E = EXPERTS[L]
                n = n_moe[L, b]
                if n:
                    dve.wait_ge(s_cw, n)
                z = logits_of(L, b)
                top(z, E)
                w = r16[:, 0, :, 0:E]
                x = n_exp[L, b]
                dve.tensor_tensor(w, z, spread(v8[:, :, 0], E), ALU.subtract).then_inc(s_lr, 1)
                mask = r16[:, 1, :, 0:E]
                chosen(mask, 4 if L == 1 else 1, E)
                dve.wait_ge(s_le, x + 1)
                ex = r16[:, 2, :, 0:E]
                em = r16[:, 3, :, 0:E]
                link(dve.tensor_tensor(em, ex, mask, ALU.mult))
                link(dve.tensor_reduce(r1[:, 0, :], em if L == 1 else ex, AX.X, ALU.add))
                link(dve.reciprocal(r1[:, 1, :], r1[:, 0, :]))
                dve.tensor_tensor(tiles(C, b)[:, :, 0:E], em, spread(r1[:, 1, :], E), ALU.mult).then_inc(s_cw, 1)
                dve.wait_ge(s_cw, n + 1)

            def route_mha(L, b):
                E = EXPERTS[L]
                n = n_moe[L, b]
                z = logits_of(L, b)
                top(z, E)
                link(dve.tensor_tensor(r1[:, 2, :], if8[:, :, 0], if8[:, :, 1], ALU.max))
                dve.tensor_tensor(tiles(C, b)[:, :, 0:E], over(const("iota16")[:, 0:E], TPB), spread(r1[:, 2, :], E),
                                  ALU.is_equal).then_inc(s_cw, 1)
                dve.wait_ge(s_cw, n + 1)

            def route_glu(L, b):
                n = n_moe[L, b]
                dve.wait_ge(s_cw, n)
                dve.wait_ge(*slots.is_read(("R", L, b)))
                sig, s = r16[:, 0, :, :], r16[:, 1, :, :]
                link(dve.tensor_tensor(s, sig, over(row("rb7"), TPB), ALU.add))
                link(dve.tensor_reduce(g8[:, :, 0:4], s.rearrange("p i (g e) -> p i g e", g=4), AX.X, ALU.max))
                top(g8, 8)
                kg = r16[:, 2, :, 0:4]
                chosen(kg, 2, 4)
                kb = r16[:, 2, :, 4:8]
                link(dve.tensor_scalar(kb, kg, BIG, BIG, ALU.mult, ALU.subtract))
                sm = r16[:, 3, :, :]
                for i in range(TPB):
                    ins = dve.tensor_tensor(sm[:, i, :].rearrange("p (g e) -> p g e", g=4),
                                            s[:, i, :].rearrange("p (g e) -> p g e", g=4), spread(kg[:, i, :], 4), ALU.mult)
                link(ins)
                for i in range(TPB):
                    v = sm[:, i, :].rearrange("p (g e) -> p g e", g=4)
                    ins = dve.tensor_tensor(v, v, spread(kb[:, i, :], 4), ALU.add)
                link(ins)
                top(sm)
                mask = r16[:, 2, :, :]
                chosen(mask, 4, 16)
                c = tiles(C, b)
                link(dve.tensor_tensor(c, sig, mask, ALU.mult))
                d = c7[:, b % 2, :, :]
                link(dve.tensor_copy(c7h[:, 0, :, :], c))
                dve.tensor_copy(d[:, :, 0:16], c7h[:, 0, :, :])
                link(dve.tensor_tensor(lg[:, :, :], c, c7h[:, 0, :, :], ALU.subtract))
                link(dve.tensor_copy(c7h[:, 1, :, :], lg[:, :, :]))
                dve.tensor_copy(d[:, :, 16:32], c7h[:, 1, :, :])
                dve.tensor_tensor(d[:, :, 32:48], lg[:, :, :], c7h[:, 1, :, :], ALU.subtract).then_inc(s_cw, 1)
                dve.wait_ge(s_cw, n + 1)

            def moe_unit(L, b, hook):
                dst = H5 if L == 5 else X
                E = EXPERTS[L]
                k = made(("B2", L, b))
                d = tiles(dst, b)
                read(("B2", L, b), dve.tensor_tensor(d, PS[:, k, :].rearrange("p (i d) -> p i d", i=TPB), d, ALU.add))
                last = ("B2", L, b)
                for e in range(E):
                    k = made(("Y", L, b, e))
                    settled(last)
                    for i in range(TPB):
                        t = TPB * b + i
                        ins = dve.scalar_tensor_tensor(dst[:, t, :], PS[:, k, 128 * i:128 * i + 128],
                                                       C[:, t, e:e + 1], dst[:, t, :], ALU.mult, ALU.add)
                    last = ("Y", L, b, e)
                    read(last, ins)
                    hook(e)
                settled(last)
                if L == 5:
                    y = tiles(XN, b)
                    norm_stats("ln2", L, b, d)
                    norm_apply("ln2", L, b, d, y)
                    g, s = over(row("ln2_g"), TPB), over(row("ln2_b"), TPB)
                    link(dve.tensor_tensor(y, y, g, ALU.mult))
                    link(dve.tensor_tensor(y, y, s, ALU.add))
                    link(dve.tensor_tensor(tiles(X, b), tiles(X, b), y, ALU.add))

            def glu_unit(L, b, hook):
                for p in range(GLU_PAIRS):
                    x = (GLU_PAIRS * b + p) % 3
                    n = GLU_PAIRS * b + p
                    dve.wait_ge(s_sil, n + 1)
                    k = made(("H", L, b, p))
                    read(("H", L, b, p), dve.tensor_tensor(gl[:, x, 0, :], PS[:, k + 1, :], gl[:, x, 0, :], ALU.mult))
                    settled(("H", L, b, p))
                    k = made(("CB", L, b, p))
                    if n >= 3:
                        glu_summed(dve, n - 3)
                    read(("CB", L, b, p), dve.tensor_tensor(gl[:, x, 1, :], PS[:, k, :], gl[:, x, 0, :], ALU.mult))
                    hook(p)
                k = made(("Y", L, b))
                x = tiles(X, b)
                read(("Y", L, b), dve.tensor_tensor(x, PS[:, k, :].rearrange("p (i d) -> p i d", i=TPB), x, ALU.add))

            def window_prep():
                pt = row("pt")
                st, en, lf = lrow[:, 0, :], lrow[:, 1, :], lrow[:, 2, :]
                dve.wait_ge(s_ks1[2], 16 * 12)
                dve.wait_ge(s_ks[2], 16 * 12)
                link(dve.tensor_copy(lf, leni[:, :]))
                link(dve.tensor_scalar(st, pt, WINDOW, 0.0, ALU.subtract, ALU.max))
                link(dve.tensor_scalar(lrow[:, 3, :], pt, WINDOW, None, ALU.add))
                link(dve.tensor_tensor(en, lrow[:, 3, :], lf, ALU.min))
                io = const("iota77")
                for b in range(NB):
                    ins = dve.tensor_scalar(negm[:, b, :], io, st[:, b:b + 1], None, ALU.is_ge)
                link(ins)
                for b in range(NB):
                    ins = dve.scalar_tensor_tensor(keep[:, b, :], io, en[:, b:b + 1], negm[:, b, :], ALU.is_le, ALU.mult)
                link(ins)
                link(dve.tensor_scalar(negm[:, :, :], keep[:, :, :], MASKED, MASKED, ALU.mult, ALU.subtract))
                link(dve.tensor_scalar(gau[:, 0, :], row("pt", SK), const("iota_col", SK), None, ALU.subtract))
                dve.tensor_tensor(gau[:, 1, :], gau[:, 0, :], gau[:, 0, :], ALU.mult).then_inc(s_lg, 1)

            def local_layer(L):
                dve.wait_ge(s_ge, 1)
                for b in range(NB):
                    ins = dve.tensor_scalar(Gc[:, b, :], ctxN[:, b, :], gau[:, 2, b:b + 1], None, ALU.mult)
                ins.then_inc(s_gc, 1)
                front(L, NB - 1)
                for b in range(NB):
                    k = made(("LS", b))
                    s = LS[:, b, :, :]
                    read(("LS", b), dve.tensor_tensor(s, PS[:, k, 0:TPB * SK].rearrange("p (i s) -> p i s", i=TPB),
                                                      over(keep[:, b, :], TPB), ALU.mult))
                    settled(("LS", b))
                    link(dve.tensor_tensor(s, s, over(negm[:, b, :], TPB), ALU.add))
                    link(dve.tensor_reduce(r1[:, 0, :], s, AX.X, ALU.max))
                    dve.tensor_tensor(s, s, spread(r1[:, 0, :], SK), ALU.subtract).then_inc(s_ls, 1)
                for b in range(NB):
                    s = LS[:, b, :, :]
                    dve.wait_ge(s_lx, b + 1)
                    link(dve.tensor_reduce(r1[:, 1, :], s, AX.X, ALU.add))
                    link(dve.reciprocal(r1[:, 2, :], r1[:, 1, :]))
                    dve.tensor_tensor(s, s, spread(r1[:, 2, :], SK), ALU.mult).then_inc(s_lp, 1)
                for b in range(NB):
                    dve.wait_ge(*slots.is_read(("LO", b)))
                    x = tiles(X, b)
                    link(dve.tensor_tensor(x, tiles(XN, b), x, ALU.add))
                    front_stats(L + 1, b)
                    if b:
                        front_apply(L + 1, b - 1)
                front_apply(L + 1, NB - 1)

            def mha_layer(L):
                for i in range(TPB):
                    for b in range(NB):
                        k = made(("QKV", b, i))
                        read(("QKV", b, i), dve.tensor_tensor(QKV[:, b, i, :], PS[:, k, 0:3 * P], row("in_b"), ALU.add))
                    settled(("QKV", NB - 2, i))
                    settled(("QKV", NB - 1, i))
                    dve.engine_nop().then_inc(s_pin, 1)
                for j in range(TPB):
                    dve.wait_ge(s_p5, j + 1)
                    sc = m5[:, j % 2, 0, :]
                    link(dve.tensor_reduce(sc, PROD[j % 2].rearrange("p (x d) -> p x d", d=DK), AX.X, ALU.add))
                    sc4 = sc.rearrange("p (t s h) -> p t s h", t=NB, s=NB)
                    mx = m5[:, j % 2, 1, 0:NB * NH].rearrange("p (t h) -> p t h", t=NB)
                    link(dve.tensor_reduce(mx, sc4.rearrange("p t s h -> p t h s"), AX.X, ALU.max))
                    for t in range(NB):
                        ins = dve.tensor_tensor(sc4[:, t, :, :], sc4[:, t, :, :], over(mx[:, t, :], NB), ALU.subtract)
                    ins.then_inc(s_s5, 1)
                    dve.wait_ge(s_e5, j + 1)
                    sm = m5[:, j % 2, 1, 64:128].rearrange("p (t h) -> p t h", t=NB)
                    rs = m5[:, j % 2, 1, 128:192].rearrange("p (t h) -> p t h", t=NB)
                    link(dve.tensor_reduce(sm, sc4.rearrange("p t s h -> p t h s"), AX.X, ALU.add))
                    link(dve.reciprocal(rs, sm))
                    for t in range(NB):
                        ins = dve.tensor_tensor(sc4[:, t, :, :], sc4[:, t, :, :], over(rs[:, t, :], NB), ALU.mult)
                    link(ins)
                    pv = PV5.rearrange("p (t s c) -> p t s c", t=NB, s=NB)
                    for t in range(NB):
                        for s in range(NB):
                            ins = dve.tensor_tensor(pv[:, t, s, :].rearrange("p (h d) -> p h d", h=NH),
                                                    spread(sc4[:, t, s, :], DK),
                                                    QKV[:, s, j, 2 * P:3 * P].rearrange("p (h d) -> p h d", h=NH), ALU.mult)
                    link(ins)
                    for t in range(NB):
                        ins = dve.tensor_reduce(LCTX[:, t, j, :], pv[:, t, :, :].rearrange("p s c -> p c s"), AX.X, ALU.add)
                    ins.then_inc(s_c5, 1)
                    dve.wait_ge(s_c5, j + 1)

                def finish_h(b):
                    h = tiles(H5, b)
                    norm_apply("ln1", L, b, h, h)
                    link(dve.tensor_tensor(h, h, over(row("ln1_g"), TPB), ALU.mult))
                    dve.tensor_tensor(h, h, over(row("ln1_b"), TPB), ALU.add).then_inc(s_h5, 1)
                    dve.wait_ge(s_h5, b + 1)

                for b in range(NB):
                    k = made(("AO", b))
                    dve.wait_ge(s_ob, b + 1)
                    h = tiles(H5, b)
                    read(("AO", b), dve.tensor_tensor(h, PS[:, k, :].rearrange("p (i d) -> p i d", i=TPB), tiles(XN, b), ALU.add))
                    settled(("AO", b))
                    norm_stats("ln1", L, b, h)
                    if b:
                        finish_h(b - 1)
                route_mha(L, 0)
                finish_h(NB - 1)

            def stage_of(stage, L, b):
                if stage == "stats":
                    front_stats(L, b)
                elif stage == "norm":
                    front_apply(L, b)
                elif stage == "front":
                    if LAYERS[L] in (MOE, GLU, LOCAL):
                        front(L, b)
                elif stage == "keys":
                    dve.wait_ge(s_c, 16 * 2)
                    keys(0)
                elif stage == "values":
                    values(0)
                elif stage == "Q":
                    split_q(L, b)
                elif stage == "MT":
                    max_parts(L, b)
                elif stage == "R":
                    {MOE: route_moe, MHA: route_mha, GLU: route_glu}[LAYERS[L]](L, b)
                elif stage != "CT":
                    max_scores(L, b, int(stage[1]))

            stage[0] = NL
            dve.memset(KS1[96:128, :, :], 0.0).then_inc(s_ones, 1)
            link(dve.memset(g8[:, :, :], -3e38))
            link(dve.memset(c7[:, :, :, 48:64], 0.0))
            link(dve.memset(c7[:, :, :, 48:49], 1.0))
            dve.wait_ge(s_dl, 16)
            delta_parts()
            for x in BEFORE:
                stage_of(*x)
            for n, (L, b) in enumerate(units):
                stage[0] = L
                if LAYERS[L] == LOCAL:
                    if b == 0:
                        local_layer(L)
                    continue
                if LAYERS[L] == MHA and b == 0:
                    mha_layer(L)
                todo = plan((L, b), "dve")
                prev = units[n - 1] if n and LAYERS[units[n - 1][0]] == ATTN else None
                if prev:
                    join_heads(*prev)

                def hook(step):
                    if step == ADD_AT and prev:
                        add_out(*prev)
                    for at, *x in todo:
                        if at == step:
                            stage_of(*x)
                    if step == DIVIDE_AT and prev:
                        divide_heads(*prev)
                    if step == 3 and (L, b) == (1, 2):
                        k_prep(1)
                    if step == 3 and (L, b) == (3, 1):
                        k_prep(2)
                    if step == 3 and (L, b) == (3, 2):
                        window_prep()

                if LAYERS[L] == ATTN:
                    for p in range(PAIRS):
                        hook(p)
                else:
                    {MOE: moe_unit, MHA: moe_unit, GLU: glu_unit}[LAYERS[L]](L, b, hook)


        @block.scalar
        def _(act):
            chain = [0]

            def made(job):
                act.wait_ge(*slots.is_made(job))
                return slots.bank(job)

            def read(job, ins):
                ins.then_inc(slots.is_read(job)[0], 1)

            def move(job, dst, src):
                k = made(job)
                read(job, nc.scalar.copy(dst, src(k)))

            def front(L, b):
                move(("T", L, b), XT[:, b, :], lambda k: PS[:, k, :])

            def place_max(L, b):
                u = n_attn[L, b]
                move(("MT", L, b), T2[96:128, u % QS, :, :],
                     lambda k: PS[0:2 * NH, k, :].unsqueeze(1).to_broadcast([2 * NH, NG, SQ]))

            def attn_unit(L, b, hook):
                u = n_attn[L, b]
                for p in range(PAIRS):
                    k = made(("S", L, b, p))
                    if PAIRS * u + p >= ES:
                        values_summed(act, PAIRS * u + p - ES)
                    read(("S", L, b, p), nc.scalar.activation(Eexp[:, (PAIRS * u + p) % ES, :, :], PS[0:SK, k:k + 2, :], ACT.Exp))
                    hook(p)

            def part_heads(L, b):
                u = n_attn[L, b]
                k = made(("PV", L, b, 0))
                if u:
                    act.wait_ge(*slots.is_read(("PV", *attn_units[u - 1], 1)))
                nc.scalar.mul(att[:, 0, :], PS[:, k, :], const("high_rows"))
                read(("PV", L, b, 0), nc.scalar.mul(att[:, 1, :], PS[:, k, :], const("low_rows")))

            def route(L, b):
                E = EXPERTS[L]
                if LAYERS[L] == GLU:
                    act.wait_ge(s_cw, n_moe[L, b])
                    k = made(("R", L, b))
                    read(("R", L, b), nc.scalar.activation(r16[:, 0, :, :], PS[:, k, 0:16 * TPB].rearrange("p (i e) -> p i e", i=TPB),
                                                           ACT.Sigmoid))
                elif LAYERS[L] == MOE:
                    act.wait_ge(s_lr, n_exp[L, b] + 1)
                    nc.scalar.activation(r16[:, 2, :, 0:E], r16[:, 0, :, 0:E], ACT.Exp).then_inc(s_le, 1)

            def turn_combine(L, b):
                if LAYERS[L] == GLU:
                    move(("CT", L, b), cT7[:, b % 2, :], lambda k: PS[0:64, k, :])
                else:
                    move(("CT", L, b), cT[0:EXPERTS[L], b % 2, :], lambda k: PS[0:EXPERTS[L], k, :])

            def moe_unit(L, b, hook):
                E, NC = EXPERTS[L], HIDDEN_CHUNKS[L]
                for e in range(E):
                    k = made(("H", L, b, e))
                    n = E * b + e
                    if n >= HS:
                        act.wait_ge(*slots.is_made(("Y", L, (n - HS) // E, (n - HS) % E)))
                    for c in range(NC):
                        ins = nc.scalar.activation(hT[:, n % HS, c, :], PS[:, k + c, :], ACT.Relu if L == 3 else ACT.Gelu,
                                                   bias=col(f"b1_{L}", NC * e + c))
                    read(("H", L, b, e), ins)
                    hook(e)

            def glu_unit(L, b, hook):
                for p in range(GLU_PAIRS):
                    n = GLU_PAIRS * b + p
                    k = made(("H", L, b, p))
                    if n >= 3:
                        m = n - 3
                        act.wait_ge(*slots.is_read(("CB", L, m // GLU_PAIRS, m % GLU_PAIRS)))
                    nc.scalar.activation(gl[:, n % 3, 0, :], PS[:, k, :], ACT.Silu).then_inc(s_sil, 1)
                    hook(p)

            def local_layer(L):
                act.wait_ge(s_lg, 1)
                nc.scalar.activation(gau[:, 2, :], gau[:, 1, :], ACT.Exp, scale=-1.0 / DEV_POW).then_inc(s_ge, 1)
                move(("E4",), Eloc, lambda k: PS[:, k, 0:CK])
                front(L, NB - 1)
                for b in range(NB):
                    act.wait_ge(s_ls, b + 1)
                    nc.scalar.activation(LS[:, b, :, :], LS[:, b, :, :], ACT.Exp).then_inc(s_lx, 1)
                for b in range(NB):
                    move(("LT", b), LPT[0:SK, b, :], lambda k: PS[0:SK, k, :])
                for b in range(NB):
                    move(("LC", b), hT[:, b % HS, b // HS, :], lambda k: PS[:, k, :])
                for b in range(NB):
                    k = made(("LO", b))
                    read(("LO", b), nc.scalar.activation(XN[:, TPB * b:TPB * b + TPB, :],
                                                         PS[:, k, :].rearrange("p (i d) -> p i d", i=TPB), ACT.Tanh))

            def mha_layer(L):
                for b in range(NB):
                    front(L, b)
                for j in range(TPB):
                    act.wait_ge(s_s5, j + 1)
                    sc = m5[:, j % 2, 0, :]
                    nc.scalar.activation(sc, sc, ACT.Exp, scale=ATT_SCALE).then_inc(s_e5, 1)
                for b in range(NB):
                    move(("AT", b), hT[:, b % HS, b // HS, :], lambda k: PS[:, k, :])
                    if b == NB - 2:
                        move(("T2", L, 0), XT[:, 0, :], lambda k: PS[:, k, :])
                turn_combine(L, 0)

            def stage_of(stage, L, b):
                if stage == "front":
                    move(("T2" if LAYERS[L] == MHA else "T", L, b), XT[:, b, :], lambda k: PS[:, k, :])
                elif stage == "MT":
                    place_max(L, b)
                elif stage == "R":
                    route(L, b)
                elif stage == "CT":
                    turn_combine(L, b)

            act.wait_ge(s_c, 16 * 2)
            nc.scalar.copy(KS2[96:128, :, :], const("pick_head")[96:128, :].unsqueeze(2).to_broadcast([32, NH, CK])).then_inc(s_pick, 1)
            for x in BEFORE:
                stage_of(*x)
                if x == ("Q", 0, 0):
                    act.wait_ge(s_q3, 1)
                    for part in range(3):
                        for g in range(NG):
                            nc.scalar.copy(T1[32 * part:32 * part + 32, 0, g, :],
                                           qparts[32 * g:32 * g + 32, part, :]).then_inc(s_t1[0], 16)
            act.wait_ge(s_rows, 16 * 4)
            nc.scalar.copy(pick7[:, :], H5[0:64, 0:GLU_PAIRS, :].rearrange("p a b -> p (a b)")).then_inc(s_pick, 1)
            for n, (L, b) in enumerate(units):
                if b == 0 and L:
                    if LAYERS[L - 1] == ATTN:
                        values_summed(act, PAIRS * n_attn[L - 1, NB - 1] + PAIRS - 1)
                    elif LAYERS[L - 1] in (MOE, MHA):
                        act.wait_ge(*slots.is_made(("Y", L - 1, NB - 1, EXPERTS[L - 1] - 1)))
                if LAYERS[L] == LOCAL:
                    if b == 0:
                        local_layer(L)
                    continue
                if LAYERS[L] == MHA and b == 0:
                    mha_layer(L)
                todo = plan((L, b), "act")
                prev = units[n - 1] if n and LAYERS[units[n - 1][0]] == ATTN else None

                def hook(step):
                    for at, *x in todo:
                        if at == step:
                            stage_of(*x)
                    if step == 5 and LAYERS[L] == ATTN:
                        part_heads(L, b)

                {ATTN: attn_unit, MOE: moe_unit, MHA: moe_unit, GLU: glu_unit}[LAYERS[L]](L, b, hook)

        @block.gpsimd
        def _(pool):
            pool.memset(mhalf[:, :], -0.5).then_inc(s_pool0, 1)
            pool.memset(V2[:, :, :, :], 0.0).then_inc(s_pool0, 1)
            pool.wait_ge(s_pool0, 2)
            for half in range(2):
                for sub in range(2):
                    h0, c0 = 8 * half + 4 * sub, 16 - 16 * half + 8 * sub
                    for b in range(NB):
                        ins = pool.memset(V2[:, b, h0:h0 + 4, c0:c0 + DK], 1.0)
            ins.then_inc(s_pool0, 1)
            pool.memset(T1[96:128, :, :, :], 1.0).then_inc(s_pool0, 1)
            pool.wait_ge(s_pool0, 4)
            pool.wait_ge(s_rows, 16 * 4)
            for n, (which, L, b) in enumerate(norms):
                if (which, L, b) == ("ln1", 5, 0):
                    for j in range(TPB):
                        pool.wait_ge(s_pin, j + 1)
                        if j >= 2:
                            pool.wait_ge(s_s5, j - 1)
                        prod = PROD[j % 2].rearrange("p (t s c) -> p t s c", t=NB, s=NB)
                        for t in range(NB):
                            ins = pool.tensor_tensor(prod[:, t, :, :],
                                                     QKV[:, t, j, 0:P].unsqueeze(1).to_broadcast([P, NB, P]),
                                                     QKV[:, :, j, P:2 * P], ALU.mult)
                        ins.then_inc(s_p5, 1)
                        if j == 1:
                            for t in range(NB):
                                x = XN[:, TPB * t:TPB * t + TPB, :]
                                pool.tensor_tensor(x, x, row("out_b").unsqueeze(1).to_broadcast([P, TPB, P]),
                                                   ALU.add).then_inc(s_ob, 1)
                pool.wait_ge(s_stat, n + 1)
                pool.tensor_scalar(vare[:, n % 2, :], mv[:, n % 2, :, 1], EPS, None, ALU.add).then_inc(s_vare, 1)
                pool.wait_ge(s_vare, n + 1)
                pool.tensor_tensor(rstd[:, n % 2, :], vare[:, n % 2, :], mhalf[:, :], ALU.pow).then_inc(s_rstd, 1)
                if which == "in" and LAYERS[L] == ATTN:
                    pool.wait_ge(s_xn, n_in[L, b])
                    x = X[:, TPB * b:TPB * b + TPB, :]
                    bo = row(f"bo{ATTN_NO[L]}").unsqueeze(1).to_broadcast([P, TPB, P])
                    pool.tensor_tensor(x, x, bo, ALU.add).then_inc(s_bo, 1)

        @block.sync
        def _(sp):
            xd = A["x"].rearrange("(t p) d -> p t d", p=P)
            sp.dma_start(drow[:, 0, :], A["delta"]).then_inc(s_dl, 16)
            sp.dma_start(ctxT[:, :], A["ctxT"]).then_inc(s_kw, 16)
            sp.dma_start(wattn[:, 0, :, :], A["wattn"][:, 0]).then_inc(s_kw, 16)
            sp.dma_start(consts[:, :], A["consts"]).then_inc(s_c, 16)
            sp.dma_start(cols[:, :], A["cols"]).then_inc(s_c, 16)
            sp.dma_start(X[:, 0:TPB, :], xd[:, 0:TPB, :]).then_inc(s_x[0], 16)
            sp.dma_start(rows[:, :], A["rows"].partition_broadcast(P)).then_inc(s_rows, 16)
            sp.dma_start(ctxN[:, :, :], A["ctxN"]).then_inc(s_rows, 16)
            sp.dma_start(leni[:, :], A["lens"].partition_broadcast(P)).then_inc(s_rows, 16)
            sp.dma_start(H5[0:64, 0:GLU_PAIRS, :], A["pick_pair"]).then_inc(s_rows, 16)
            for b in range(1, NB):
                sp.dma_start(X[:, TPB * b:TPB * b + TPB, :], xd[:, TPB * b:TPB * b + TPB, :]).then_inc(s_x[b], 16)

            def place(dst, src, done):
                for g in range(NG):
                    sp.dma_start(dst(g), src(g)).then_inc(done, 16)

            def place_keys(K, parts, done):
                for q, part in enumerate(parts):
                    place(lambda g: K[32 * q:32 * q + 32, HPG * g:HPG * g + HPG, :],
                          lambda g: KB[32 * g:32 * g + 32, part, :, :], done)

            def place_queries(u, T, parts, done):
                for q, part in enumerate(parts):
                    place(lambda g: T[32 * q:32 * q + 32, u % QS, g, :],
                          lambda g: qparts[32 * g:32 * g + 32, part, :], done)

            def place_k(a):
                sp.wait_ge(s_kb, a + 1)
                place_keys(KS1, (0, 0, 0), s_ks1[a])
                if a == 0:
                    sp.wait_ge(s_q3, 1)
                    place_queries(0, T2, (0, 1, 0), s_t2[0])
                place_keys(KS2, (1, 1, 2), s_ks[a])

            def place_q(u):
                sp.wait_ge(s_q3, u + 1)
                place_queries(u, T1, (0, 1, 2), s_t1[u])
                place_queries(u, T2, (0, 1, 0), s_t2[u])

            sp.wait_ge(s_ones, 1)
            sp.wait_ge(s_delta, 1)
            for j in range(3):
                sp.dma_start(KS1[96 + j:97 + j, :, :], dparts[:, j, :].unsqueeze(1).to_broadcast([1, NH, CK])).then_inc(s_drow, 16)
            place_k(0)
            place_q(1)
            sp.dma_start(router[:, :], A["router"]).then_inc(s_w["a"], 16)
            for a in (1, 2):
                sp.dma_start(wattn[:, a, :, :], A["wattn"][:, a]).then_inc(s_w["a"], 16)
            for L in (1, 3, 5):
                sp.dma_start(w1[L][:, :, :] if L > 1 else w1[L], A[f"w1_{L}"]).then_inc(s_w[f"m{L}"], 16)
                sp.dma_start(w2[L][:, :, :, :] if L > 1 else w2[L], A[f"w2_{L}"]).then_inc(s_w[f"m{L}"], 16)
                sp.dma_start(b2[L][:, :], A[f"b2_{L}"]).then_inc(s_w[f"m{L}"], 16)
            sp.dma_start(wloc[:, :, :], A["wloc"]).then_inc(s_w["loc"], 16)
            sp.dma_start(win5[:, :], A["win5"]).then_inc(s_w["loc"], 16)
            for u in range(2, 4):
                place_q(u)
            place_k(1)
            for u in range(4, 8):
                place_q(u)
            place_k(2)
            sp.wait_ge(s_c5, TPB)
            sp.dma_start(w1[7], A["w1_7"]).then_inc(s_w["m7"], 16)
            sp.dma_start(w3_7, A["w3_7"]).then_inc(s_w["m7"], 16)
            sp.dma_start(w2[7], A["w2_7"]).then_inc(s_w["m7"], 16)
            for u in range(8, 12):
                place_q(u)
            od = out.rearrange("(t p) d -> p t d", p=P)
            for b in range(NB):
                sp.wait_ge(*slots.is_read(("Y", 7, b)))
                sp.dma_start(od[:, TPB * b:TPB * b + TPB, :], X[:, TPB * b:TPB * b + TPB, :]).then_inc(s_out, 16)
            sp.wait_ge(s_out, 16 * NB)


def constants():
    r = np.arange(P)
    c = np.zeros((P, CONSTS_N), np.float32)

    def put(name, v):
        a, b = CONSTS[name]
        c[:, a:b] = v

    put("ident", np.eye(P))
    put("head_mask", (r[:, None] % 32) // DK == np.arange(HPG)[None])
    put("low_rows", (r % 32 < 16)[:, None])
    put("high_rows", (r % 32 >= 16)[:, None])
    put("pick_head", r[:, None] % NH == np.arange(NH)[None])
    put("iota16", np.arange(16)[None])
    put("iota77", np.arange(SK)[None])
    put("iota_col", r[:, None])
    pick = np.zeros((64, GLU_PAIRS, P), np.float32)
    for p in range(GLU_PAIRS - 1):
        for half in range(2):
            for part in range(3):
                pick[16 * part + 2 * p + half, p, 64 * half:64 * half + 64] = 1
    pick[48, GLU_PAIRS - 1, :] = 1
    return c, pick


def lay_out(i):
    f = {k: np.asarray(v) for k, v in i.items()}
    A = {}
    A["consts"], A["pick_pair"] = constants()
    A["x"] = f["x"].reshape(NB * SQ, P)
    A["ctxT"] = f["ctx_1024"].reshape(CK, P).T
    A["ctxN"] = f["ctx_1024"].transpose(1, 0, 2)
    A["delta"] = f["fside_BxS2_0"].reshape(1, CK)
    A["lens"] = f["_lenS2"]
    order = np.zeros(P, np.int64)
    for h in range(NH):
        order[num_row(h):num_row(h) + DK] = DK * h + np.arange(DK)
    sets = []
    for L in (0, 1, 3):
        w = [f[f"L{L}_xcond_W{n}"].T for n in "qkvo"]
        w[3] = w[3][order]
        sets.append(np.stack(w, 1))
    A["wattn"] = np.stack(sets, 1)
    A["router"] = np.concatenate([f["L0_ffn_router_w"], f["L1_ffn_Wr"], f["L2_ffn_router_w"].T, f["L3_ffn_gate_w"].T], 1)
    for L, n, k1, k2, kb in ((1, 0, "w1", "w2", "b2"), (3, 1, "W1", "W2", "b2")):
        A[f"w1_{L}"] = f[f"L{n}_ffn_{k1}"].transpose(1, 0, 2)
        w = f[f"L{n}_ffn_{k2}"]
        A[f"w2_{L}"] = w.reshape(w.shape[0], 2, P, P).transpose(2, 0, 1, 3)
        A[f"b2_{L}"] = f[f"L{n}_ffn_{kb}"]
    A["w1_5"] = f["L2_ffn_w1"].transpose(2, 0, 1)
    A["w2_5"] = f["L2_ffn_w2"].transpose(2, 0, 1)[:, :, None]
    A["b2_5"] = f["L2_ffn_b2"]
    A["wloc"] = np.stack([f["L2_xcond_W_a"].T, f["L2_xcond_W_c"][:, :P].T, f["L2_xcond_W_c"][:, P:].T], 1)
    A["win5"] = np.concatenate([f["L2_ffn_in_proj_w"].T, f["L2_ffn_out_w"].T], 1)
    pad = np.zeros((P, 64), np.float32)
    for n in (1, 3):
        w = np.concatenate([f[f"L3_ffn_w{n}"].reshape(16 * 64, P).T, f[f"L3_ffn_ws{n}"].T, pad], 1)
        A[f"w{n}_7"] = w.reshape(P, GLU_PAIRS, P)
    w = np.concatenate([f["L3_ffn_w2"].transpose(0, 2, 1).reshape(16 * 64, P), f["L3_ffn_ws2"].T, pad.T], 0)
    A["w2_7"] = w.reshape(GLU_PAIRS, P, P).transpose(1, 0, 2)
    cols = [f[f"L{L}_xcond_b{n}"][:, None] for n in "qk" for L in (0, 1, 3)]
    cols += [f["L0_ffn_b1"].reshape(32, P).T, f["L1_ffn_b1"].reshape(16, P).T, f["L2_ffn_b1"].T]
    A["cols"] = np.concatenate(cols, 1)
    A["rows"] = np.concatenate([f[f"L{L}_xcond_b{n}"] for n in "vo" for L in (0, 1, 3)] + [
        f["L0_ffn_router_b"], f["L1_ffn_br"], f["L2_ffn_router_b"], f["L3_ffn_gate_bias"], f["L2_ffn_in_proj_b"],
        f["L2_ffn_out_b"], f["L2_ffn_ln1_g"], f["L2_ffn_ln1_b"], f["L2_ffn_ln2_g"], f["L2_ffn_ln2_b"],
        f["condB_tau"], f["condB_pt"]])
    return {k: np.ascontiguousarray(v) for k, v in A.items()}


def kernel(**inputs):
    import numpy as _np
    import concourse.bacc as _bacc
    from concourse import mybir as _mybir
    from concourse.bass_utils import run_bass_kernel_spmd as _run

    nc = _bacc.Bacc("TRN2", target_bir_lowering=False, num_devices=1)
    arrays = {f"in_{k}": v for k, v in lay_out(inputs).items()}
    args = {k[3:]: nc.dram_tensor(k, v.shape, _mybir.dt.from_np(v.dtype), kind="ExternalInput").ap()
            for k, v in arrays.items()}
    out = nc.dram_tensor("out_0", (NB * SQ, P), F32, kind="ExternalOutput").ap()
    build(nc, args, out)
    r = _run(nc, [arrays], core_ids=[0])
    return _np.asarray(r.results[0]["out_0"]).reshape(NB, SQ, P)
```

```python
from contextlib import ExitStack

import numpy as np

import concourse.bass as bass
from concourse import mybir
from concourse.alu_op_type import AluOpType as ALU

F32 = mybir.dt.float32
BF16 = mybir.dt.bfloat16
U32 = mybir.dt.uint32
I32 = mybir.dt.int32
ACT = mybir.ActivationFunctionType
AX = mybir.AxisListType

P = 128
NB = 4
SQ = 512
TPB = SQ // P
NT = NB * TPB
SK = 77
CK = NB * SK
NH = 16
DK = P // NH
NG = 4
HPG = NH // NG
PAIRS = NH // 2
EPS = 1e-5
ATT_SCALE = float(np.float32(1.0) / np.sqrt(np.float32(DK)))
BIG = 1e30
LOCAL_EARLY = 2
POOL_FROM = 3
WINDOW, DEV_POW, MASKED = 16.0, 128.0, 1e9

PLACES = {
    0: {"M0": (0, 0, 0), "M1": (1, 0, 0), "M2": (2, 2, 0), "M3": (3, 3, 0), "MT": (5, 3, 7),
        "front": (1, 0, 3), "R": (2, 4, 5), "CT": (7, 6, 7), "Q": (2, 2, 3), "stats+": (0, 6, 0),
        "norm+": (0, 7, 0), "front+": (2, 0, 3), "stats": (1, 0, 0), "norm": (0, 1, 0)},
    1: {"front": (3, 0, 4), "R": (6, 6, 7), "CT": (11, 9, 11), "M0": (0, 0, 0), "M1": (2, 2, 0),
        "M2": (4, 3, 0), "M3": (8, 6, 2), "MT": (9, 6, 13), "Q": (4, 5, 5), "stats+": (0, 12, 0),
        "norm+": (0, 14, 0), "front+": (0, 0, 2), "stats": (0, 0, 0), "norm": (0, 1, 0)},
    2: {"M0": (0, 0, 0), "M1": (1, 1, 0), "M2": (2, 2, 0), "M3": (5, 5, 2), "MT": (7, 5, 7),
        "front": (1, 0, 2), "R": (2, 3, 3), "CT": (7, 6, 7), "Q": (2, 3, 3), "stats+": (2, 7, 2),
        "norm+": (0, 7, 0), "front+": (0, 0, 1), "stats": (0, 0, 0), "norm": (0, 1, 0)},
    3: {"front": (2, 0, 2), "R": (3, 3, 3), "CT": (7, 6, 7), "LE": (2, 5, 2), "LS0": (3, 4, 5),
        "LN0": (0, 6, 0), "LT0": (7, 1, 7), "LS1": (1, 0, 3), "LN1": (0, 3, 0), "LT1": (5, 0, 6),
        "LS2": (4, 4, 5), "LN2": (0, 6, 0), "LT2": (7, 0, 7), "stats": (0, 0, 0), "norm": (0, 1, 0),
        "LC0": (2, 0, 3), "LO0": (5, 7, 6), "LC1": (6, 0, 6), "LO1": (7, 7, 7)},
    5: {"front": (0, 0, 1), "R": (5, 5, 5), "CT": (7, 6, 7), "M0": (0, 0, 0), "M1": (1, 0, 0),
        "M2": (2, 1, 0), "M3": (4, 3, 1), "MT": (4, 3, 6), "Q": (2, 3, 3), "stats+": (0, 3, 0),
        "norm+": (0, 7, 0), "front+": (0, 0, 2)},
    6: {"M0": (0, 0, 0), "M1": (1, 1, 0), "M2": (2, 2, 0), "M3": (3, 3, 0), "MT": (6, 3, 7),
        "front": (2, 0, 3), "R": (3, 4, 4), "CT": (7, 6, 7), "Q": (2, 2, 3), "stats+": (0, 6, 0),
        "norm+": (0, 7, 0), "front+": (1, 0, 2), "stats": (0, 0, 0), "norm": (0, 1, 0)},
    7: {"front": (1, 1, 3), "R": (1, 3, 3), "CT": (7, 6, 8), "stats": (0, 0, 0), "norm": (0, 2, 0)},
}
EPILOGUE = {0: (3, 7, 7), 1: (3, 8, 7), 2: (3, 7, 6), 3: (1, 7, 7), 6: (3, 6, 7), 7: (3, 8, 8)}

ATTN, MOE, LOCAL, MHA, GLU = "attn", "moe", "local", "mha", "glu"
LAYERS = [ATTN, MOE, ATTN, MOE, LOCAL, MHA, ATTN, GLU]
NL = len(LAYERS)
ATTN_NO = {0: 0, 2: 1, 6: 2}
EXPERTS = {1: 16, 3: 8, 5: 8, 7: 16}
HIDDEN_CHUNKS = {1: 2, 3: 2, 5: 1}
GLU_PAIRS = 9

ROWS = {}
ROWS_N = 0
for _name, _n in (("bv0", 128), ("bv1", 128), ("bv2", 128), ("bo0", 128), ("bo1", 128), ("bo2", 128),
                  ("rb1", 16), ("rb3", 8), ("rb5", 8), ("rb7", 16), ("in_b", 384), ("out_b", 128),
                  ("ln1_g", 128), ("ln1_b", 128), ("ln2_g", 128), ("ln2_b", 128), ("tau", 4), ("pt", 4)):
    ROWS[_name] = (ROWS_N, ROWS_N + _n)
    ROWS_N += _n

CONSTS = {}
CONSTS_N = 0
for _name, _n in (("ident", 128), ("head_mask", HPG), ("low_rows", 1), ("high_rows", 1), ("pick_head", NH),
                  ("iota16", 16), ("iota77", SK), ("iota_col", 1)):
    CONSTS[_name] = (CONSTS_N, CONSTS_N + _n)
    CONSTS_N += _n

COLS = {}
COLS_N = 0
for _name, _n in (("bq0", 1), ("bq1", 1), ("bq2", 1), ("bk0", 1), ("bk1", 1), ("bk2", 1),
                  ("b1_1", 32), ("b1_3", 16), ("b1_5", 8)):
    COLS[_name] = (COLS_N, COLS_N + _n)
    COLS_N += _n

WIDE = ("wide0", "wide1")
SMALL = ("small0", "small1")
ACC = ("acc0", "acc1")
BANK = {"wide0": 0, "wide1": 2, "small0": 4, "small1": 5, "acc0": 6, "acc1": 7}


def num_row(h):
    return 32 * (h % 4) + 8 * ((h // 4) % 2) + 16 * (h // 8)


class Slots:

    def __init__(self, made, read):
        self.made, self.read = made, read
        self.uses = dict.fromkeys(BANK, 0)
        self.turn = {}
        self.where = {}

    def take(self, job, kind):
        turn = self.turn.get(kind, 0)
        self.turn[kind] = turn + 1
        slot = kind[turn % len(kind)]
        self.uses[slot] += 1
        self.where[job] = (slot, self.uses[slot])
        return slot

    def before(self, job):
        slot, n = self.where[job]
        return (self.read[slot], n - 1) if n > 1 else None

    def is_made(self, job):
        slot, n = self.where[job]
        return self.made[slot], n

    def is_read(self, job):
        slot, n = self.where[job]
        return self.read[slot], n

    def bank(self, job):
        return BANK[self.where[job][0]]


def build(nc, A, out):
    with ExitStack() as ctx:
        def sb(name, shape, dt=F32):
            return ctx.enter_context(nc.sbuf_tensor("s_" + name, shape, dt))

        def sem(name):
            return ctx.enter_context(nc.semaphore(name))

        PS = ctx.enter_context(nc.psum_tensor("psum_all", [P, 8, 512], F32))

        X = sb("x_resid", [P, NT, P])
        XN = sb("x_normed", [P, NT, P])
        XT = sb("x_turned", [P, NB, SQ])
        consts = sb("consts", [P, CONSTS_N])
        rows = sb("rows", [P, ROWS_N])
        cols = sb("cols", [P, COLS_N])
        ctxT = sb("ctxT", [P, CK])
        ctxN = sb("ctxN", [SK, NB, P])
        wattn = sb("wattn", [P, 3, 4, P])
        arena = sb("arena", [P, 8192])
        w1 = {1: arena[:, 0:4096].rearrange("p (e h) -> p e h", e=16)}
        w2 = {1: arena[:, 4096:8192].rearrange("p (e c d) -> p e c d", e=16, c=2)}
        w1[3] = sb("w1_3", [P, 8, 256])
        w2[3] = sb("w2_3", [P, 8, 2, P])
        w1[5] = sb("w1_5", [P, 8, P])
        w2[5] = sb("w2_5", [P, 8, 1, P])
        w1[7], w3_7, w2[7] = (arena[:, 1152 * j:1152 * j + 1152].rearrange("p (e c) -> p e c", e=GLU_PAIRS)
                              for j in range(3))
        b2 = {1: sb("b2_1", [16, P]), 3: sb("b2_3", [8, P]), 5: sb("b2_5", [8, P])}
        router = sb("router", [P, 16 + 8 + 8 + 16])
        rw = {1: router[:, 0:16], 3: router[:, 16:24], 5: router[:, 24:32], 7: router[:, 32:48]}
        wloc = sb("wloc", [P, 3, P])
        win5 = sb("win5", [P, 4 * P])
        QKV = arena[:, 0:6144].rearrange("p (t s c) -> p t s c", t=NB, s=TPB)
        H5 = sb("h5", [P, NT, P])
        local_ctx = H5[:, :, :].rearrange("p t d -> p (t d)").rearrange("p (b s) -> p b s", b=NB)
        PV5 = [w.rearrange("p (t s c) -> p t s c", t=NB, s=NB) for w in
               (w1[3][:, :, :].rearrange("p e c -> p (e c)"), w2[3][:, :, :, :].rearrange("p e c d -> p (e c d)"))]

        stats = sb("stats", [P, TPB, 6])
        mv = sb("mv", [P, 2, TPB, 2])
        vare = sb("vare", [P, 2, TPB])
        rstd = sb("rstd", [P, 2, TPB])
        mhalf = sb("minus_half", [P, TPB])

        KS1 = sb("ks1", [P, NH, CK], BF16)
        KS2 = sb("ks2", [P, NH, CK], BF16)
        att = sb("att", [P, 6, SQ])
        spare = att[:, :, :].rearrange("p a b -> p (a b)")
        kf, kr = spare[:, 0:CK], spare[:, CK:2 * CK]
        kparts = spare[:, 2 * CK:2 * CK + 3 * CK // 2].bitcast(BF16).rearrange("p (j s) -> p j s", j=3)
        KB = spare[:, 1078:1078 + 3 * HPG * CK // 2].bitcast(BF16).rearrange("p (j h s) -> p j h s", j=3, h=HPG)
        keep = spare[:, 0:CK].rearrange("p (b s) -> p b s", b=NB)
        negm = spare[:, CK:2 * CK].rearrange("p (b s) -> p b s", b=NB)
        Eloc = spare[:, 2 * CK:3 * CK]
        Gc = spare[0:SK, 3 * CK:3 * CK + NB * P].rearrange("p (b d) -> p b d", b=NB)
        m5 = spare[:, 1536:2560].rearrange("p (a b c) -> p a b c", a=2, b=2)
        V2 = sb("v2", [SK, NB, NH, 32])
        tscale = sb("tscale", [P, 4, NB])
        QS = 3
        qf = sb("qf", [P, SQ])
        qr = sb("qr", [P, SQ])
        qparts = sb("qparts", [P, 3, SQ], BF16)
        T1 = sb("t1", [P, QS, NG, SQ], BF16)
        T2 = sb("t2", [P, QS, NG, SQ], BF16)
        nmx = sb("nmx", [P, 2, TPB, NH])
        nmxh = sb("nmxh", [P, TPB, NH], BF16)
        nmx2 = sb("nmx2", [P, 2, TPB, 2 * NH])
        ES = 3
        HS = 3
        hT = sb("hT", [P, HS, 2, SQ])
        Eexp = hT[0:SK, :, :, :]
        gl = hT
        PROD = (arena[:, 6144:8192], hT[:, 0:2, :, :].rearrange("p a b c -> p (a b c)"))
        drow = hT[0:1, 0, :, :].rearrange("p a b -> p (a b)")[:, 0:3 * CK].rearrange("p (j s) -> p j s", j=3)
        dparts = hT[0:1, 1, 0, 0:3 * CK // 2].bitcast(BF16).rearrange("p (j s) -> p j s", j=3)
        LPT = T1[:, 0:2, :, :].rearrange("p a b c -> p (a b c)").bitcast(F32).rearrange("p (b c) -> p b c", b=NB)
        LS = (T2[:, 0:2, :, :].rearrange("p a b c -> p (a b c)").bitcast(F32)[:, 0:NB * TPB * SK]
              .rearrange("p (b i s) -> p b i s", b=NB, i=TPB))
        C = sb("combine", [P, NT, 16])
        cT = sb("cT", [64, 2, SQ])
        cT7 = cT[:, 0, :].bitcast(BF16).rearrange("p (a b) -> p a b", a=2)
        lg = sb("lg", [P, TPB, 16])
        v8 = sb("v8", [P, TPB, 8])
        i8 = sb("i8", [P, TPB, 8], U32)
        if8 = sb("if8", [P, TPB, 8])
        oh = sb("oh", [P, TPB, 4, 16])
        r16 = sb("r16", [P, 4, TPB, 16])
        g8 = sb("g8", [P, TPB, 8])
        r1 = sb("r1", [P, 4, TPB])
        lrow = sb("lrow", [P, 6, NB])
        leni = sb("leni", [P, NB], I32)
        gau = sb("gau", [SK, 3, NB])
        c7h = sb("c7h", [P, 2, TPB, 16], BF16)
        c7 = sb("c7", [P, 2, TPB, 64])
        pick7 = sb("pick7", [64, GLU_PAIRS * P], BF16)

        ident = consts[:, 0:128]

        def const(name, n=P):
            a, b = CONSTS[name]
            return consts[0:n, a:b]

        def row(name, n=P):
            a, b = ROWS[name]
            return rows[0:n, a:b]

        def col(name, j=0):
            a = COLS[name][0] + j
            return cols[:, a:a + 1]

        slots = Slots({s: sem(f"made_{s}") for s in BANK}, {s: sem(f"read_{s}") for s in BANK})
        s_x = [sem(f"x_loaded{b}") for b in range(NB)]
        s_dl = sem("delta_loaded")
        s_kw = sem("context_and_key_weights_loaded")
        s_c = sem("consts_loaded")
        s_rows = sem("rows_loaded")
        s_pick = sem("picks_ready")
        s_tau = sem("scales_ready")
        s_ob = sem("out_bias_added")
        s_w = {k: sem(f"weights_loaded_{k}") for k in ("a", "m1", "m3", "m5", "m7", "loc")}
        s_out = sem("out_written")
        s_stat = sem("mean_var_ready")
        s_vare = sem("var_eps_ready")
        s_rstd = sem("rstd_ready")
        s_xn = sem("normed_ready")
        s_bo = sem("bo_added")
        s_pool0 = sem("pool_consts_ready")
        s_ones = sem("dve_consts_ready")
        s_delta = sem("delta_parts_ready")
        s_drow = sem("delta_rows_placed")
        s_kb = sem("k_blocks_ready")
        s_ks1 = [sem(f"ks1_placed{a}") for a in range(3)]
        s_ks = [sem(f"ks2_placed{a}") for a in range(3)]
        s_v2 = sem("v2_ready")
        s_q3 = sem("q_parts_ready")
        s_t1 = [sem(f"t1_placed{u}") for u in range(12)]
        s_t2 = [sem(f"t2_placed{u}") for u in range(12)]
        s_nmx = sem("max_ready")
        s_prod = sem("att_out_ready")
        s_lr = sem("logits_ready")
        s_le = sem("logit_exps_ready")
        s_cw = sem("combine_ready")
        s_sil = sem("silu_ready")
        s_lg = sem("gauss_arg_ready")
        s_ge = sem("gauss_ready")
        s_gc = sem("gauss_context_ready")
        s_ls = sem("local_scores_ready")
        s_lx = sem("local_exps_ready")
        s_lp = sem("local_probs_ready")
        s_p5 = sem("qk_products_ready")
        s_s5 = sem("mha_shifted_ready")
        s_e5 = sem("mha_exps_ready")
        s_pr5 = sem("mha_probs_ready")
        s_pv5 = sem("mha_pool_values_ready")
        s_c5 = sem("mha_values_ready")
        s_av5 = sem("mha_values_summed")
        s_h5 = sem("h_ready")
        s_pin = sem("qkv_ready")
        s_dve = [sem(f"dve_chain{i}") for i in range(NL + 1)]
        s_pv = sem("values_summed")
        s_yglu = sem("glu_summed")

        units = [(L, b) for L in range(NL) for b in range(NB)]
        attn_units = [(L, b) for L, b in units if LAYERS[L] == ATTN]
        n_attn = {u: i for i, u in enumerate(attn_units)}
        moe_units = [(L, b) for L, b in units if LAYERS[L] in (MOE, MHA, GLU)]
        n_moe = {u: i for i, u in enumerate(moe_units)}
        exp_units = [u for u in moe_units if LAYERS[u[0]] == MOE]
        n_exp = {u: i for i, u in enumerate(exp_units)}
        def steps_of(L):
            return PAIRS if LAYERS[L] == ATTN else GLU_PAIRS if LAYERS[L] == GLU else EXPERTS[L]

        def following(u):
            L, b = u
            if b < NB - 1:
                return (L, b + 1)
            return (L + 1, 0) if L + 1 < NL and LAYERS[L + 1] not in (LOCAL, MHA) else None

        def ahead(u, n):
            L, b = u
            v = (L, b + n) if b + n < NB else (L + 1, b + n - NB)
            return v if v[0] < NL and LAYERS[v[0]] == ATTN else None

        def plan(u, engine):
            L, b = u
            todo = []
            v = following(u)
            if v:
                todo += [(stage, *v) for stage in (("M0", "M1", "M2", "M3", "MT") if LAYERS[v[0]] == ATTN
                                                   else ("front", "R", "CT") if LAYERS[v[0]] == MHA
                                                   else ("stats", "norm", "front", "R", "CT"))]
            v = ahead(u, 2)
            if v:
                todo += [(stage, *v) for stage in ("front", "Q")]
            v = ahead(u, 3)
            if v:
                todo += [("stats", *v), ("norm", *v)]
            if L + 1 < NL and LAYERS[L + 1] == LOCAL and b:
                todo += [("stats", L + 1, b - 1), ("norm", L + 1, b - 1), ("front", L + 1, b - 1)]
                for c in {2: (0,), 3: (1, 2)}.get(b, ()):
                    todo += [(stage + str(c), L + 1, c) for stage in ("LS", "LN", "LT")]
                if b == 3:
                    todo += [(stage + str(c), L + 1, c) for c in range(LOCAL_EARLY) for stage in ("LC", "LO")]
                if b == 2:
                    todo += [("LE", L + 1, 0)]
            which = ("pe", "dve", "act").index(engine)
            todo = [(PLACES[L][x[0] + "+" * (x[0] in ("stats", "norm", "front") and LAYERS[x[1]] == ATTN)][which], *x)
                    for x in todo]
            todo.sort(key=lambda x: x[0])
            return todo

        BEFORE = ([(stage, 0, 0) for stage in ("keys", "stats", "norm", "front", "values", "Q", "M0", "M1")]
                  + [("stats", 0, 1)] + [(stage, 0, 0) for stage in ("M2", "M3", "MT")]
                  + [(stage, 0, 1) for stage in ("norm", "front", "Q")] + [("stats", 0, 2), ("norm", 0, 2)])

        norms = [("in", L, b) for stage, L, b in BEFORE if stage == "stats"]
        for L, b in units:
            if LAYERS[L] == LOCAL:
                if b == 0:
                    norms += [("in", L, NB - 1)]
                continue
            if LAYERS[L] == MHA and b == 0:
                norms += [("in", L, c) for c in range(NB)] + [("ln1", L, c) for c in range(NB)]
            norms += [("in", *v) for _, stage, *v in plan((L, b), "dve")
                      if stage == "stats"]
            if LAYERS[L] == MHA:
                norms.append(("ln2", L, b))
        n_in = {x[1:]: i + 1 for i, x in enumerate(x for x in norms if x[0] == "in")}

        def values_summed(eng, n):
            u, p = divmod(n, PAIRS)
            g = p // 2
            if g % 2:
                eng.wait_ge(*slots.is_made(("PV", *attn_units[u], g // 2)))
            else:
                eng.wait_ge(s_pv, 2 * u + g // 2 + 1)

        def glu_summed(eng, n):
            b, p = divmod(n, GLU_PAIRS)
            if p < GLU_PAIRS - 1:
                eng.wait_ge(s_yglu, (GLU_PAIRS - 1) * b + p + 1)
            else:
                eng.wait_ge(*slots.is_made(("Y", 7, b)))

        block = ctx.enter_context(nc.Block())

        @block.tensor
        def _(pe):
            def start(job, kind):
                slots.take(job, kind)
                w = slots.before(job)
                if w:
                    pe.wait_ge(*w)
                return slots.bank(job)

            def finish(job, ins):
                ins.then_inc(slots.is_made(job)[0], 1)

            def have(job):
                pe.wait_ge(*slots.is_read(job))

            def turn(job, src, ready, value):
                pe.wait_ge(ready, value)
                k = start(job, SMALL)
                for i in range(TPB):
                    mm = pe.transpose(PS[:, k, 128 * i:128 * i + 128], src[:, i, :], ident)
                finish(job, mm)

            def front(L, b):
                turn(("T", L, b), XN[:, TPB * b:TPB * b + TPB, :], s_xn, n_in[L, b])

            def keys(a):
                if a:
                    pe.wait_ge(s_w["a"], 16 * 3)
                else:
                    pe.wait_ge(s_kw, 16 * 2)
                k = start(("K", a), SMALL)
                finish(("K", a), pe.matmul(PS[:, k, 0:CK], wattn[:, a, 1, :], ctxT[:, :], start=True, stop=True))

            def values(a):
                k = start(("V", a), SMALL)
                for b in range(NB):
                    mm = pe.matmul(PS[0:SK, k, 128 * b:128 * b + 128], ctxT[:, SK * b:SK * b + SK],
                                   wattn[:, a, 2, :], start=True, stop=True)
                finish(("V", a), mm)

            def k_prep(a):
                keys(a)
                values(a)

            def project_q(L, b):
                have(("T", L, b))
                k = start(("Q", L, b), SMALL)
                finish(("Q", L, b), pe.matmul(PS[:, k, :], wattn[:, ATTN_NO[L], 0, :], XT[:, b, :],
                                              start=True, stop=True))

            def max_scores(L, b, i, groups=range(NG)):
                u = n_attn[L, b]
                if i == 0 and groups[0] == 0:
                    pe.wait_ge(s_t1[u], 16 * 12)
                    pe.wait_ge(s_ks1[ATTN_NO[L]], 16 * 12)
                    pe.wait_ge(s_drow, 16 * 3)
                    pe.wait_ge(s_pool0, 4)
                for g in groups:
                    k = start(("M", L, b, i, g), SMALL)
                    o = PS[:, k, 0:HPG * SK].rearrange("p (h s) -> p h s", h=HPG)
                    finish(("M", L, b, i, g),
                           pe.matmul(o, T1[:, u % QS, g, 128 * i:128 * i + 128],
                                     KS1[:, HPG * g:HPG * g + HPG, SK * b:SK * b + SK], start=True, stop=True))

            def turn_max(L, b):
                u = n_attn[L, b]
                pe.wait_ge(s_nmx, u + 1)
                k = start(("MT", L, b), SMALL)
                for i in range(TPB):
                    mm = pe.transpose(PS[0:2 * NH, k, 128 * i:128 * i + 128], nmx2[:, u % 2, i, :], ident)
                finish(("MT", L, b), mm)

            def attn_unit(L, b, hook):
                u = n_attn[L, b]

                def scores(p):
                    k = start(("S", L, b, p), WIDE)
                    for y in range(2):
                        h = 2 * p + y
                        keys = slice(SK * b, SK * b + SK)
                        pe.matmul(PS[0:SK, k + y, :], KS1[:, h, keys], T1[:, u % QS, h // HPG, :],
                                  start=True, stop=False)
                        mm = pe.matmul(PS[0:SK, k + y, :], KS2[:, h, keys], T2[:, u % QS, h // HPG, :],
                                       start=False, stop=True)
                    finish(("S", L, b, p), mm)

                have(("MT", L, b))
                pe.wait_ge(s_t2[u], 16 * 12)
                pe.wait_ge(s_ks[ATTN_NO[L]], 16 * 12)
                pe.wait_ge(s_pick, 1)
                pe.wait_ge(s_v2, ATTN_NO[L] + 1)
                scores(0)
                scores(1)
                for p in range(PAIRS):
                    if p % 2:
                        g = p // 2
                        if g % 2 == 0:
                            k = start(("PV", L, b, g // 2), ACC)
                        have(("S", L, b, p - 1))
                        have(("S", L, b, p))
                        for j in range(HPG):
                            mm = pe.matmul(PS[32 * j:32 * j + 32, k, :], V2[:, b, HPG * g + j, :],
                                           Eexp[:, (PAIRS * u + p - 1 + j // 2) % ES, j % 2, :],
                                           start=(g % 2 == 0), stop=(g % 2 == 1))
                        if g % 2:
                            finish(("PV", L, b, g // 2), mm)
                        else:
                            mm.then_inc(s_pv, 1)
                    hook(p, early=True)
                    if p + 2 < PAIRS:
                        scores(p + 2)
                    hook(p)

            def attn_out(L, b):
                pe.wait_ge(s_prod, n_attn[L, b] + 1)
                k = start(("O", L, b), SMALL)
                for i in range(TPB):
                    mm = pe.matmul(PS[:, k, 128 * i:128 * i + 128], att[:, 5, 128 * i:128 * i + 128],
                                   wattn[:, ATTN_NO[L], 3, :], start=True, stop=True)
                finish(("O", L, b), mm)

            def route(L, b):
                have(("T2" if LAYERS[L] == MHA else "T", L, b))
                if (L, b) == (1, 0):
                    pe.wait_ge(s_w["a"], 16 * 3)
                k = start(("R", L, b), SMALL)
                for i in range(TPB):
                    mm = pe.matmul(PS[:, k, 16 * i:16 * i + EXPERTS[L]], XT[:, b, 128 * i:128 * i + 128], rw[L],
                                   start=True, stop=True)
                finish(("R", L, b), mm)

            def turn_combine(L, b):
                n = n_moe[L, b]
                pe.wait_ge(s_cw, n + 1)
                k = start(("CT", L, b), SMALL)
                for i in range(TPB):
                    if LAYERS[L] == GLU:
                        mm = pe.transpose(PS[0:64, k, 128 * i:128 * i + 128], c7[:, b % 2, i, :], ident)
                    else:
                        mm = pe.transpose(PS[0:EXPERTS[L], k, 128 * i:128 * i + 128],
                                          C[:, TPB * b + i, 0:EXPERTS[L]], ident)
                finish(("CT", L, b), mm)

            def moe_unit(L, b, hook):
                E, NC = EXPERTS[L], HIDDEN_CHUNKS[L]
                pe.wait_ge(s_w[f"m{L}"], 16 * 3)

                def hidden(e):
                    k = start(("H", L, b, e), WIDE)
                    for c in range(NC):
                        mm = pe.matmul(PS[:, k + c, :], w1[L][:, e, 128 * c:128 * c + 128], XT[:, b, :],
                                       start=True, stop=True)
                    finish(("H", L, b, e), mm)

                hidden(0)
                have(("CT", L, b))
                k = start(("B2", L, b), ACC)
                for i in range(TPB):
                    mm = pe.matmul(PS[:, k, 128 * i:128 * i + 128], cT[0:E, b % 2, 128 * i:128 * i + 128],
                                   b2[L][:, :], start=True, stop=True)
                finish(("B2", L, b), mm)
                for e in range(E):
                    if e + 1 < E:
                        hidden(e + 1)
                    k = start(("Y", L, b, e), ACC)
                    have(("H", L, b, e))
                    hs = (E * b + e) % HS
                    for i in range(TPB):
                        for c in range(NC):
                            mm = pe.matmul(PS[:, k, 128 * i:128 * i + 128],
                                           hT[:, hs, c, 128 * i:128 * i + 128],
                                           w2[L][:, e, c, :], start=(c == 0), stop=(c == NC - 1))
                    finish(("Y", L, b, e), mm)
                    hook(e)

            def glu_unit(L, b, hook):
                pe.wait_ge(s_w["m7"], 16 * 3)
                pe.wait_ge(s_pick, 2)

                def hidden(p):
                    k = start(("H", L, b, p), WIDE)
                    pe.matmul(PS[:, k, :], w1[7][:, p, :], XT[:, b, :], start=True, stop=True)
                    finish(("H", L, b, p),
                           pe.matmul(PS[:, k + 1, :], w3_7[:, p, :], XT[:, b, :], start=True, stop=True))
                    have(("CT", L, b))
                    k = start(("CB", L, b, p), SMALL)
                    finish(("CB", L, b, p), pe.matmul(PS[:, k, :], pick7[:, 128 * p:128 * p + 128],
                                                      cT7[:, b % 2, :], start=True, stop=True))

                hidden(0)
                hidden(1)
                for p in range(GLU_PAIRS):
                    if p + 2 < GLU_PAIRS:
                        hidden(p + 2)
                    if p == 0:
                        k = start(("Y", L, b), ACC)
                    have(("CB", L, b, p))
                    for i in range(TPB):
                        mm = pe.matmul(PS[:, k, 128 * i:128 * i + 128], gl[:, (GLU_PAIRS * b + p) % 3, 1, 128 * i:128 * i + 128],
                                       w2[7][:, p, :], start=(p == 0 and i == 0), stop=(p == GLU_PAIRS - 1),
                                       skip_group_check=True)
                    if p == GLU_PAIRS - 1:
                        finish(("Y", L, b), mm)
                    else:
                        mm.then_inc(s_yglu, 1)
                    hook(p)

            def turn_context():
                pe.wait_ge(s_w["loc"], 16 * 2)
                pe.wait_ge(s_lg, 1)
                k = start(("E4",), SMALL)
                finish(("E4",), pe.matmul(PS[:, k, 0:CK], wloc[:, 0, :], ctxT[:, :], start=True, stop=True))

            def local_scores(L, b):
                have(("T", L, b))
                have(("E4",))
                k = start(("LS", b), SMALL)
                for i in range(TPB):
                    mm = pe.matmul(PS[:, k, SK * i:SK * i + SK], XT[:, b, 128 * i:128 * i + 128],
                                   Eloc[:, SK * b:SK * b + SK], start=True, stop=True)
                finish(("LS", b), mm)

            def turn_local(L, b):
                pe.wait_ge(s_lp, b + 1)
                k = start(("LT", b), SMALL)
                for i in range(TPB):
                    mm = pe.transpose(PS[0:SK, k, 128 * i:128 * i + 128], LS[:, b, i, :], ident)
                finish(("LT", b), mm)

            def local_context(L, b):
                pe.wait_ge(s_gc, 1)
                have(("LT", b))
                k = start(("LC", b), SMALL)
                finish(("LC", b), pe.matmul(PS[:, k, :], Gc[:, b, :], LPT[0:SK, b, :], start=True, stop=True))

            def local_out(L, b):
                have(("LC", b))
                k = start(("LO", b), SMALL)
                for i in range(TPB):
                    o = PS[:, k, 128 * i:128 * i + 128]
                    pe.matmul(o, local_ctx[:, b, 128 * i:128 * i + 128], wloc[:, 1, :], start=True, stop=False)
                    mm = pe.matmul(o, XT[:, b, 128 * i:128 * i + 128], wloc[:, 2, :], start=False, stop=True)
                finish(("LO", b), mm)

            def local_layer(L):
                front(L, NB - 1)
                local_scores(L, NB - 1)
                for b in range(LOCAL_EARLY):
                    front(L + 1, b)
                turn_local(L, NB - 1)
                for b in range(LOCAL_EARLY, NB):
                    local_context(L, b)
                for b in range(LOCAL_EARLY, NB):
                    local_out(L, b)
                for b in range(LOCAL_EARLY, NB):
                    front(L + 1, b)

            def mha_layer(L):
                pe.wait_ge(s_w["m5"], 16 * 3)
                for b in range(NB):
                    have(("T", L, b))
                for i in range(TPB):
                    for b in range(NB):
                        k = start(("QKV", b, i), SMALL)
                        finish(("QKV", b, i), pe.matmul(PS[:, k, 0:3 * P], XT[:, b, 128 * i:128 * i + 128],
                                                        win5[:, 0:3 * P], start=True, stop=True))
                ks = [start(("AT", c), WIDE) for c in range(2)]
                for j in range(TPB):
                    pe.wait_ge(s_c5, j + 1)
                    pe.wait_ge(s_pv5, j + 1)
                    for t in range(NB):
                        for s in range(NB):
                            mm = pe.matmul(PS[:, ks[t // 2] + t % 2, 128 * j:128 * j + 128], PV5[j % 2][:, t, s, :], ident,
                                           start=(s == 0), stop=(s == NB - 1))
                        if j == TPB - 1 and t % 2:
                            finish(("AT", t // 2), mm)
                    if j < TPB - 1:
                        mm.then_inc(s_av5, 1)
                for b in range(NB):
                    have(("AT", b // 2))
                    k = start(("AO", b), SMALL)
                    for i in range(TPB):
                        mm = pe.matmul(PS[:, k, 128 * i:128 * i + 128],
                                       hT[:, b % HS, b // HS, 128 * i:128 * i + 128],
                                       win5[:, 3 * P:4 * P], start=True, stop=True)
                    finish(("AO", b), mm)
                    if b == NB - 2:
                        mha_front(L, 0)
                route(L, 0)
                turn_combine(L, 0)

            def mha_front(L, b):
                turn(("T2", L, b), H5[:, TPB * b:TPB * b + TPB, :], s_h5, b + 1)

            def stage_of(stage, L, b):
                if stage in ("stats", "norm"):
                    pass
                elif stage == "keys":
                    pe.wait_ge(s_c, 16 * 2)
                    keys(0)
                elif stage == "values":
                    values(0)
                elif stage[0] == "L":
                    {"E": lambda L, b: turn_context(), "S": local_scores, "N": lambda L, b: None,
                     "T": turn_local, "C": local_context, "O": local_out}[stage[1]](L, b)
                elif stage == "front":
                    (mha_front if LAYERS[L] == MHA else front)(L, b)
                elif stage == "Q":
                    project_q(L, b)
                elif stage == "MT":
                    turn_max(L, b)
                elif stage == "R":
                    route(L, b)
                elif stage == "CT":
                    turn_combine(L, b)
                else:
                    max_scores(L, b, int(stage[1]))

            for x in BEFORE:
                stage_of(*x)
            for n, (L, b) in enumerate(units):
                if LAYERS[L] == LOCAL:
                    if b == 0:
                        local_layer(L)
                    continue
                if LAYERS[L] == MHA and b == 0:
                    mha_layer(L)
                todo = plan((L, b), "pe")
                prev = units[n - 1] if n and LAYERS[units[n - 1][0]] == ATTN else None

                def hook(step, early=False):
                    for at, stage, *v in todo:
                        if at != step:
                            continue
                        if LAYERS[L] == ATTN and stage[0] == "M" and stage != "MT":
                            max_scores(*v, int(stage[1]), range(NG // 2) if early else range(NG // 2, NG))
                        elif not early:
                            stage_of(stage, *v)
                    if early:
                        return
                    if prev and step == EPILOGUE[L][1]:
                        attn_out(*prev)
                    if step == 3 and (L, b) == (1, 2):
                        k_prep(1)
                    if step == 1 and (L, b) == (3, 1):
                        k_prep(2)

                {ATTN: attn_unit, MOE: moe_unit, MHA: moe_unit, GLU: glu_unit}[LAYERS[L]](L, b, hook)

        @block.vector
        def _(dve):
            count = [0] * (NL + 1)
            stage = [0]
            routing = []

            def link(ins):
                j = stage[0]
                count[j] += 1
                ins.then_inc(s_dve[j], 1)
                dve.wait_ge(s_dve[j], count[j])

            def made(job):
                dve.wait_ge(*slots.is_made(job))
                return slots.bank(job)

            def read(job, ins):
                ins.then_inc(slots.is_read(job)[0], 1)

            def settled(job):
                dve.wait_ge(*slots.is_read(job))

            def norm_stats(which, L, b, src):
                n = norms.index((which, L, b))
                if n >= 1:
                    dve.wait_ge(s_stat, n)
                for i in range(TPB):
                    ins = dve.bn_stats(stats[:, i, :], src[:, i, :])
                link(ins)
                for i in range(TPB):
                    ins = dve.bn_aggr(mv[:, n % 2, i, :], stats[:, i, :])
                ins.then_inc(s_stat, 1)

            def norm_apply(which, L, b, src, dst):
                n = norms.index((which, L, b))
                dve.wait_ge(s_stat, n + 1)
                dve.wait_ge(s_rstd, n + 1)
                for i in range(TPB):
                    ins = dve.tensor_scalar(dst[:, i, :], src[:, i, :], mv[:, n % 2, i, 0:1], rstd[:, n % 2, i:i + 1],
                                            ALU.subtract, ALU.mult)
                if which == "in":
                    ins.then_inc(s_xn, 1)
                else:
                    link(ins)

            def tiles(t, b):
                return t[:, TPB * b:TPB * b + TPB, :]

            def front_stats(L, b):
                if L == 0:
                    dve.wait_ge(s_x[b], 16)
                norm_stats("in", L, b, tiles(X, b))

            def front_apply(L, b):
                norm_apply("in", L, b, tiles(X, b), tiles(XN, b))

            def front(L, b):
                front_stats(L, b)
                front_apply(L, b)

            def delta_parts():
                link(dve.tensor_scalar(drow[:, 1, :], drow[:, 0, :], ATT_SCALE, None, ALU.mult))
                link(dve.tensor_copy(dparts[:, 0, :], drow[:, 1, :]))
                link(dve.tensor_tensor(drow[:, 2, :], drow[:, 1, :], dparts[:, 0, :], ALU.subtract))
                link(dve.tensor_copy(dparts[:, 1, :], drow[:, 2, :]))
                dve.tensor_tensor(dparts[:, 2, :], drow[:, 2, :], dparts[:, 1, :], ALU.subtract).then_inc(s_delta, 1)

            def keys(a):
                k = made(("K", a))
                read(("K", a), dve.tensor_scalar(kf[:, :], PS[:, k, 0:CK], col(f"bk{a}"), None, ALU.add))
                settled(("K", a))
                link(dve.tensor_copy(kparts[:, 0, :], kf[:, :]))
                link(dve.tensor_tensor(kr[:, :], kf[:, :], kparts[:, 0, :], ALU.subtract))
                link(dve.tensor_copy(kparts[:, 1, :], kr[:, :]))
                link(dve.tensor_tensor(kparts[:, 2, :], kr[:, :], kparts[:, 1, :], ALU.subtract))
                if a:
                    dve.wait_ge(s_ks1[a - 1], 16 * 12)
                    dve.wait_ge(s_ks[a - 1], 16 * 12)
                mask = const("head_mask")
                for j in range(3):
                    for h in range(HPG):
                        ins = dve.tensor_scalar(KB[:, j, h, :], kparts[:, j, :], mask[:, h:h + 1], None, ALU.mult)
                ins.then_inc(s_kb, 1)

            def values(a):
                k = made(("V", a))
                dve.wait_ge(s_pool0, 3)
                v = PS[0:SK, k, :].rearrange("s (b h d) -> s b h d", b=NB, h=NH)
                bias = row(f"bv{a}", SK).rearrange("s (h d) -> s h d", h=NH)
                for half in range(2):
                    for sub in range(2):
                        hs = slice(8 * half + 4 * sub, 8 * half + 4 * sub + 4)
                        c0 = 16 * half + 8 * sub
                        for b in range(NB):
                            ins = dve.tensor_tensor(V2[:, b, hs, c0:c0 + DK], v[:, b, hs, :], bias[:, hs, :], ALU.add)
                read(("V", a), ins)
                settled(("V", a))
                dve.engine_nop().then_inc(s_v2, 1)

            def k_prep(a):
                keys(a)
                values(a)

            def split_q(L, b):
                u = n_attn[L, b]
                q = qparts
                settled(("Q", L, b))
                if u:
                    dve.wait_ge(s_q3, u)
                    dve.wait_ge(s_t1[u - 1], 16 * 12)
                    dve.wait_ge(s_t2[u - 1], 16 * 12)
                link(dve.tensor_tensor(qr[:, :], qf[:, :], q[:, 0, :], ALU.subtract))
                link(dve.tensor_copy(q[:, 1, :], qr[:, :]))
                dve.tensor_tensor(q[:, 2, :], qr[:, :], q[:, 1, :], ALU.subtract).then_inc(s_q3, 1)

            def max_scores(L, b, i):
                u = n_attn[L, b]
                if u >= 1 and i == 0:
                    dve.wait_ge(s_nmx, u)
                for g in range(NG):
                    job = ("M", L, b, i, g)
                    k = made(job)
                    read(job, dve.tensor_reduce(nmx[:, u % 2, i, HPG * g:HPG * g + HPG],
                                                PS[:, k, 0:HPG * SK].rearrange("p (h s) -> p h s", h=HPG),
                                                AX.X, ALU.max, negate=True))

            def max_parts(L, b):
                u = n_attn[L, b]
                settled(("M", L, b, TPB - 1, NG - 2))
                settled(("M", L, b, TPB - 1, NG - 1))
                m = nmx[:, u % 2, :, :]
                link(dve.tensor_copy(nmxh[:, :, :], m))
                dve.tensor_copy(nmx2[:, u % 2, :, 0:NH], nmxh[:, :, :])
                dve.tensor_tensor(nmx2[:, u % 2, :, NH:2 * NH], m, nmxh[:, :, :], ALU.subtract).then_inc(s_nmx, 1)

            def join_heads(L, b):
                u = n_attn[L, b]
                low, high = const("low_rows"), const("high_rows")
                jb = ("PV", L, b, 1)
                settled(("PV", L, b, 0))
                k = made(jb)
                dve.scalar_tensor_tensor(att[:, 2, :], PS[:, k, :], low, att[:, 0, :], ALU.mult, ALU.add)
                read(jb, dve.scalar_tensor_tensor(att[:, 3, :], PS[:, k, :], high, att[:, 1, :], ALU.mult, ALU.add))

            def divide_heads(L, b):
                u = n_attn[L, b]
                settled(("PV", L, b, 1))
                link(dve.reciprocal(att[:, 4, :], att[:, 2, :]))
                link(dve.stream_shuffle(att[:, 2, :], att[:, 4, :], [(i + 16) % 32 for i in range(32)]))
                dve.tensor_tensor(att[:, 5, :], att[:, 3, :], att[:, 2, :], ALU.mult).then_inc(s_prod, 1)

            def add_out(L, b):
                k = made(("O", L, b))
                dve.wait_ge(s_bo, n_attn[L, b] + 1)
                x = tiles(X, b)
                read(("O", L, b), dve.tensor_tensor(x, PS[:, k, :].rearrange("p (i d) -> p i d", i=TPB), x, ALU.add))
                settled(("O", L, b))

            def spread(ap, n):
                return ap.unsqueeze(len(ap.shape)).to_broadcast(list(ap.shape) + [n])

            def over(ap, n):
                return ap.unsqueeze(1).to_broadcast([ap.shape[0], n] + list(ap.shape[1:]))

            def top(values, n=16):
                for i in range(TPB):
                    ins = dve.max(v8[:, i, :], values[:, i, 0:n])
                link(ins)
                for i in range(TPB):
                    ins = dve.max_index(i8[:, i, :], v8[:, i, :], values[:, i, 0:n])
                link(ins)
                link(dve.tensor_copy(if8[:, :, :], i8[:, :, :]))

            def chosen(dst, K, n):
                io = const("iota16")[:, 0:n]
                for i in range(TPB):
                    ins = dve.tensor_tensor(oh[:, i, 0:K, 0:n], over(io, K), spread(if8[:, i, 0:K], n), ALU.is_equal)
                link(ins)
                for i in range(TPB):
                    ins = dve.tensor_reduce(dst[:, i, :], oh[:, i, 0:K, 0:n].rearrange("p k e -> p e k"), AX.X, ALU.add)
                link(ins)

            def logits_of(L, b):
                k = made(("R", L, b))
                E = EXPERTS[L]
                z = PS[:, k, 0:16 * TPB].rearrange("p (i e) -> p i e", i=TPB)[:, :, 0:E]
                read(("R", L, b), dve.tensor_tensor(lg[:, :, 0:E], z, over(row(f"rb{L}"), TPB), ALU.add))
                settled(("R", L, b))
                return lg[:, :, 0:E]

            def route_moe(L, b):
                E = EXPERTS[L]
                n = n_moe[L, b]
                if n:
                    dve.wait_ge(s_cw, n)
                z = logits_of(L, b)
                top(z, E)
                w = r16[:, 0, :, 0:E]
                x = n_exp[L, b]
                dve.tensor_tensor(w, z, spread(v8[:, :, 0], E), ALU.subtract).then_inc(s_lr, 1)
                yield
                mask = r16[:, 1, :, 0:E]
                chosen(mask, 4 if L == 1 else 1, E)
                yield
                dve.wait_ge(s_le, x + 1)
                ex = r16[:, 2, :, 0:E]
                em = r16[:, 3, :, 0:E]
                link(dve.tensor_tensor(em, ex, mask, ALU.mult))
                link(dve.tensor_reduce(r1[:, 0, :], em if L == 1 else ex, AX.X, ALU.add))
                link(dve.reciprocal(r1[:, 1, :], r1[:, 0, :]))
                dve.tensor_tensor(tiles(C, b)[:, :, 0:E], em, spread(r1[:, 1, :], E), ALU.mult).then_inc(s_cw, 1)
                dve.wait_ge(s_cw, n + 1)

            def route_mha(L, b):
                E = EXPERTS[L]
                n = n_moe[L, b]
                z = logits_of(L, b)
                top(z, E)
                yield
                link(dve.tensor_tensor(r1[:, 2, :], if8[:, :, 0], if8[:, :, 1], ALU.max))
                dve.tensor_tensor(tiles(C, b)[:, :, 0:E], over(const("iota16")[:, 0:E], TPB), spread(r1[:, 2, :], E),
                                  ALU.is_equal).then_inc(s_cw, 1)
                dve.wait_ge(s_cw, n + 1)

            def route_glu(L, b):
                n = n_moe[L, b]
                dve.wait_ge(s_cw, n)
                dve.wait_ge(*slots.is_read(("R", L, b)))
                sig, s = r16[:, 0, :, :], r16[:, 1, :, :]
                link(dve.tensor_tensor(s, sig, over(row("rb7"), TPB), ALU.add))
                link(dve.tensor_reduce(g8[:, :, 0:4], s.rearrange("p i (g e) -> p i g e", g=4), AX.X, ALU.max))
                top(g8, 8)
                yield
                kg = r16[:, 2, :, 0:4]
                chosen(kg, 2, 4)
                kb = r16[:, 2, :, 4:8]
                link(dve.tensor_scalar(kb, kg, BIG, BIG, ALU.mult, ALU.subtract))
                sm = r16[:, 3, :, :]
                for i in range(TPB):
                    ins = dve.tensor_tensor(sm[:, i, :].rearrange("p (g e) -> p g e", g=4),
                                            s[:, i, :].rearrange("p (g e) -> p g e", g=4), spread(kg[:, i, :], 4), ALU.mult)
                link(ins)
                for i in range(TPB):
                    v = sm[:, i, :].rearrange("p (g e) -> p g e", g=4)
                    ins = dve.tensor_tensor(v, v, spread(kb[:, i, :], 4), ALU.add)
                link(ins)
                yield
                top(sm)
                yield
                mask = r16[:, 2, :, :]
                chosen(mask, 4, 16)
                c = tiles(C, b)
                link(dve.tensor_tensor(c, sig, mask, ALU.mult))
                d = c7[:, b % 2, :, :]
                link(dve.tensor_copy(c7h[:, 0, :, :], c))
                dve.tensor_copy(d[:, :, 0:16], c7h[:, 0, :, :])
                link(dve.tensor_tensor(lg[:, :, :], c, c7h[:, 0, :, :], ALU.subtract))
                link(dve.tensor_copy(c7h[:, 1, :, :], lg[:, :, :]))
                dve.tensor_copy(d[:, :, 16:32], c7h[:, 1, :, :])
                dve.tensor_tensor(d[:, :, 32:48], lg[:, :, :], c7h[:, 1, :, :], ALU.subtract).then_inc(s_cw, 1)
                dve.wait_ge(s_cw, n + 1)

            def moe_unit(L, b, hook):
                dst = H5 if L == 5 else X
                E = EXPERTS[L]
                k = made(("B2", L, b))
                d = tiles(dst, b)
                read(("B2", L, b), dve.tensor_tensor(d, PS[:, k, :].rearrange("p (i d) -> p i d", i=TPB), d, ALU.add))
                last = ("B2", L, b)
                for e in range(E):
                    k = made(("Y", L, b, e))
                    settled(last)
                    for i in range(TPB):
                        t = TPB * b + i
                        ins = dve.scalar_tensor_tensor(dst[:, t, :], PS[:, k, 128 * i:128 * i + 128],
                                                       C[:, t, e:e + 1], dst[:, t, :], ALU.mult, ALU.add)
                    last = ("Y", L, b, e)
                    read(last, ins)
                    hook(e)
                settled(last)
                if L == 5:
                    y = tiles(XN, b)
                    norm_stats("ln2", L, b, d)
                    norm_apply("ln2", L, b, d, y)
                    g, s = over(row("ln2_g"), TPB), over(row("ln2_b"), TPB)
                    link(dve.tensor_tensor(y, y, g, ALU.mult))
                    link(dve.tensor_tensor(y, y, s, ALU.add))
                    link(dve.tensor_tensor(tiles(X, b), tiles(X, b), y, ALU.add))

            def glu_unit(L, b, hook):
                for p in range(GLU_PAIRS):
                    x = (GLU_PAIRS * b + p) % 3
                    n = GLU_PAIRS * b + p
                    dve.wait_ge(s_sil, n + 1)
                    k = made(("H", L, b, p))
                    read(("H", L, b, p), dve.tensor_tensor(gl[:, x, 0, :], PS[:, k + 1, :], gl[:, x, 0, :], ALU.mult))
                    settled(("H", L, b, p))
                    k = made(("CB", L, b, p))
                    if n >= 3:
                        glu_summed(dve, n - 3)
                    read(("CB", L, b, p), dve.tensor_tensor(gl[:, x, 1, :], PS[:, k, :], gl[:, x, 0, :], ALU.mult))
                    hook(p)
                k = made(("Y", L, b))
                x = tiles(X, b)
                read(("Y", L, b), dve.tensor_tensor(x, PS[:, k, :].rearrange("p (i d) -> p i d", i=TPB), x, ALU.add))

            def window_prep():
                pt = row("pt")
                st, en, lf = lrow[:, 0, :], lrow[:, 1, :], lrow[:, 2, :]
                dve.wait_ge(s_ks1[2], 16 * 12)
                dve.wait_ge(s_ks[2], 16 * 12)
                link(dve.tensor_copy(lf, leni[:, :]))
                link(dve.tensor_scalar(st, pt, WINDOW, 0.0, ALU.subtract, ALU.max))
                link(dve.tensor_scalar(lrow[:, 3, :], pt, WINDOW, None, ALU.add))
                link(dve.tensor_tensor(en, lrow[:, 3, :], lf, ALU.min))
                io = const("iota77")
                for b in range(NB):
                    ins = dve.tensor_scalar(negm[:, b, :], io, st[:, b:b + 1], None, ALU.is_ge)
                link(ins)
                for b in range(NB):
                    ins = dve.scalar_tensor_tensor(keep[:, b, :], io, en[:, b:b + 1], negm[:, b, :], ALU.is_le, ALU.mult)
                link(ins)
                link(dve.tensor_scalar(negm[:, :, :], keep[:, :, :], MASKED, MASKED, ALU.mult, ALU.subtract))
                link(dve.tensor_scalar(gau[:, 0, :], row("pt", SK), const("iota_col", SK), None, ALU.subtract))
                dve.tensor_tensor(gau[:, 1, :], gau[:, 0, :], gau[:, 0, :], ALU.mult).then_inc(s_lg, 1)

            def gauss_context():
                dve.wait_ge(s_ge, 1)
                for b in range(NB):
                    ins = dve.tensor_scalar(Gc[:, b, :], ctxN[:, b, :], gau[:, 2, b:b + 1], None, ALU.mult)
                ins.then_inc(s_gc, 1)

            def local_scores(L, b):
                k = made(("LS", b))
                s = LS[:, b, :, :]
                read(("LS", b), dve.tensor_tensor(s, PS[:, k, 0:TPB * SK].rearrange("p (i s) -> p i s", i=TPB),
                                                  over(keep[:, b, :], TPB), ALU.mult))
                settled(("LS", b))
                link(dve.tensor_tensor(s, s, over(negm[:, b, :], TPB), ALU.add))
                link(dve.tensor_reduce(r1[:, 0, :], s, AX.X, ALU.max))
                dve.tensor_tensor(s, s, spread(r1[:, 0, :], SK), ALU.subtract).then_inc(s_ls, 1)

            def local_probs(L, b):
                s = LS[:, b, :, :]
                dve.wait_ge(s_lx, b + 1)
                link(dve.tensor_reduce(r1[:, 1, :], s, AX.X, ALU.add))
                link(dve.reciprocal(r1[:, 2, :], r1[:, 1, :]))
                dve.tensor_tensor(s, s, spread(r1[:, 2, :], SK), ALU.mult).then_inc(s_lp, 1)

            def local_add(L, b):
                dve.wait_ge(*slots.is_read(("LO", b)))
                x = tiles(X, b)
                link(dve.tensor_tensor(x, tiles(XN, b), x, ALU.add))

            def local_layer(L):
                front(L, NB - 1)
                front_stats(L + 1, 0)
                local_scores(L, NB - 1)
                front_apply(L + 1, 0)
                for b in range(1, LOCAL_EARLY):
                    front(L + 1, b)
                local_probs(L, NB - 1)
                for b in range(LOCAL_EARLY, NB):
                    local_add(L, b)
                    front_stats(L + 1, b)
                    if b > LOCAL_EARLY:
                        front_apply(L + 1, b - 1)
                front_apply(L + 1, NB - 1)

            def mha_layer(L):
                def project(i):
                    for b in range(NB):
                        k = made(("QKV", b, i))
                        read(("QKV", b, i), dve.tensor_tensor(QKV[:, b, i, :], PS[:, k, 0:3 * P], row("in_b"), ALU.add))
                    settled(("QKV", NB - 2, i))
                    settled(("QKV", NB - 1, i))
                    dve.engine_nop().then_inc(s_pin, 1)

                def parts(j):
                    sc4 = m5[:, j % 2, 0, :].rearrange("p (t s h) -> p t s h", t=NB, s=NB)
                    mx, sm, rs = (m5[:, j % 2, 1, 64 * x:64 * x + 64].rearrange("p (t h) -> p t h", t=NB)
                                  for x in range(3))
                    return sc4, mx, sm, rs

                def scores(j):
                    sc4, mx, _, _ = parts(j)
                    dve.wait_ge(s_p5, j + 1)
                    link(dve.tensor_reduce(m5[:, j % 2, 0, :], PROD[j % 2].rearrange("p (x d) -> p x d", d=DK), AX.X, ALU.add))
                    link(dve.tensor_reduce(mx, sc4.rearrange("p t s h -> p t h s"), AX.X, ALU.max))
                    for t in range(NB):
                        ins = dve.tensor_tensor(sc4[:, t, :, :], sc4[:, t, :, :], over(mx[:, t, :], NB), ALU.subtract)
                    ins.then_inc(s_s5, 1)

                def probs(j):
                    sc4, _, sm, rs = parts(j)
                    dve.wait_ge(s_e5, j + 1)
                    link(dve.tensor_reduce(sm, sc4.rearrange("p t s h -> p t h s"), AX.X, ALU.add))
                    link(dve.reciprocal(rs, sm))
                    for t in range(NB):
                        ins = dve.tensor_tensor(sc4[:, t, :, :], sc4[:, t, :, :], over(rs[:, t, :], NB), ALU.mult)
                    ins.then_inc(s_pr5, 1)
                    dve.wait_ge(s_pr5, j + 1)

                def weighted_values(j):
                    sc4, _, _, _ = parts(j)
                    pv = PV5[j % 2]
                    if j >= 2:
                        dve.wait_ge(s_av5, j - 1)
                    for t in range(POOL_FROM):
                        for s in range(NB):
                            ins = dve.tensor_tensor(pv[:, t, s, :].rearrange("p (h d) -> p h d", h=NH),
                                                    spread(sc4[:, t, s, :], DK),
                                                    QKV[:, s, j, 2 * P:3 * P].rearrange("p (h d) -> p h d", h=NH), ALU.mult)
                    ins.then_inc(s_c5, 1)

                project(0)
                project(1)
                scores(0)
                project(2)
                project(3)
                for j in range(TPB):
                    probs(j)
                    if j + 1 < TPB:
                        scores(j + 1)
                    weighted_values(j)

                def finish_h(b):
                    h = tiles(H5, b)
                    norm_apply("ln1", L, b, h, h)
                    link(dve.tensor_tensor(h, h, over(row("ln1_g"), TPB), ALU.mult))
                    dve.tensor_tensor(h, h, over(row("ln1_b"), TPB), ALU.add).then_inc(s_h5, 1)
                    dve.wait_ge(s_h5, b + 1)

                for b in range(NB):
                    k = made(("AO", b))
                    dve.wait_ge(s_ob, b + 1)
                    h = tiles(H5, b)
                    read(("AO", b), dve.tensor_tensor(h, PS[:, k, :].rearrange("p (i d) -> p i d", i=TPB), tiles(XN, b), ALU.add))
                    settled(("AO", b))
                    norm_stats("ln1", L, b, h)
                    if b:
                        finish_h(b - 1)
                for _ in route_mha(L, 0):
                    pass
                finish_h(NB - 1)

            def stage_of(stage, L, b):
                if stage == "stats":
                    front_stats(L, b)
                elif stage == "norm":
                    front_apply(L, b)
                elif stage == "front":
                    pass
                elif stage[0] == "L":
                    {"E": lambda L, b: gauss_context(), "S": local_scores, "N": local_probs,
                     "T": lambda L, b: None, "C": lambda L, b: None, "O": local_add}[stage[1]](L, b)
                elif stage == "keys":
                    dve.wait_ge(s_c, 16 * 2)
                    keys(0)
                elif stage == "values":
                    values(0)
                    link(dve.tensor_scalar(tscale[:, 0, :], row("tau"), ATT_SCALE, None, ALU.mult))
                    for a in range(3):
                        ins = dve.tensor_scalar(tscale[:, 1 + a, :], tscale[:, 0, :], col(f"bq{a}"), None, ALU.mult)
                    ins.then_inc(s_tau, 1)
                elif stage == "Q":
                    split_q(L, b)
                elif stage == "MT":
                    max_parts(L, b)
                elif stage == "R":
                    routing[:] = [{MOE: route_moe, MHA: route_mha, GLU: route_glu}[LAYERS[L]](L, b)]
                    next(routing[0], None)
                elif stage != "CT":
                    max_scores(L, b, int(stage[1]))

            stage[0] = NL
            dve.memset(KS1[96:128, :, :], 0.0).then_inc(s_ones, 1)
            link(dve.memset(g8[:, :, :], -3e38))
            link(dve.memset(c7[:, :, :, 48:64], 0.0))
            link(dve.memset(c7[:, :, :, 48:49], 1.0))
            dve.wait_ge(s_dl, 16)
            delta_parts()
            for x in BEFORE:
                stage_of(*x)
                if x[0] == "Q":
                    u = x[2]
                    dve.wait_ge(s_q3, u + 1)
                    for part in (1, 2):
                        for g in range(2 - part, NG):
                            dve.tensor_copy(T1[32 * part:32 * part + 32, u, g, :],
                                            qparts[32 * g:32 * g + 32, part, :]).then_inc(s_t1[u], 16)
            for n, (L, b) in enumerate(units):
                stage[0] = L
                if LAYERS[L] == LOCAL:
                    if b == 0:
                        local_layer(L)
                    continue
                if LAYERS[L] == MHA and b == 0:
                    mha_layer(L)
                todo = plan((L, b), "dve")
                prev = units[n - 1] if n and LAYERS[units[n - 1][0]] == ATTN else None
                if prev:
                    join_heads(*prev)

                def hook(step):
                    if prev and step == EPILOGUE[L][2]:
                        add_out(*prev)
                    if routing:
                        next(routing[0], None)
                    for at, *x in todo:
                        if at == step:
                            stage_of(*x)
                    if prev and step == EPILOGUE[L][0]:
                        divide_heads(*prev)
                    if step == 3 and (L, b) == (1, 2):
                        k_prep(1)
                    if step == 1 and (L, b) == (3, 1):
                        k_prep(2)
                    if step == 1 and (L, b) == (3, 2):
                        window_prep()

                if LAYERS[L] == ATTN:
                    for p in range(PAIRS):
                        hook(p)
                else:
                    {MOE: moe_unit, MHA: moe_unit, GLU: glu_unit}[LAYERS[L]](L, b, hook)


        @block.scalar
        def _(act):
            def made(job):
                act.wait_ge(*slots.is_made(job))
                return slots.bank(job)

            def read(job, ins):
                ins.then_inc(slots.is_read(job)[0], 1)

            def move(job, dst, src):
                k = made(job)
                read(job, nc.scalar.copy(dst, src(k)))

            def front(L, b):
                move(("T", L, b), XT[:, b, :], lambda k: PS[:, k, :])

            def make_q(L, b):
                u = n_attn[L, b]
                k = made(("Q", L, b))
                act.wait_ge(s_tau, 1)
                if u:
                    act.wait_ge(s_q3, u)
                    act.wait_ge(s_t1[u - 1], 16 * 12)
                    act.wait_ge(s_t2[u - 1], 16 * 12)
                scale, bias = tscale[:, 0, b:b + 1], tscale[:, 1 + ATTN_NO[L], b:b + 1]
                nc.scalar.activation(qf[:, :], PS[:, k, :], ACT.Identity, bias=bias, scale=scale)
                read(("Q", L, b), nc.scalar.activation(qparts[:, 0, :], PS[:, k, :], ACT.Identity, bias=bias, scale=scale))

            def place_max(L, b):
                u = n_attn[L, b]
                move(("MT", L, b), T2[96:128, u % QS, :, :],
                     lambda k: PS[0:2 * NH, k, :].unsqueeze(1).to_broadcast([2 * NH, NG, SQ]))

            def attn_unit(L, b, hook):
                u = n_attn[L, b]
                for p in range(PAIRS):
                    k = made(("S", L, b, p))
                    if PAIRS * u + p >= ES:
                        values_summed(act, PAIRS * u + p - ES)
                    read(("S", L, b, p), nc.scalar.activation(Eexp[:, (PAIRS * u + p) % ES, :, :], PS[0:SK, k:k + 2, :], ACT.Exp))
                    hook(p)

            def part_heads(L, b):
                u = n_attn[L, b]
                k = made(("PV", L, b, 0))
                if u:
                    act.wait_ge(*slots.is_read(("PV", *attn_units[u - 1], 1)))
                nc.scalar.mul(att[:, 0, :], PS[:, k, :], const("high_rows"))
                read(("PV", L, b, 0), nc.scalar.mul(att[:, 1, :], PS[:, k, :], const("low_rows")))

            def route(L, b):
                E = EXPERTS[L]
                if LAYERS[L] == GLU:
                    act.wait_ge(s_cw, n_moe[L, b])
                    k = made(("R", L, b))
                    read(("R", L, b), nc.scalar.activation(r16[:, 0, :, :], PS[:, k, 0:16 * TPB].rearrange("p (i e) -> p i e", i=TPB),
                                                           ACT.Sigmoid))
                elif LAYERS[L] == MOE:
                    act.wait_ge(s_lr, n_exp[L, b] + 1)
                    nc.scalar.activation(r16[:, 2, :, 0:E], r16[:, 0, :, 0:E], ACT.Exp).then_inc(s_le, 1)

            def turn_combine(L, b):
                if LAYERS[L] == GLU:
                    move(("CT", L, b), cT7[:, b % 2, :], lambda k: PS[0:64, k, :])
                else:
                    move(("CT", L, b), cT[0:EXPERTS[L], b % 2, :], lambda k: PS[0:EXPERTS[L], k, :])

            def moe_unit(L, b, hook):
                E, NC = EXPERTS[L], HIDDEN_CHUNKS[L]
                for e in range(E):
                    k = made(("H", L, b, e))
                    n = E * b + e
                    if n >= HS:
                        act.wait_ge(*slots.is_made(("Y", L, (n - HS) // E, (n - HS) % E)))
                    for c in range(NC):
                        ins = nc.scalar.activation(hT[:, n % HS, c, :], PS[:, k + c, :], ACT.Relu if L == 3 else ACT.Gelu,
                                                   bias=col(f"b1_{L}", NC * e + c))
                    read(("H", L, b, e), ins)
                    hook(e)

            def glu_unit(L, b, hook):
                for p in range(GLU_PAIRS):
                    n = GLU_PAIRS * b + p
                    k = made(("H", L, b, p))
                    if n >= 3:
                        m = n - 3
                        act.wait_ge(*slots.is_read(("CB", L, m // GLU_PAIRS, m % GLU_PAIRS)))
                    nc.scalar.activation(gl[:, n % 3, 0, :], PS[:, k, :], ACT.Silu).then_inc(s_sil, 1)
                    hook(p)

            def gauss():
                act.wait_ge(s_lg, 1)
                nc.scalar.activation(gau[:, 2, :], gau[:, 1, :], ACT.Exp, scale=-1.0 / DEV_POW).then_inc(s_ge, 1)
                move(("E4",), Eloc, lambda k: PS[:, k, 0:CK])

            def local_exps(L, b):
                act.wait_ge(s_ls, b + 1)
                nc.scalar.activation(LS[:, b, :, :], LS[:, b, :, :], ACT.Exp).then_inc(s_lx, 1)

            def turn_local(L, b):
                move(("LT", b), LPT[0:SK, b, :], lambda k: PS[0:SK, k, :])

            def local_context(L, b):
                move(("LC", b), local_ctx[:, b, :], lambda k: PS[:, k, :])

            def local_out(L, b):
                k = made(("LO", b))
                read(("LO", b), nc.scalar.activation(XN[:, TPB * b:TPB * b + TPB, :],
                                                     PS[:, k, :].rearrange("p (i d) -> p i d", i=TPB), ACT.Tanh))

            def local_layer(L):
                front(L, NB - 1)
                local_exps(L, NB - 1)
                for b in range(LOCAL_EARLY):
                    front(L + 1, b)
                turn_local(L, NB - 1)
                for b in range(LOCAL_EARLY, NB):
                    local_context(L, b)
                for b in range(LOCAL_EARLY, NB):
                    local_out(L, b)
                for b in range(LOCAL_EARLY, NB):
                    front(L + 1, b)

            def mha_layer(L):
                for j in range(TPB):
                    act.wait_ge(s_s5, j + 1)
                    sc = m5[:, j % 2, 0, :]
                    nc.scalar.activation(sc, sc, ACT.Exp, scale=ATT_SCALE).then_inc(s_e5, 1)
                for b in range(NB):
                    k = made(("AT", b // 2))
                    ins = nc.scalar.copy(hT[:, b % HS, b // HS, :], PS[:, k + b % 2, :])
                    if b % 2:
                        read(("AT", b // 2), ins)
                move(("T2", L, 0), XT[:, 0, :], lambda k: PS[:, k, :])
                turn_combine(L, 0)

            def stage_of(stage, L, b):
                if stage == "front":
                    move(("T2" if LAYERS[L] == MHA else "T", L, b), XT[:, b, :], lambda k: PS[:, k, :])
                elif stage[0] == "L":
                    {"E": lambda L, b: gauss(), "S": local_exps, "N": lambda L, b: None, "T": turn_local,
                     "C": local_context, "O": local_out}[stage[1]](L, b)
                elif stage == "Q":
                    make_q(L, b)
                elif stage == "MT":
                    place_max(L, b)
                elif stage == "R":
                    route(L, b)
                elif stage == "CT":
                    turn_combine(L, b)

            act.wait_ge(s_c, 16 * 2)
            nc.scalar.copy(KS2[96:128, :, :], const("pick_head")[96:128, :].unsqueeze(2).to_broadcast([32, NH, CK])).then_inc(s_pick, 1)
            for x in BEFORE:
                stage_of(*x)
                if x[0] == "Q":
                    u = x[2]
                    act.wait_ge(*slots.is_read(x))
                    for g in range(NG):
                        nc.scalar.copy(T1[0:32, u, g, :], qparts[32 * g:32 * g + 32, 0, :]).then_inc(s_t1[u], 16)
                    act.wait_ge(s_q3, u + 1)
                    nc.scalar.copy(T1[32:64, u, 0, :], qparts[0:32, 1, :]).then_inc(s_t1[u], 16)
            act.wait_ge(s_rows, 16 * 4)
            nc.scalar.copy(pick7[:, :], H5[0:64, 0:GLU_PAIRS, :].rearrange("p a b -> p (a b)")).then_inc(s_pick, 1)
            for n, (L, b) in enumerate(units):
                if b == 0 and L:
                    if LAYERS[L - 1] == ATTN:
                        values_summed(act, PAIRS * n_attn[L - 1, NB - 1] + PAIRS - 1)
                    elif LAYERS[L - 1] in (MOE, MHA):
                        act.wait_ge(*slots.is_made(("Y", L - 1, NB - 1, EXPERTS[L - 1] - 1)))
                if LAYERS[L] == LOCAL:
                    if b == 0:
                        local_layer(L)
                    continue
                if LAYERS[L] == MHA and b == 0:
                    mha_layer(L)
                todo = plan((L, b), "act")
                prev = units[n - 1] if n and LAYERS[units[n - 1][0]] == ATTN else None

                def hook(step):
                    for at, *x in todo:
                        if at == step:
                            stage_of(*x)
                    if step == 5 and LAYERS[L] == ATTN:
                        part_heads(L, b)

                {ATTN: attn_unit, MOE: moe_unit, MHA: moe_unit, GLU: glu_unit}[LAYERS[L]](L, b, hook)

        @block.gpsimd
        def _(pool):
            pool.memset(mhalf[:, :], -0.5).then_inc(s_pool0, 1)
            pool.memset(V2[:, :, :, :], 0.0).then_inc(s_pool0, 1)
            pool.wait_ge(s_pool0, 2)
            for half in range(2):
                for sub in range(2):
                    h0, c0 = 8 * half + 4 * sub, 16 - 16 * half + 8 * sub
                    for b in range(NB):
                        ins = pool.memset(V2[:, b, h0:h0 + 4, c0:c0 + DK], 1.0)
            ins.then_inc(s_pool0, 1)
            pool.memset(T1[96:128, :, :, :], 1.0).then_inc(s_pool0, 1)
            pool.wait_ge(s_pool0, 4)
            pool.wait_ge(s_rows, 16 * 4)

            def weighted_values(j):
                pool.wait_ge(s_pr5, j + 1)
                if j >= 2:
                    pool.wait_ge(s_av5, j - 1)
                pv = PV5[j % 2]
                for t in range(POOL_FROM, NB):
                    for s in range(NB):
                        prob = m5[:, j % 2, 0, 16 * (NB * t + s):16 * (NB * t + s) + 16]
                        ins = pool.tensor_tensor(pv[:, t, s, :].rearrange("p (h d) -> p h d", h=NH),
                                                 prob.unsqueeze(2).to_broadcast([P, NH, DK]),
                                                 QKV[:, s, j, 2 * P:3 * P].rearrange("p (h d) -> p h d", h=NH), ALU.mult)
                ins.then_inc(s_pv5, 1)

            for n, (which, L, b) in enumerate(norms):
                if (which, L, b) == ("ln1", 5, 0):
                    for j in range(TPB):
                        pool.wait_ge(s_pin, j + 1)
                        if j >= 2:
                            pool.wait_ge(s_s5, j - 1)
                        prod = PROD[j % 2].rearrange("p (t s c) -> p t s c", t=NB, s=NB)
                        for t in range(NB):
                            ins = pool.tensor_tensor(prod[:, t, :, :],
                                                     QKV[:, t, j, 0:P].unsqueeze(1).to_broadcast([P, NB, P]),
                                                     QKV[:, :, j, P:2 * P], ALU.mult)
                        ins.then_inc(s_p5, 1)
                        if j == 1:
                            for t in range(NB):
                                x = XN[:, TPB * t:TPB * t + TPB, :]
                                pool.tensor_tensor(x, x, row("out_b").unsqueeze(1).to_broadcast([P, TPB, P]),
                                                   ALU.add).then_inc(s_ob, 1)
                        if j:
                            weighted_values(j - 1)
                    weighted_values(TPB - 1)
                pool.wait_ge(s_stat, n + 1)
                pool.tensor_scalar(vare[:, n % 2, :], mv[:, n % 2, :, 1], EPS, None, ALU.add).then_inc(s_vare, 1)
                pool.wait_ge(s_vare, n + 1)
                pool.tensor_tensor(rstd[:, n % 2, :], vare[:, n % 2, :], mhalf[:, :], ALU.pow).then_inc(s_rstd, 1)
                if which == "in" and LAYERS[L] == ATTN:
                    pool.wait_ge(s_xn, n_in[L, b])
                    x = X[:, TPB * b:TPB * b + TPB, :]
                    bo = row(f"bo{ATTN_NO[L]}").unsqueeze(1).to_broadcast([P, TPB, P])
                    pool.tensor_tensor(x, x, bo, ALU.add).then_inc(s_bo, 1)

        @block.sync
        def _(sp):
            xd = A["x"].rearrange("(t p) d -> p t d", p=P)
            sp.dma_start(drow[:, 0, :], A["delta"]).then_inc(s_dl, 16)
            sp.dma_start(ctxT[:, :], A["ctxT"]).then_inc(s_kw, 16)
            sp.dma_start(wattn[:, 0, :, :], A["wattn"][:, 0]).then_inc(s_kw, 16)
            sp.dma_start(consts[:, :], A["consts"]).then_inc(s_c, 16)
            sp.dma_start(cols[:, :], A["cols"]).then_inc(s_c, 16)
            sp.dma_start(X[:, 0:TPB, :], xd[:, 0:TPB, :]).then_inc(s_x[0], 16)
            sp.dma_start(rows[:, :], A["rows"].partition_broadcast(P)).then_inc(s_rows, 16)
            sp.dma_start(ctxN[:, :, :], A["ctxN"]).then_inc(s_rows, 16)
            sp.dma_start(leni[:, :], A["lens"].partition_broadcast(P)).then_inc(s_rows, 16)
            sp.dma_start(H5[0:64, 0:GLU_PAIRS, :], A["pick_pair"]).then_inc(s_rows, 16)
            for b in range(1, NB):
                sp.dma_start(X[:, TPB * b:TPB * b + TPB, :], xd[:, TPB * b:TPB * b + TPB, :]).then_inc(s_x[b], 16)

            def place(dst, src, done):
                for g in range(NG):
                    sp.dma_start(dst(g), src(g)).then_inc(done, 16)

            def place_keys(K, parts, done):
                for q, part in enumerate(parts):
                    place(lambda g: K[32 * q:32 * q + 32, HPG * g:HPG * g + HPG, :],
                          lambda g: KB[32 * g:32 * g + 32, part, :, :], done)

            def place_queries(u, T, parts, done):
                for q, part in enumerate(parts):
                    place(lambda g: T[32 * q:32 * q + 32, u % QS, g, :],
                          lambda g: qparts[32 * g:32 * g + 32, part, :], done)

            def place_k(a):
                sp.wait_ge(s_kb, a + 1)
                place_keys(KS1, (0, 0, 0), s_ks1[a])
                place_keys(KS2, (1, 1, 2), s_ks[a])

            def place_q(u):
                sp.wait_ge(s_q3, u + 1)
                place_queries(u, T1, (0, 1, 2), s_t1[u])
                place_queries(u, T2, (0, 1, 0), s_t2[u])

            sp.wait_ge(s_ones, 1)
            sp.wait_ge(s_delta, 1)
            for j in range(3):
                sp.dma_start(KS1[96 + j:97 + j, :, :], dparts[:, j, :].unsqueeze(1).to_broadcast([1, NH, CK])).then_inc(s_drow, 16)
            place_k(0)
            for u in range(2):
                sp.wait_ge(s_q3, u + 1)
                place_queries(u, T2, (0, 1, 0), s_t2[u])
            sp.dma_start(router[:, :], A["router"]).then_inc(s_w["a"], 16)
            for a in (1, 2):
                sp.dma_start(wattn[:, a, :, :], A["wattn"][:, a]).then_inc(s_w["a"], 16)
            def load_experts(L):
                sp.dma_start(w1[L][:, :, :] if L > 1 else w1[L], A[f"w1_{L}"]).then_inc(s_w[f"m{L}"], 16)
                sp.dma_start(w2[L][:, :, :, :] if L > 1 else w2[L], A[f"w2_{L}"]).then_inc(s_w[f"m{L}"], 16)
                sp.dma_start(b2[L][:, :], A[f"b2_{L}"]).then_inc(s_w[f"m{L}"], 16)

            place_q(2)
            load_experts(1)
            place_q(3)
            load_experts(3)
            load_experts(5)
            sp.dma_start(wloc[:, :, :], A["wloc"]).then_inc(s_w["loc"], 16)
            sp.dma_start(win5[:, :], A["win5"]).then_inc(s_w["loc"], 16)
            place_k(1)
            for u in range(4, 8):
                place_q(u)
            place_k(2)
            sp.wait_ge(s_c5, TPB)
            sp.wait_ge(s_pv5, TPB)
            sp.dma_start(w1[7], A["w1_7"]).then_inc(s_w["m7"], 16)
            sp.dma_start(w3_7, A["w3_7"]).then_inc(s_w["m7"], 16)
            sp.dma_start(w2[7], A["w2_7"]).then_inc(s_w["m7"], 16)
            for u in range(8, 12):
                place_q(u)
            od = out.rearrange("(t p) d -> p t d", p=P)
            for b in range(NB):
                sp.wait_ge(*slots.is_read(("Y", 7, b)))
                sp.dma_start(od[:, TPB * b:TPB * b + TPB, :], X[:, TPB * b:TPB * b + TPB, :]).then_inc(s_out, 16)
            sp.wait_ge(s_out, 16 * NB)


def constants():
    r = np.arange(P)
    c = np.zeros((P, CONSTS_N), np.float32)

    def put(name, v):
        a, b = CONSTS[name]
        c[:, a:b] = v

    put("ident", np.eye(P))
    put("head_mask", (r[:, None] % 32) // DK == np.arange(HPG)[None])
    put("low_rows", (r % 32 < 16)[:, None])
    put("high_rows", (r % 32 >= 16)[:, None])
    put("pick_head", r[:, None] % NH == np.arange(NH)[None])
    put("iota16", np.arange(16)[None])
    put("iota77", np.arange(SK)[None])
    put("iota_col", r[:, None])
    pick = np.zeros((64, GLU_PAIRS, P), np.float32)
    for p in range(GLU_PAIRS - 1):
        for half in range(2):
            for part in range(3):
                pick[16 * part + 2 * p + half, p, 64 * half:64 * half + 64] = 1
    pick[48, GLU_PAIRS - 1, :] = 1
    return c, pick


def lay_out(i):
    f = {k: np.asarray(v) for k, v in i.items()}
    A = {}
    A["consts"], A["pick_pair"] = constants()
    A["x"] = f["x"].reshape(NB * SQ, P)
    A["ctxT"] = f["ctx_1024"].reshape(CK, P).T
    A["ctxN"] = f["ctx_1024"].transpose(1, 0, 2)
    A["delta"] = f["fside_BxS2_0"].reshape(1, CK)
    A["lens"] = f["_lenS2"]
    order = np.zeros(P, np.int64)
    for h in range(NH):
        order[num_row(h):num_row(h) + DK] = DK * h + np.arange(DK)
    sets = []
    for L in (0, 1, 3):
        w = [f[f"L{L}_xcond_W{n}"].T for n in "qkvo"]
        w[3] = w[3][order]
        sets.append(np.stack(w, 1))
    A["wattn"] = np.stack(sets, 1)
    A["router"] = np.concatenate([f["L0_ffn_router_w"], f["L1_ffn_Wr"], f["L2_ffn_router_w"].T, f["L3_ffn_gate_w"].T], 1)
    for L, n, k1, k2, kb in ((1, 0, "w1", "w2", "b2"), (3, 1, "W1", "W2", "b2")):
        A[f"w1_{L}"] = f[f"L{n}_ffn_{k1}"].transpose(1, 0, 2)
        w = f[f"L{n}_ffn_{k2}"]
        A[f"w2_{L}"] = w.reshape(w.shape[0], 2, P, P).transpose(2, 0, 1, 3)
        A[f"b2_{L}"] = f[f"L{n}_ffn_{kb}"]
    A["w1_5"] = f["L2_ffn_w1"].transpose(2, 0, 1)
    A["w2_5"] = f["L2_ffn_w2"].transpose(2, 0, 1)[:, :, None]
    A["b2_5"] = f["L2_ffn_b2"]
    A["wloc"] = np.stack([f["L2_xcond_W_a"].T, f["L2_xcond_W_c"][:, :P].T, f["L2_xcond_W_c"][:, P:].T], 1)
    A["win5"] = np.concatenate([f["L2_ffn_in_proj_w"].T, f["L2_ffn_out_w"].T], 1)
    pad = np.zeros((P, 64), np.float32)
    for n in (1, 3):
        w = np.concatenate([f[f"L3_ffn_w{n}"].reshape(16 * 64, P).T, f[f"L3_ffn_ws{n}"].T, pad], 1)
        A[f"w{n}_7"] = w.reshape(P, GLU_PAIRS, P)
    w = np.concatenate([f["L3_ffn_w2"].transpose(0, 2, 1).reshape(16 * 64, P), f["L3_ffn_ws2"].T, pad.T], 0)
    A["w2_7"] = w.reshape(GLU_PAIRS, P, P).transpose(1, 0, 2)
    cols = [f[f"L{L}_xcond_b{n}"][:, None] for n in "qk" for L in (0, 1, 3)]
    cols += [f["L0_ffn_b1"].reshape(32, P).T, f["L1_ffn_b1"].reshape(16, P).T, f["L2_ffn_b1"].T]
    A["cols"] = np.concatenate(cols, 1)
    A["rows"] = np.concatenate([f[f"L{L}_xcond_b{n}"] for n in "vo" for L in (0, 1, 3)] + [
        f["L0_ffn_router_b"], f["L1_ffn_br"], f["L2_ffn_router_b"], f["L3_ffn_gate_bias"], f["L2_ffn_in_proj_b"],
        f["L2_ffn_out_b"], f["L2_ffn_ln1_g"], f["L2_ffn_ln1_b"], f["L2_ffn_ln2_g"], f["L2_ffn_ln2_b"],
        f["condB_tau"], f["condB_pt"]])
    return {k: np.ascontiguousarray(v) for k, v in A.items()}


def kernel(**inputs):
    import numpy as _np
    import concourse.bacc as _bacc
    from concourse import mybir as _mybir
    from concourse.bass_utils import run_bass_kernel_spmd as _run

    nc = _bacc.Bacc("TRN2", target_bir_lowering=False, num_devices=1)
    arrays = {f"in_{k}": v for k, v in lay_out(inputs).items()}
    args = {k[3:]: nc.dram_tensor(k, v.shape, _mybir.dt.from_np(v.dtype), kind="ExternalInput").ap()
            for k, v in arrays.items()}
    out = nc.dram_tensor("out_0", (NB * SQ, P), F32, kind="ExternalOutput").ap()
    build(nc, args, out)
    r = _run(nc, [arrays], core_ids=[0])
    return _np.asarray(r.results[0]["out_0"]).reshape(NB, SQ, P)
```
